# Optimizing a Trainium2 kernel written in Bass

```python
import numpy as np
import jax
import jax.numpy as jnp

def _softmax(x, axis=-1):
    return jax.nn.softmax(x, axis=axis)

def _gelu(x):
    return jax.nn.gelu(x, approximate=True)

def _silu(x):
    return jax.nn.silu(x)

def _sigmoid(x):
    return jax.nn.sigmoid(x)

def _layernorm(x, axis=-1, eps=1e-05):
    m = jnp.mean(x, axis=axis, keepdims=True)
    v = jnp.var(x, axis=axis, keepdims=True)
    return (x - m) / jnp.sqrt(v + eps)

def _scatter_add(tgt, idx, src, axis=0):
    return tgt.at[idx].add(src)

def _segment_sum(src, seg, n):
    return jax.ops.segment_sum(src, seg, n)
kernel_name = 'mk_perceiver_d1_seqx_r4_47c91e'

def setup_inputs(seed: int=0):
    np.random.seed(seed)
    _w = jnp.asarray

    def _rec_inputs():
        import jax
        import jax.numpy as jnp
        _rk = jax.random.key(seed)
        x = -0.0003929 + 0.9999 * jax.random.normal(jax.random.fold_in(_rk, 1), (64, 32, 512), jnp.float32)
        _lenS = 32 - jax.random.randint(jax.random.fold_in(_rk, 7), (64,), 0, max(1, 32 // 4) + 1, jnp.int32)
        _lenS2 = 257 - jax.random.randint(jax.random.fold_in(_rk, 8), (64,), 0, max(1, 257 // 4) + 1, jnp.int32)
        _ctx_1024P = jax.random.normal(jax.random.fold_in(_rk, 11), (64, 16, 256), jnp.float32)
        _ctx_1024c = jax.random.dirichlet(jax.random.fold_in(_rk, 511), 0.3 * jnp.ones((16,), jnp.float32), (64, 257))
        _ctx_1024t = jnp.einsum('bsk,bkd->bsd', _ctx_1024c, _ctx_1024P)
        _ctx_1024t = _ctx_1024t * jax.lax.rsqrt(jnp.mean(jnp.square(_ctx_1024t)) + 1e-12) * 0.953939
        ctx_1024 = 0.000227908 + 0.99994 * (_ctx_1024t + 0.3 * jax.random.normal(jax.random.fold_in(_rk, 611), (64, 257, 256), jnp.float32))
        return (x, ctx_1024)
    x, ctx_1024 = _rec_inputs()

    def _L0_xattn_setup():
        import jax, jax.numpy as jnp
        import numpy as np
        EPS = 1e-05

        def rmsnorm(x, g, eps=EPS):
            var = jnp.mean(jnp.square(x), axis=-1, keepdims=True)
            return x * jax.lax.rsqrt(var + eps) * g
        key = jax.random.key(seed)
        ks = jax.random.split(key, 8)
        B, Sq, Skv = (2, 1024, 128)
        dim, cdim, H, D = (512, 256, 16, 128)
        inner = H * D
        s = lambda f: 1.0 / np.sqrt(f)
        return {'hidden_states': jax.random.normal(ks[0], (B, Sq, dim), jnp.float32), 'encoder_hidden_states': jax.random.normal(ks[1], (B, Skv, cdim), jnp.float32), 'Wq': jax.random.normal(ks[2], (dim, inner), jnp.float32) * s(dim), 'Wk': jax.random.normal(ks[3], (cdim, inner), jnp.float32) * s(cdim), 'Wv': jax.random.normal(ks[4], (cdim, inner), jnp.float32) * s(cdim), 'Wo': jax.random.normal(ks[5], (inner, dim), jnp.float32) * s(inner), 'gq': jnp.ones((D,), jnp.float32), 'gk': jnp.ones((D,), jnp.float32)}
    _L0_xattn_all = _L0_xattn_setup()
    _L0_xattn_in = {k: v for k, v in _L0_xattn_all.items() if k in ('Wq', 'Wk', 'Wv', 'Wo', 'gq', 'gk')}
    del _L0_xattn_all

    def _L0_attn_setup():
        import jax, jax.numpy as jnp
        import numpy as np
        B, SQ, H = (2, 512, 512)
        NH = 16
        HN = H // NH
        key = jax.random.key(seed)
        ks = jax.random.split(key, 6)
        query = jax.random.normal(ks[0], (B, SQ, H), dtype=jnp.float32)
        k_in = jax.random.normal(ks[1], (B, SQ, H), dtype=jnp.float32)
        v_in = jax.random.normal(ks[2], (B, SQ, H), dtype=jnp.float32)
        Wqkv = jax.random.normal(ks[3], (3 * H, H), dtype=jnp.float32) * (1.0 / np.sqrt(H))
        Wproj = jax.random.normal(ks[4], (H, H), dtype=jnp.float32) * (1.0 / np.sqrt(H))
        bproj = jnp.zeros((H,), dtype=jnp.float32)
        return {'query': query, 'key': k_in, 'value': v_in, 'Wqkv': Wqkv, 'Wproj': Wproj, 'bproj': bproj}
    _L0_attn_all = _L0_attn_setup()
    _L0_attn_in = {k: v for k, v in _L0_attn_all.items() if k in ('key', 'value', 'Wqkv', 'Wproj', 'bproj')}
    del _L0_attn_all

    def _L0_ffn_setup():
        import jax, jax.numpy as jnp
        import numpy as np
        E, TOP_K, D, H = (8, 2, 512, 352)
        B, S = (2, 512)
        key = jax.random.key(seed)
        ks = jax.random.split(key, 8)
        x = jax.random.normal(ks[0], (B, S, D), dtype=jnp.float32)
        gate_w = jax.random.normal(ks[1], (E, D), dtype=jnp.float32) * (1.0 / np.sqrt(D))
        gate_b = jax.random.normal(ks[2], (E,), dtype=jnp.float32) * 0.01
        bias = jnp.zeros((E,), dtype=jnp.float32)
        w1 = jax.random.normal(ks[3], (E, H, D), dtype=jnp.float32) * (1.0 / np.sqrt(D))
        b1 = jax.random.normal(ks[4], (E, H), dtype=jnp.float32) * 0.01
        w2 = jax.random.normal(ks[5], (E, D, H), dtype=jnp.float32) * (1.0 / np.sqrt(H))
        b2 = jax.random.normal(ks[6], (E, D), dtype=jnp.float32) * 0.01
        return {'x': x, 'gate_w': gate_w, 'gate_b': gate_b, 'bias': bias, 'w1': w1, 'b1': b1, 'w2': w2, 'b2': b2}
    _L0_ffn_all = _L0_ffn_setup()
    _L0_ffn_in = {k: v for k, v in _L0_ffn_all.items() if k in ('gate_w', 'gate_b', 'bias', 'w1', 'b1', 'w2', 'b2')}
    del _L0_ffn_all
    return {'x': x, 'ctx_1024': ctx_1024, 'L0_xattn_Wq': _L0_xattn_in['Wq'], 'L0_xattn_Wk': _L0_xattn_in['Wk'], 'L0_xattn_Wv': _L0_xattn_in['Wv'], 'L0_xattn_Wo': _L0_xattn_in['Wo'], 'L0_xattn_gq': _L0_xattn_in['gq'], 'L0_xattn_gk': _L0_xattn_in['gk'], 'L0_attn_key': _L0_attn_in['key'], 'L0_attn_value': _L0_attn_in['value'], 'L0_attn_Wqkv': _L0_attn_in['Wqkv'], 'L0_attn_Wproj': _L0_attn_in['Wproj'], 'L0_attn_bproj': _L0_attn_in['bproj'], 'L0_ffn_gate_w': _L0_ffn_in['gate_w'], 'L0_ffn_gate_b': _L0_ffn_in['gate_b'], 'L0_ffn_bias': _L0_ffn_in['bias'], 'L0_ffn_w1': _L0_ffn_in['w1'], 'L0_ffn_b1': _L0_ffn_in['b1'], 'L0_ffn_w2': _L0_ffn_in['w2'], 'L0_ffn_b2': _L0_ffn_in['b2']}

def reference(x, ctx_1024, L0_xattn_Wq, L0_xattn_Wk, L0_xattn_Wv, L0_xattn_Wo, L0_xattn_gq, L0_xattn_gk, L0_attn_key, L0_attn_value, L0_attn_Wqkv, L0_attn_Wproj, L0_attn_bproj, L0_ffn_gate_w, L0_ffn_gate_b, L0_ffn_bias, L0_ffn_w1, L0_ffn_b1, L0_ffn_w2, L0_ffn_b2):
    import jax
    import jax.numpy as jnp

    def _L0_xattn_ref(hidden_states, encoder_hidden_states, Wq, Wk, Wv, Wo, gq, gk):
        import jax, jax.numpy as jnp
        import numpy as np
        EPS = 1e-05

        def rmsnorm(x, g, eps=EPS):
            var = jnp.mean(jnp.square(x), axis=-1, keepdims=True)
            return x * jax.lax.rsqrt(var + eps) * g
        B, Sq, _ = hidden_states.shape
        Skv = encoder_hidden_states.shape[1]
        D = gq.shape[0]
        H = Wq.shape[1] // D
        scale = 1.0 / np.sqrt(D)
        q = (hidden_states @ Wq).reshape(B, Sq, H, D)
        k = (encoder_hidden_states @ Wk).reshape(B, Skv, H, D)
        v = (encoder_hidden_states @ Wv).reshape(B, Skv, H, D)
        q = rmsnorm(q, gq)
        k = rmsnorm(k, gk)
        scores = jnp.einsum('bqhd,bkhd->bhqk', q, k) * scale
        attn = jax.nn.softmax(scores, axis=-1)
        out = jnp.einsum('bhqk,bkhd->bqhd', attn, v)
        out = out.reshape(B, Sq, H * D)
        return out @ Wo

    def _L0_attn_ref(query, key, value, Wqkv, Wproj, bproj):
        import jax, jax.numpy as jnp
        import numpy as np
        B, SQ, H = (2, 512, 512)
        NH = 16
        HN = H // NH
        b, sq, h = query.shape
        nh, hn = (NH, HN)
        norm = 1.0 / jnp.sqrt(jnp.asarray(hn, query.dtype))
        x = jnp.transpose(query, (1, 0, 2)).reshape(sq * b, h)
        mixed = x @ Wqkv.T
        mixed = mixed.reshape(sq, b, nh, 3, hn)
        q = mixed[..., 0, :]
        k = mixed[..., 1, :]
        v = mixed[..., 2, :]
        q = q.reshape(sq, b * nh, hn).transpose(1, 0, 2)
        k = k.reshape(sq, b * nh, hn).transpose(1, 0, 2)
        v = v.reshape(sq, b * nh, hn).transpose(1, 0, 2)
        attn = jnp.einsum('gqd,gkd->gqk', q, k) * norm
        attn = jax.nn.softmax(attn, axis=-1)
        ctx = jnp.einsum('gqk,gkd->gqd', attn, v)
        ctx = ctx.reshape(nh, b, sq, hn)
        ctx = jnp.transpose(ctx, (2, 1, 0, 3)).reshape(sq * b, h)
        out = ctx @ Wproj.T + bproj
        out = out.reshape(sq, b, h)
        return jnp.transpose(out, (1, 0, 2))

    def _L0_ffn_ref(x, gate_w, gate_b, bias, w1, b1, w2, b2):
        import jax, jax.numpy as jnp
        import numpy as np
        E, TOP_K, D, H = (8, 2, 512, 352)
        B, S = (2, 512)
        b, s, d = x.shape
        xf = x.reshape(-1, d)
        scores = xf @ gate_w.T + gate_b + bias
        top_scores, top_idx = jax.lax.top_k(scores, TOP_K)
        gates = jax.nn.softmax(top_scores, axis=-1)
        comb = jnp.sum(jax.nn.one_hot(top_idx, E, dtype=gates.dtype) * gates[..., None], axis=1)
        h = jax.nn.silu(jnp.einsum('td,ehd->teh', xf, w1) + b1)
        y = jnp.einsum('teh,edh->ted', h, w2) + b2
        out = jnp.einsum('ted,te->td', y, comb)
        return out.reshape(b, s, d)
    x = x + _L0_xattn_ref(_layernorm(x, axis=-1), ctx_1024, L0_xattn_Wq, L0_xattn_Wk, L0_xattn_Wv, L0_xattn_Wo, L0_xattn_gq, L0_xattn_gk)
    x = x + _L0_attn_ref(_layernorm(x, axis=-1), L0_attn_key, L0_attn_value, L0_attn_Wqkv, L0_attn_Wproj, L0_attn_bproj)
    x = x + _L0_ffn_ref(_layernorm(x, axis=-1), L0_ffn_gate_w, L0_ffn_gate_b, L0_ffn_bias, L0_ffn_w1, L0_ffn_b1, L0_ffn_w2, L0_ffn_b2)
    return x

_drawn_inputs = setup_inputs


def setup_inputs(seed=0):
    import zlib

    import numpy as np

    out = dict(_drawn_inputs(seed))
    spreads = {'L0_xattn_gq': (1.0, 0.2),
     'L0_xattn_gk': (1.0, 0.2),
     'L0_attn_bproj': (0.0, 0.1),
     'L0_ffn_bias': (0.0, 0.1)}
    factors = {'L0_ffn_gate_b': 2.762, 'L0_ffn_b1': 8.0, 'L0_ffn_b2': 8.0}
    for name, (base, spread) in spreads.items():
        noise = np.random.default_rng([zlib.crc32(name.encode()), seed]).standard_normal(out[name].shape)
        drawn = base * np.exp(spread * noise) if base else spread * noise
        out[name] = jnp.asarray(drawn.astype(out[name].dtype))
    for name, factor in factors.items():
        out[name] = (out[name] * factor).astype(out[name].dtype)
    return out
```

```python
from contextlib import ExitStack

import concourse.bass as bass
from concourse import mybir

F32 = mybir.dt.float32
F32R = mybir.dt.float32r
ALU = mybir.AluOpType
ACT = mybir.ActivationFunctionType
AX_X = mybir.AxisListType.X

P = 128
BANK = 512
EPS = 1e-5
LOWEST = -3.0e38


def three_products(pe, out, left, right, first, last):
    (left_hi, left_lo), (right_hi, right_lo) = left, right
    pe.matmul(out, left_hi, right_hi, start=first, stop=False)
    pe.matmul(out, left_hi, right_lo, start=False, stop=False)
    return pe.matmul(out, left_lo, right_hi, start=False, stop=last)


class Memory:

    def __init__(self, nc, stack, phase):
        self.nc, self.stack, self.phase = nc, stack, phase
        self.sems = []
        stack.callback(self.clear)

    def clear(self):
        if self.sems:
            self.nc.clear_and_free_semaphores(self.sems)
            self.nc.all_engine_barrier(sem_only=True)

    def sbuf(self, name, shape, dtype=F32):
        return self.stack.enter_context(self.nc.sbuf_tensor(f"{self.phase}_{name}", shape, dtype))

    def pair(self, name, shape):
        return self.sbuf(name + "_hi", shape, F32R), self.sbuf(name + "_lo", shape, F32R)

    def banks(self, name, count):
        return [self.stack.enter_context(self.nc.psum_tensor(f"{self.phase}_{name}{i}", [P, BANK], F32))
                for i in range(count)]

    def sem(self, name):
        self.sems.append(self.nc.alloc_semaphore(f"{self.phase}_{name}"))
        return self.sems[-1]


def shared_constants(nc, ident, minus_half, eps):
    with ExitStack() as stack:
        mem = Memory(nc, stack, "const")
        filled = mem.sem("filled")
        with nc.Block() as block:
            @block.gpsimd
            def _(pool):
                pool.memset(minus_half[:, :], -0.5)
                pool.memset(eps[:, :], EPS)
                pool.memset(ident[:, :], 0.0).then_inc(filled, 1)
                pool.wait_ge(filled, 1)
                pool.affine_select(out=ident[:, :], in_=ident[:, :], compare_op=ALU.not_equal, fill=1.0,
                                   base=0, pattern=[[-1, P]], channel_multiplier=1)


def queries(nc, x, wq, wk_t, gq, gk, scores_scratch, ident, minus_half, eps):
    B, Q, M = x.shape
    D, H, C = wk_t.shape
    MC, CC, HG = M // P, C // P, H // 4
    BT = P // Q
    T = 2
    W = T * P
    BLOCKS = B // (T * BT)
    x_blocks = x.rearrange("(i t b) q m -> i (b q) t m", t=T, b=BT)
    wq_rows = wq.rearrange("(c p) n -> p c n", p=P)
    out_blocks = scores_scratch.rearrange("(i b) p c h q -> i p b c (h q)", b=T * BT)

    with ExitStack() as stack:
        mem = Memory(nc, stack, "q")
        piece = [mem.sbuf(f"piece{i}", [P, H * D]) for i in range(2)]
        gain = mem.sbuf("gain", [P, 3])
        wq_hl = mem.pair("wq", [P, MC, H * D])
        wk_hl = mem.pair("wk", [P, H, C])
        x_in = mem.sbuf("x_in", [P, T, M])
        stats = mem.sbuf("stats", [P, T, 6])
        moments = mem.sbuf("moments", [P, T, 2])
        x_rstd = mem.sbuf("x_rstd", [P, T, 2])
        x_norm = mem.sbuf("x_norm", [P, T, M])
        x_hl = mem.pair("x", [P, MC, W])
        q_sb = mem.sbuf("q_sb", [P, 2, T, 4, D])
        q_sq = mem.sbuf("q_sq", [P, T, 4, D])
        spare = mem.sbuf("spare", [P, 1])
        q_var = mem.sbuf("q_var", [P, 2, T, 4])
        q_rstd = mem.sbuf("q_rstd", [P, 2, T, 4])
        q_hl = [mem.pair(f"q{i}", [P, 4, W]) for i in range(2)]
        staged = [mem.sbuf(f"staged{i}", [P, T * BT, CC, 4 * Q]) for i in range(2)]
        ps_q = mem.banks("ps_q", T)
        ps_xt = mem.banks("ps_xt", T)
        ps_qt = mem.banks("ps_qt", T)
        ps_out = mem.banks("ps_out", 2)

        piece_in = [mem.sem(f"piece_in{i}") for i in range(2)]
        gains_in = mem.sem("gains_in")
        gain_made = mem.sem("gain_made")
        wk_scaled = mem.sem("wk_scaled")
        w_hi = mem.sem("w_hi")
        w_lo = mem.sem("w_lo")
        x_loaded = mem.sem("x_loaded")
        x_stats = mem.sem("x_stats")
        x_moments = mem.sem("x_moments")
        x_var = mem.sem("x_var")
        x_root = mem.sem("x_root")
        x_normed = mem.sem("x_normed")
        xt_ready = mem.sem("xt_ready")
        xt_hi = mem.sem("xt_hi")
        xt_lo = mem.sem("xt_lo")
        q_ready = mem.sem("q_ready")
        q_copied = mem.sem("q_copied")
        q_summed = mem.sem("q_summed")
        q_root = mem.sem("q_root")
        q_scaled = mem.sem("q_scaled")
        qt_ready = mem.sem("qt_ready")
        qt_hi = mem.sem("qt_hi")
        qt_lo = mem.sem("qt_lo")
        out_ready = mem.sem("out_ready")
        out_by_act = mem.sem("out_by_act")
        out_by_dve = mem.sem("out_by_dve")
        stored = [mem.sem(f"stored{i}") for i in range(2)]

        wk_flat = wk_t.rearrange("d h c -> d (h c)")
        wk_hl_flat = [w[:, :, :].rearrange("p h c -> p (h c)") for w in wk_hl]
        PW = H * D
        WK_PIECES = H * C // PW
        pieces = [("wq", n) for n in range(HG - 1)] + [("wk", 0), ("wq", HG - 1)]
        pieces += [("wk", n) for n in range(1, WK_PIECES)]
        PIECES = len(pieces)
        SPLIT_BEFORE = {0: (0, 1), 1: (2,), 2: (3,), 3: (4,)}
        SPLIT_AFTER = range(5, PIECES)

        def scaled_before(k):
            return sum(kind == "wk" for kind, _ in pieces[:k + 1])

        def half_of_piece(k, which):
            kind, n = pieces[k]
            if kind == "wq":
                return wq_hl[which][:, :, n * BANK:(n + 1) * BANK]
            return wk_hl_flat[which][:, n * PW:(n + 1) * PW]

        def raw_piece(k):
            if pieces[k][0] == "wq":
                return piece[k % 2][:, :].rearrange("p (c n) -> p c n", c=MC)
            return piece[k % 2][:, :]

        def each_block(eng, block_of):
            block_of(0, True, False)
            with eng.Fori(1, BLOCKS - 1) as i:
                block_of(i, False, False)
            block_of(BLOCKS - 1, False, True)

        with nc.Block() as block:
            @block.sync
            def _(sp):
                def load_x(i):
                    sp.wait_ge(x_normed, T * i)
                    sp.dma_start(x_in[:, :, :], x_blocks[i]).then_inc(x_loaded, 16)

                sp.dma_start(x_in[:, :, :], x_blocks[0]).then_inc(x_loaded, 16)
                sp.dma_start(gain[:, 0:1], gq.rearrange("(d a) -> d a", a=1)).then_inc(gains_in, 16)
                sp.dma_start(gain[:, 1:2], gk.rearrange("(d a) -> d a", a=1)).then_inc(gains_in, 16)
                for k in range(PIECES):
                    if k >= 2:
                        sp.wait_ge(w_lo, k - 1)
                    kind, n = pieces[k]
                    src = wq_rows[:, :, n * BANK:(n + 1) * BANK] if kind == "wq" else wk_flat[:, n * PW:(n + 1) * PW]
                    sp.dma_start(raw_piece(k), src).then_inc(piece_in[k % 2], 16)
                    if k == 1:
                        load_x(1)

                def store(i, n):
                    sp.wait_ge(out_by_act, 2 * (HG * i + n) + 2)
                    sp.wait_ge(out_by_dve, 2 * (HG * i + n) + 2)
                    for c in range(CC):
                        sp.dma_start(out_blocks[i, :, :, c, 4 * Q * n:4 * Q * (n + 1)],
                                     staged[n % 2][:, :, c, :]).then_inc(stored[n % 2], 16)

                def block_of(i, first, last):
                    for n in range(HG):
                        if n == 0 and not first and not last:
                            load_x(i + 1)
                        if n >= 2:
                            store(i, n - 2)
                        elif not first:
                            store(i - 1, n + HG - 2)
                each_block(sp, block_of)
                store(BLOCKS - 1, HG - 2)
                store(BLOCKS - 1, HG - 1)
                for s in stored:
                    sp.wait_ge(s, 16 * CC * BLOCKS * HG // 2)

            def norm_stats(dve, i):
                for t in range(T):
                    if t == 0:
                        dve.wait_ge(x_loaded, 16 * (i + 1))
                    dve.bn_stats(stats[:, t, :], x_in[:, t, :]).then_inc(x_stats, 1)
                dve.wait_ge(x_stats, T * (i + 1))
                dve.memset(spare[:, :], 0.0)
                for t in range(T):
                    dve.bn_aggr(moments[:, t, :], stats[:, t, :]).then_inc(x_moments, 1)

            def norm_apply(dve, i):
                for t in range(T):
                    dve.wait_ge(x_root, T * i + t + 1)
                    dve.tensor_scalar(x_norm[:, t, :], x_in[:, t, :], moments[:, t, 0:1], x_rstd[:, t, 1:2],
                                      ALU.subtract, ALU.mult).then_inc(x_normed, 1)

            def norm_root(pool, i):
                for t in range(T):
                    pool.wait_ge(x_moments, T * i + t + 1)
                    pool.tensor_tensor(x_rstd[:, t, 0:1], moments[:, t, 1:2], eps[:, 0:1],
                                       ALU.add).then_inc(x_var, 1)
                    pool.wait_ge(x_var, T * i + t + 1)
                    pool.tensor_tensor(x_rstd[:, t, 1:2], x_rstd[:, t, 0:1], minus_half[:, 0:1],
                                       ALU.pow).then_inc(x_root, 1)

            @block.tensor
            def _(pe):
                def x_transposes(i):
                    for t in range(T):
                        pe.wait_ge(x_normed, T * i + t + 1)
                        for c in range(MC):
                            done = pe.transpose(ps_xt[t][:, c * P:(c + 1) * P], x_norm[:, t, c * P:(c + 1) * P],
                                                ident[:, :])
                        done.then_inc(xt_ready, 1)

                def project(i, n, first):
                    if first:
                        pe.wait_ge(w_lo, pieces.index(("wq", n)) + 1)
                    for t in range(T):
                        if n == 0:
                            pe.wait_ge(xt_lo, T * (i + 1))
                        if not (first and n == 0):
                            pe.wait_ge(q_copied, T * (HG * i + n) + t - 1)
                        for c in range(MC):
                            done = three_products(
                                pe, ps_q[t][:, :], [w[:, c, t * P:(t + 1) * P] for w in x_hl],
                                [w[:, c, n * BANK:(n + 1) * BANK] for w in wq_hl], c == 0, c == MC - 1)
                        done.then_inc(q_ready, 1)

                def q_transposes(i, n, first):
                    for t in range(T):
                        pe.wait_ge(q_scaled, T * (HG * i + n) + t + 1)
                        if not (first and n == 0):
                            pe.wait_ge(qt_lo, T * (HG * i + n) + t - 1)
                        for h in range(4):
                            done = pe.transpose(ps_qt[t][:, h * P:(h + 1) * P], q_sb[:, n % 2, t, h, :],
                                                ident[:, :])
                        done.then_inc(qt_ready, 1)

                def through_wk(i, n, first):
                    if first and n == 0:
                        pe.wait_ge(w_lo, pieces.index(("wk", 0)) + 1)
                    pe.wait_ge(qt_lo, T * (HG * i + n) + T)
                    for h in range(4):
                        if not (first and n == 0 and h < 2):
                            pe.wait_ge(out_by_act if h % 2 == 0 else out_by_dve, 2 * (HG * i + n) + h // 2)
                        for c in range(CC):
                            done = three_products(
                                pe, ps_out[h % 2][:, c * W:(c + 1) * W],
                                [w[:, 4 * n + h, c * P:(c + 1) * P] for w in wk_hl],
                                [w[:, h, :] for w in q_hl[n % 2]], True, True)
                        done.then_inc(out_ready, 1)

                x_transposes(0)

                def block_of(i, first, last):
                    for n in range(HG):
                        project(i, n, first)
                        if n == HG - 1 and not last:
                            x_transposes(i + 1)
                        if n >= 1:
                            q_transposes(i, n - 1, first)
                        elif not first:
                            q_transposes(i - 1, HG - 1, False)
                        if n >= 2:
                            through_wk(i, n - 2, first)
                        elif not first:
                            through_wk(i - 1, n + HG - 2, False)
                    if first:
                        pe.wait_ge(w_lo, PIECES)
                each_block(pe, block_of)
                q_transposes(BLOCKS - 1, HG - 1, False)
                through_wk(BLOCKS - 1, HG - 2, False)
                through_wk(BLOCKS - 1, HG - 1, False)

            @block.scalar
            def _(act):
                def split_high(k):
                    if pieces[k][0] == "wq":
                        act.wait_ge(piece_in[k % 2], 16 * (k // 2 + 1))
                    else:
                        act.wait_ge(wk_scaled, scaled_before(k))
                    act.activation(half_of_piece(k, 0), raw_piece(k), ACT.Copy).then_inc(w_hi, 1)

                def x_high(i, first):
                    for t in range(T):
                        act.wait_ge(xt_ready, T * i + t + 1)
                        if t == 0 and not first:
                            act.wait_ge(q_ready, T * HG * i)
                        act.activation(x_hl[0][:, :, t * P:(t + 1) * P],
                                       ps_xt[t][:, :].rearrange("p (c w) -> p c w", c=MC),
                                       ACT.Copy).then_inc(xt_hi, 1)

                def q_copy(i, n, first):
                    for t in range(T):
                        act.wait_ge(q_ready, T * (HG * i + n) + t + 1)
                        if not (first and n < 2):
                            act.wait_ge(qt_ready, T * (HG * i + n - 2) + t + 1)
                        act.activation(q_sb[:, n % 2, t, :, :],
                                       ps_q[t][:, :].rearrange("p (h d) -> p h d", h=4),
                                       ACT.Copy).then_inc(q_copied, 1)

                def q_high(i, n, first):
                    for t in range(T):
                        act.wait_ge(qt_ready, T * (HG * i + n) + t + 1)
                        if not (first and n < 2):
                            act.wait_ge(out_ready, 4 * (HG * i + n - 2) + 4)
                        act.activation(q_hl[n % 2][0][:, :, t * P:(t + 1) * P],
                                       ps_qt[t][:, :].rearrange("p (h w) -> p h w", h=4),
                                       ACT.Copy).then_inc(qt_hi, 1)

                def read_out(i, n, first):
                    if not (first and n < 2):
                        act.wait_ge(stored[n % 2], 16 * CC * (HG // 2 * i + n // 2))
                    for h in (0, 2):
                        act.wait_ge(out_ready, 4 * (HG * i + n) + h + 1)
                        act.activation(
                            staged[n % 2][:, :, :, h * Q:(h + 1) * Q].rearrange("p b c q -> p c b q"),
                            ps_out[h % 2][:, :].rearrange("p (c b q) -> p c b q", c=CC, q=Q),
                            ACT.Copy).then_inc(out_by_act, 1)

                x_high(0, True)

                def block_of(i, first, last):
                    for n in range(HG):
                        if first:
                            for k in SPLIT_BEFORE[n]:
                                split_high(k)
                        q_copy(i, n, first)
                        if n == HG - 1 and not last:
                            x_high(i + 1, False)
                        if n >= 1:
                            q_high(i, n - 1, first)
                        elif not first:
                            q_high(i - 1, HG - 1, False)
                        if n >= 2:
                            read_out(i, n - 2, first)
                        elif not first:
                            read_out(i - 1, n + HG - 2, False)
                    if first:
                        for k in SPLIT_AFTER:
                            split_high(k)
                each_block(act, block_of)
                q_high(BLOCKS - 1, HG - 1, False)
                read_out(BLOCKS - 1, HG - 2, False)
                read_out(BLOCKS - 1, HG - 1, False)

            @block.vector
            def _(dve):
                norm_stats(dve, 0)
                norm_apply(dve, 0)
                dve.wait_ge(gains_in, 32)
                dve.tensor_tensor(gain[:, 2:3], gain[:, 0:1], gain[:, 1:2], ALU.mult).then_inc(gain_made, 1)
                def split_low(k):
                    if pieces[k][0] == "wk":
                        dve.wait_ge(gain_made, 1)
                        dve.wait_ge(piece_in[k % 2], 16 * (k // 2 + 1))
                        dve.tensor_scalar(raw_piece(k), raw_piece(k), gain[:, 2:3], float(D) ** -0.5,
                                          ALU.mult, ALU.mult).then_inc(wk_scaled, 1)
                    dve.wait_ge(w_hi, k + 1)
                    dve.tensor_tensor(half_of_piece(k, 1), raw_piece(k), half_of_piece(k, 0).bitcast(F32),
                                      ALU.subtract).then_inc(w_lo, 1)

                def x_low(i):
                    for t in range(T):
                        dve.wait_ge(xt_hi, T * i + t + 1)
                        dve.tensor_tensor(x_hl[1][:, :, t * P:(t + 1) * P],
                                          ps_xt[t][:, :].rearrange("p (c w) -> p c w", c=MC),
                                          x_hl[0][:, :, t * P:(t + 1) * P].bitcast(F32),
                                          ALU.subtract).then_inc(xt_lo, 1)

                def q_squares(i, n, first):
                    for t in range(T):
                        dve.wait_ge(q_copied, T * (HG * i + n) + t + 1)
                        if not (first and n < 2):
                            dve.wait_ge(q_root, T * (HG * i + n - 2) + t + 1)
                        if not (first and n == 0):
                            dve.wait_ge(q_summed, T * (HG * i + n - 1) + t + 1)
                        for h in range(4):
                            done = dve.tensor_tensor_reduce(
                                q_sq[:, t, h, :], q_sb[:, n % 2, t, h, :], q_sb[:, n % 2, t, h, :], 1.0 / D, EPS,
                                ALU.mult, ALU.add, q_var[:, n % 2, t, h:h + 1])
                        done.then_inc(q_summed, 1)

                def q_low(i, n):
                    for t in range(T):
                        dve.wait_ge(qt_hi, T * (HG * i + n) + t + 1)
                        dve.tensor_tensor(q_hl[n % 2][1][:, :, t * P:(t + 1) * P],
                                          ps_qt[t][:, :].rearrange("p (h w) -> p h w", h=4),
                                          q_hl[n % 2][0][:, :, t * P:(t + 1) * P].bitcast(F32),
                                          ALU.subtract).then_inc(qt_lo, 1)

                def read_out(i, n, first):
                    if not (first and n < 2):
                        dve.wait_ge(stored[n % 2], 16 * CC * (HG // 2 * i + n // 2))
                    for h in (1, 3):
                        dve.wait_ge(out_ready, 4 * (HG * i + n) + h + 1)
                        dve.tensor_copy(
                            staged[n % 2][:, :, :, h * Q:(h + 1) * Q].rearrange("p b c q -> p c b q"),
                            ps_out[h % 2][:, :].rearrange("p (c b q) -> p c b q", c=CC, q=Q),
                        ).then_inc(out_by_dve, 1)

                x_low(0)

                def block_of(i, first, last):
                    for n in range(HG):
                        if first:
                            for k in SPLIT_BEFORE[n]:
                                split_low(k)
                        q_squares(i, n, first)
                        if n == HG - 1 and not last:
                            x_low(i + 1)
                        if n >= 1:
                            q_low(i, n - 1)
                        elif not first:
                            q_low(i - 1, HG - 1)
                        if n >= 2:
                            read_out(i, n - 2, first)
                        elif not first:
                            read_out(i - 1, n + HG - 2, False)
                        if n == 0 and not last:
                            norm_stats(dve, i + 1)
                        if n == 1 and not last:
                            dve.wait_ge(xt_ready, T * (i + 1))
                            norm_apply(dve, i + 1)
                    if first:
                        for k in SPLIT_AFTER:
                            split_low(k)
                each_block(dve, block_of)
                q_low(BLOCKS - 1, HG - 1)
                read_out(BLOCKS - 1, HG - 2, False)
                read_out(BLOCKS - 1, HG - 1, False)

            @block.gpsimd
            def _(pool):
                norm_root(pool, 0)

                def q_norm(i, n):
                    for t in range(T):
                        at = T * (HG * i + n) + t + 1
                        pool.wait_ge(q_summed, at)
                        pool.tensor_tensor(q_rstd[:, n % 2, t, :], q_var[:, n % 2, t, :], minus_half[:, 0:4],
                                           ALU.pow).then_inc(q_root, 1)
                        pool.wait_ge(q_root, at)
                        pool.tensor_tensor(q_sb[:, n % 2, t, :, :], q_sb[:, n % 2, t, :, :],
                                           q_rstd[:, n % 2, t, :].unsqueeze(2).to_broadcast([P, 4, D]),
                                           ALU.mult).then_inc(q_scaled, 1)

                def block_of(i, first, last):
                    for n in range(HG):
                        q_norm(i, n)
                        if n == 0 and not last:
                            norm_root(pool, i + 1)
                each_block(pool, block_of)


def attend(nc, ctx_t, ctx_rows, ctx_last, last_t, wk, scores_scratch, values_scratch, ident, minus_half, eps):
    B, _, CC, SP2 = ctx_t.shape
    ST = 2
    L = ST * P
    S = L + 1
    HD = wk.shape[1]
    C = CC * P
    H = HD // P
    HG = H // 4
    Q = P // 4
    KN = HD // BANK
    UNITS = ST * KN
    LAST = 2 * Q + 1
    wk_rows = wk.rearrange("(c p) (j n) -> j p c n", p=P, n=BANK)

    def within(i, k):
        return not isinstance(i, int) or 0 <= 2 * i + k < B

    with ExitStack() as stack:
        mem = Memory(nc, stack, "a")
        piece = [mem.sbuf(f"piece{i}", [P, CC, BANK]) for i in range(KN)]
        wk_hl = mem.pair("wk", [P, CC, HD])
        last_in = mem.sbuf("last_in", [P, CC, P])
        last_hl = mem.pair("last", [P, CC, P])
        ctx_t_in = [mem.sbuf(f"ctx_t_in{i}", [P, CC, SP2]) for i in range(2)]
        ctx_t_hl = [mem.pair(f"ctx_t{i}", [P, CC, SP2]) for i in range(2)]
        rows_in = [mem.sbuf(f"rows_in{i}", [P, ST, C]) for i in range(2)]
        row_in = [mem.sbuf(f"row_in{i}", [LAST, C]) for i in range(2)]
        rows_hl = mem.pair("rows", [P, ST, C])
        row_parts = mem.sbuf("row_parts", [LAST, C], F32R)
        q_in = [mem.sbuf(f"q_in{i}", [P, CC, H * Q]) for i in range(2)]
        q_hl = mem.pair("q", [P, CC, H * Q])
        k_sq = [mem.sbuf(f"k_sq{i}", [P, BANK]) for i in range(2)]
        k_ms = mem.sbuf("k_ms", [P, ST, H])
        k_var = mem.sbuf("k_var", [P, ST, H])
        k_rstd = mem.sbuf("k_rstd", [P, ST, H])
        last_ms = mem.sbuf("last_ms", [P, H])
        last_var = mem.sbuf("last_var", [P, H])
        last_rstd = mem.sbuf("last_rstd", [P, H])
        last_factor = mem.sbuf("last_factor", [P, HG, P])
        factor = mem.sbuf("factor", [P, HG, S])
        scaled = mem.sbuf("scaled", [P, HG, S])
        top = mem.sbuf("top", [P, HG])
        minus_top = mem.sbuf("minus_top", [P, HG])
        probs = mem.sbuf("probs", [P, HG, S])
        total = mem.sbuf("total", [P, HG])
        share = mem.sbuf("share", [P, HG])
        probs_hl = mem.pair("probs", [P, ST, H * Q])
        prob_parts = mem.sbuf("prob_parts", [LAST, H * Q], F32R)
        out_sb = [mem.sbuf(f"out_sb{i}", [P, CC, H * Q]) for i in range(2)]
        spare = mem.sbuf("spare", [P, 1])
        zeros = mem.sbuf("zeros", [Q + H, L])
        spread_f32 = mem.sbuf("spread_f32", [Q + H, HG, P])
        spread = mem.sbuf("spread", [Q + H, HG, P], F32R)
        turned_parts = mem.sbuf("turned_parts", [Q + H, L], F32R)
        spare2 = mem.sbuf("spare2", [P, 1])
        ps_scores = mem.banks("ps_scores", HG)
        ps_keys = mem.banks("ps_keys", 2)
        ps_turn = mem.banks("ps_turn", 2)

        piece_in = [mem.sem(f"piece_in{i}") for i in range(KN)]
        wk_hi = mem.sem("wk_hi")
        wk_lo = mem.sem("wk_lo")
        padded = mem.sem("padded")
        last_loaded = mem.sem("last_loaded")
        last_hi = mem.sem("last_hi")
        last_lo = mem.sem("last_lo")
        ctx_t_loaded = [mem.sem(f"ctx_t_loaded{i}") for i in range(2)]
        rows_loaded = [mem.sem(f"rows_loaded{i}") for i in range(2)]
        q_loaded = [mem.sem(f"q_loaded{i}") for i in range(2)]
        ctx_t_hi = mem.sem("ctx_t_hi")
        ctx_t_lo = mem.sem("ctx_t_lo")
        rows_hi = mem.sem("rows_hi")
        rows_lo = mem.sem("rows_lo")
        row_lo = mem.sem("row_lo")
        q_hi = mem.sem("q_hi")
        q_lo = mem.sem("q_lo")
        keys_ready = mem.sem("keys_ready")
        keys_squared = mem.sem("keys_squared")
        keys_summed = mem.sem("keys_summed")
        keys_var = mem.sem("keys_var")
        keys_root = mem.sem("keys_root")
        spread_filled = mem.sem("spread_filled")
        spread_made = mem.sem("spread_made")
        turned = mem.sem("turned")
        turned_hi = mem.sem("turned_hi")
        turned_lo = mem.sem("turned_lo")
        last_turned = mem.sem("last_turned")
        last_kept = mem.sem("last_kept")
        factor_turned = mem.sem("factor_turned")
        factor_out = mem.sem("factor_out")
        factor_last = mem.sem("factor_last")
        scores_ready = mem.sem("scores_ready")
        scores_scaled = mem.sem("scores_scaled")
        top_ready = mem.sem("top_ready")
        exp_ready = mem.sem("exp_ready")
        share_ready = mem.sem("share_ready")
        probs_ready = mem.sem("probs_ready")
        probs_turned = mem.sem("probs_turned")
        probs_hi = mem.sem("probs_hi")
        probs_lo = mem.sem("probs_lo")
        out_ready = mem.sem("out_ready")
        out_copied = mem.sem("out_copied")
        stored = [mem.sem(f"stored{i}") for i in range(2)]

        def unit(i, k, u):
            return 2 * UNITS * i + UNITS * k + KN + u

        def by_pairs(eng, one, tail):
            for k in range(2):
                one(0, k)
            with eng.Fori(1, B // 2 - tail) as i:
                for k in range(2):
                    one(i, k)
            for i in range(B // 2 - tail, B // 2):
                for k in range(2):
                    one(i, k)

        with nc.Block() as block:
            @block.sync
            def _(sp):
                def load_ctx_t(i, k):
                    if within(i, k - 2):
                        sp.wait_ge(ctx_t_lo, 2 * i + k - 1)
                    sp.dma_start(ctx_t_in[k % 2][:, :, :], ctx_t[2 * i + k]).then_inc(ctx_t_loaded[k % 2], 16)

                def load_rows(i, k):
                    if within(i, k - 2):
                        sp.wait_ge(rows_lo, 2 * i + k - 1)
                        sp.wait_ge(row_lo, 2 * i + k - 1)
                    b = 2 * i + k
                    sp.dma_start(rows_in[k % 2][:, :, :],
                                 ctx_rows[b].rearrange("(t p) c -> p t c", p=P)).then_inc(rows_loaded[k % 2], 16)
                    sp.dma_start(row_in[k % 2][0:LAST:Q, :],
                                 ctx_last[b].to_broadcast([3, C])).then_inc(rows_loaded[k % 2], 16)

                def load_q(i, k):
                    if within(i, k - 2):
                        sp.wait_ge(q_lo, 2 * i + k - 1)
                    sp.dma_start(q_in[k % 2][:, :, :],
                                 scores_scratch[2 * i + k].rearrange("p c h q -> p c (h q)")
                                 ).then_inc(q_loaded[k % 2], 16)

                def store(i, k):
                    sp.wait_ge(out_copied, CC * (2 * i + k + 1))
                    sp.dma_start(values_scratch[2 * i + k].rearrange("p c h q -> p c (h q)"),
                                 out_sb[k % 2][:, :, :]).then_inc(stored[k % 2], 16)

                sp.dma_start(piece[0][:, :, :], wk_rows[0]).then_inc(piece_in[0], 16)
                sp.wait_ge(padded, 1)
                sp.dma_start(last_in[:, :, 0:B], last_t.rearrange("(c p) b -> p c b", p=P)).then_inc(last_loaded, 16)
                for n in range(1, KN):
                    sp.dma_start(piece[n][:, :, :], wk_rows[n]).then_inc(piece_in[n], 16)
                load_ctx_t(0, 0)
                load_ctx_t(0, 1)
                load_q(0, 0)
                sp.wait_ge(padded, 3)
                load_rows(0, 0)
                load_q(0, 1)
                load_ctx_t(0, 2)

                def one(i, k):
                    if within(i, k - 1):
                        store(i, k - 1)
                    if within(i, k + 1):
                        load_rows(i, k + 1)
                    if within(i, k + 2):
                        load_q(i, k + 2)
                    if within(i, k + 3):
                        load_ctx_t(i, k + 3)
                by_pairs(sp, one, 2)
                store(B // 2 - 1, 1)
                for s in stored:
                    sp.wait_ge(s, 16 * B // 2)

            @block.tensor
            def _(pe):
                def last_keys(n):
                    if n >= 2:
                        pe.wait_ge(keys_squared, n - 1)
                    for c in range(CC):
                        done = three_products(pe, ps_keys[n % 2][:, :], [w[:, c, :] for w in last_hl],
                                              [w[:, c, n * BANK:(n + 1) * BANK] for w in wk_hl],
                                              c == 0, c == CC - 1)
                    done.then_inc(keys_ready, 1)

                def turn_factors(count, tiles):
                    pe.wait_ge(keys_root, ST * count + 1)
                    for t, factors in enumerate(tiles):
                        done = pe.transpose(ps_turn[1][0:H, t * P:(t + 1) * P], factors, ident[:, :])
                    done.then_inc(turned, 1)

                def keys(i, k, units):
                    for u in units:
                        t, n = u // KN, u % KN
                        if u == 0:
                            pe.wait_ge(ctx_t_lo, 2 * i + k + 1)
                        pe.wait_ge(keys_squared, unit(i, k, u) - 1)
                        for c in range(CC):
                            done = three_products(
                                pe, ps_keys[u % 2][:, :], [w[:, c, t * P:(t + 1) * P] for w in ctx_t_hl[k % 2]],
                                [w[:, c, n * BANK:(n + 1) * BANK] for w in wk_hl], c == 0, c == CC - 1)
                        done.then_inc(keys_ready, 1)

                def one(i, k):
                    pe.wait_ge(q_lo, 2 * i + k + 1)
                    for g in range(HG):
                        for c in range(CC):
                            done = three_products(
                                pe, ps_scores[g][:, 0:SP2], [w[:, c, g * P:(g + 1) * P] for w in q_hl],
                                [w[:, c, :] for w in ctx_t_hl[k % 2]], c == 0, c == CC - 1)
                        done.then_inc(scores_ready, 1)
                    if within(i, k - 1):
                        pe.wait_ge(out_copied, CC * (2 * i + k))
                    turn_factors(2 * i + k + 1, [k_rstd[:, t, :] for t in range(ST)])
                    if within(i, k + 1):
                        keys(i, k + 1, range(0, 1))
                    pe.wait_ge(turned_lo, 2 * i + k + 2)
                    for g in range(HG):
                        done = pe.matmul(ps_turn[g // 2][:, g % 2 * L:(g % 2 + 1) * L], spread[:, g, :],
                                         turned_parts[:, :], start=True, stop=True)
                        if g % 2:
                            done.then_inc(factor_turned, 1)
                    if within(i, k + 1):
                        keys(i, k + 1, range(1, 5))
                    pe.wait_ge(factor_out, 2 * (2 * i + k) + 2)
                    for t in range(ST):
                        for g in range(HG):
                            if t == 0:
                                pe.wait_ge(probs_ready, HG * (2 * i + k) + g + 1)
                            done = pe.transpose(ps_turn[t][:, g * P:(g + 1) * P], probs[:, g, t * P:(t + 1) * P],
                                                ident[:, :])
                        done.then_inc(probs_turned, 1)
                    for g in range(HG):
                        done = pe.transpose(ps_scores[0][0:LAST, g * P:(g + 1) * P],
                                            probs[:, g, L:S].to_broadcast([P, LAST]), ident[:, :])
                    done.then_inc(probs_turned, 1)
                    if within(i, k + 1):
                        keys(i, k + 1, range(5, UNITS))
                    pe.wait_ge(probs_lo, 3 * (2 * i + k) + 3)
                    pe.wait_ge(rows_lo, 2 * i + k + 1)
                    pe.wait_ge(row_lo, 2 * i + k + 1)
                    for c in range(CC):
                        for t in range(ST):
                            three_products(pe, ps_turn[c][:, :], [w[:, t, c * P:(c + 1) * P] for w in rows_hl],
                                           [w[:, t, :] for w in probs_hl], t == 0, False)
                        pe.matmul(ps_turn[c][:, :], row_parts[:, c * P:(c + 1) * P], prob_parts[:, :],
                                  start=False, stop=True).then_inc(out_ready, 1)

                pe.wait_ge(last_lo, 1)
                for n in range(KN):
                    pe.wait_ge(wk_lo, n + 1)
                    last_keys(n)
                keys(0, 0, range(UNITS))
                turn_factors(0, [last_rstd[:, :]])
                pe.wait_ge(spread_made, 1)
                pe.wait_ge(turned_lo, 1)
                for g in range(HG):
                    done = pe.matmul(ps_turn[0][:, g * P:(g + 1) * P], spread[:, g, :], turned_parts[:, 0:P],
                                     start=True, stop=True)
                done.then_inc(last_turned, 1)
                pe.wait_ge(last_kept, 1)
                by_pairs(pe, one, 1)

            @block.scalar
            def _(act):
                def square(g, place, first):
                    act.wait_ge(keys_ready, g + 1)
                    if not first:
                        act.wait_ge(keys_summed, g - 1)
                    act.activation(k_sq[place][:, :], ps_keys[place][:, :], ACT.Square,
                                   scale=float(P) ** -0.5).then_inc(keys_squared, 1)

                def squares(i, k, units):
                    if within(i, k):
                        for u in units:
                            square(unit(i, k, u), u % 2, False)

                def turned_high(count, width):
                    act.wait_ge(turned, count + 1)
                    act.activation(turned_parts[0:H, 0:width], ps_turn[1][0:H, 0:width],
                                   ACT.Copy).then_inc(turned_hi, 1)

                def one(i, k):
                    turned_high(2 * i + k + 1, L)
                    squares(i, k + 1, range(0, 1))
                    if within(i, k - 1):
                        act.wait_ge(scores_scaled, HG * (2 * i + k))
                    for j in range(2):
                        act.wait_ge(factor_turned, 2 * (2 * i + k) + j + 1)
                        act.activation(factor[:, 2 * j:2 * j + 2, 0:L],
                                       ps_turn[j][:, :].rearrange("p (g s) -> p g s", g=2),
                                       ACT.Copy).then_inc(factor_out, 1)
                    squares(i, k + 1, range(1, 2))
                    if within(i, k - 1):
                        act.wait_ge(probs_turned, 3 * (2 * i + k))
                    for g in range(HG):
                        if g % 2 == 0:
                            act.wait_ge(top_ready, 2 * (2 * i + k) + g // 2 + 1)
                        act.activation(probs[:, g, :], scaled[:, g, :], ACT.Exp, bias=minus_top[:, g:g + 1],
                                       accum_out=total[:, g:g + 1]).then_inc(exp_ready, 1)
                        if g == 1:
                            squares(i, k + 1, range(2, 3))
                    squares(i, k + 1, range(3, 5))
                    if within(i, k - 1):
                        act.wait_ge(out_ready, CC * (2 * i + k))
                    for t in range(ST):
                        act.wait_ge(probs_turned, 3 * (2 * i + k) + t + 1)
                        act.activation(probs_hl[0][:, t, :], ps_turn[t][:, :], ACT.Copy).then_inc(probs_hi, 1)
                    act.wait_ge(probs_turned, 3 * (2 * i + k) + 3)
                    act.activation(prob_parts[:, :], ps_scores[0][0:LAST, :], ACT.Copy).then_inc(probs_hi, 1)
                    squares(i, k + 1, range(5, UNITS))
                    if within(i, k - 2):
                        act.wait_ge(stored[k % 2], 16 * i)
                    for c in range(CC):
                        act.wait_ge(out_ready, CC * (2 * i + k) + c + 1)
                        act.activation(out_sb[k % 2][:, c, :], ps_turn[c][:, :], ACT.Copy).then_inc(out_copied, 1)

                for n in range(KN):
                    act.wait_ge(piece_in[n], 16)
                    act.activation(wk_hl[0][:, :, n * BANK:(n + 1) * BANK], piece[n][:, :, :],
                                   ACT.Copy).then_inc(wk_hi, 1)
                for n in range(KN):
                    square(n, n % 2, n < 2)
                squares(0, 0, range(UNITS))
                turned_high(0, P)
                act.wait_ge(last_turned, 1)
                act.activation(last_factor[:, :, :], ps_turn[0][:, :].rearrange("p (g b) -> p g b", g=HG),
                               ACT.Copy).then_inc(last_kept, 1)
                by_pairs(act, one, 1)

            @block.vector
            def _(dve):
                def sum_heads(out, place):
                    dve.tensor_reduce(out, k_sq[place][:, :].rearrange("p (h d) -> p h d", h=4), AX_X,
                                      ALU.add).then_inc(keys_summed, 1)

                def sums(i, k, units):
                    if within(i, k):
                        for u in units:
                            if u % KN == 0:
                                dve.wait_ge(keys_var, ST * (2 * i + k - 1) + u // KN + 2)
                            dve.wait_ge(keys_squared, unit(i, k, u) + 1)
                            at = u % KN * 4
                            sum_heads(k_ms[:, u // KN, at:at + 4], u % 2)

                def scale(i, k, j):
                    b = 2 * i + k
                    dve.wait_ge(scores_ready, HG * b + 2 * j + 2)
                    if j == 0:
                        dve.wait_ge(factor_last, b + 1)
                    if j == 0 and within(i, k - 1):
                        dve.wait_ge(exp_ready, HG * b)
                    dve.wait_ge(factor_out, 2 * b + j + 1)
                    dve.memset(spare[:, :], 0.0)
                    for g in (2 * j, 2 * j + 1):
                        dve.tensor_tensor_reduce(scaled[:, g, :], ps_scores[g][:, 0:S], factor[:, g, :], 1.0, LOWEST,
                                                 ALU.mult, ALU.max, top[:, g:g + 1]).then_inc(scores_scaled, 1)
                    dve.wait_ge(scores_scaled, HG * b + 2 * j + 2)
                    dve.tensor_scalar(minus_top[:, 2 * j:2 * j + 2], top[:, 2 * j:2 * j + 2], -1.0, None,
                                      ALU.mult).then_inc(top_ready, 1)

                def rows_high(i, k):
                    dve.wait_ge(rows_loaded[k % 2], 32 * (i + k // 2 + 1))
                    dve.tensor_copy(rows_hl[0][:, :, :], rows_in[k % 2][:, :, :]).then_inc(rows_hi, 1)
                    dve.tensor_copy(row_parts[:, :], row_in[k % 2][:, :]).then_inc(rows_hi, 1)
                    dve.wait_ge(rows_hi, 2 * (2 * i + k) + 2)
                    dve.tensor_tensor(row_parts[Q:Q + 1, :], row_in[k % 2][Q:Q + 1, :],
                                      row_parts[Q:Q + 1, :].bitcast(F32), ALU.subtract).then_inc(row_lo, 1)

                def q_high(i, k):
                    dve.wait_ge(q_loaded[k % 2], 16 * (i + k // 2 + 1))
                    dve.tensor_copy(q_hl[0][:, :, :], q_in[k % 2][:, :, :]).then_inc(q_hi, 1)

                def ctx_t_high(i, k):
                    dve.wait_ge(ctx_t_loaded[k % 2], 16 * (i + k // 2 + 1))
                    dve.tensor_copy(ctx_t_hl[k % 2][0][:, :, :], ctx_t_in[k % 2][:, :, :]).then_inc(ctx_t_hi, 1)

                def turned_low(count, width):
                    dve.wait_ge(turned_hi, count + 1)
                    dve.tensor_tensor(turned_parts[Q:Q + H, 0:width], ps_turn[1][0:H, 0:width],
                                      turned_parts[0:H, 0:width].bitcast(F32), ALU.subtract).then_inc(turned_lo, 1)

                def one(i, k):
                    b = 2 * i + k
                    if within(i, k - 1):
                        dve.wait_ge(out_ready, CC * b)
                    rows_high(i, k)
                    turned_low(b + 1, L)
                    dve.wait_ge(scores_ready, HG * b + HG)
                    if within(i, k + 1):
                        q_high(i, k + 1)
                    if within(i, k + 2):
                        ctx_t_high(i, k + 2)
                    sums(i, k + 1, range(0, 1))
                    scale(i, k, 0)
                    scale(i, k, 1)
                    sums(i, k + 1, range(1, 2))
                    dve.wait_ge(exp_ready, HG * b + HG)
                    dve.reciprocal(share[:, :], total[:, :]).then_inc(share_ready, 1)
                    dve.wait_ge(share_ready, b + 1)
                    for g in range(HG):
                        dve.tensor_scalar(probs[:, g, :], probs[:, g, :], share[:, g:g + 1], None,
                                          ALU.mult).then_inc(probs_ready, 1)
                    sums(i, k + 1, range(2, 5))
                    for t in range(ST):
                        dve.wait_ge(probs_hi, 3 * b + t + 1)
                        dve.tensor_tensor(probs_hl[1][:, t, :], ps_turn[t][:, :],
                                          probs_hl[0][:, t, :].bitcast(F32), ALU.subtract).then_inc(probs_lo, 1)
                    dve.wait_ge(probs_hi, 3 * b + 3)
                    dve.tensor_tensor(prob_parts[2 * Q:LAST, :], ps_scores[0][2 * Q:LAST, :],
                                      prob_parts[2 * Q:LAST, :].bitcast(F32), ALU.subtract).then_inc(probs_lo, 1)
                    sums(i, k + 1, range(5, UNITS))

                dve.wait_ge(last_loaded, 16)
                dve.tensor_copy(last_hl[0][:, :, :], last_in[:, :, :]).then_inc(last_hi, 1)
                dve.wait_ge(last_hi, 1)
                dve.tensor_tensor(last_hl[1][:, :, :], last_in[:, :, :], last_hl[0][:, :, :].bitcast(F32),
                                  ALU.subtract).then_inc(last_lo, 1)
                for n in range(KN):
                    dve.wait_ge(wk_hi, n + 1)
                    dve.tensor_tensor(wk_hl[1][:, :, n * BANK:(n + 1) * BANK], piece[n][:, :, :],
                                      wk_hl[0][:, :, n * BANK:(n + 1) * BANK].bitcast(F32),
                                      ALU.subtract).then_inc(wk_lo, 1)
                ctx_t_high(0, 0)
                ctx_t_high(0, 1)
                q_high(0, 0)
                dve.wait_ge(padded, 4)
                dve.tensor_copy(turned_parts[:, :], zeros[:, :])
                dve.wait_ge(spread_filled, 3)
                dve.tensor_copy(spread[:, :, :], spread_f32[:, :, :]).then_inc(spread_made, 1)
                for n in range(KN):
                    dve.wait_ge(keys_squared, n + 1)
                    sum_heads(last_ms[:, 4 * n:4 * n + 4], n % 2)
                for u in range(UNITS):
                    dve.wait_ge(keys_squared, unit(0, 0, u) + 1)
                    sum_heads(k_ms[:, u // KN, u % KN * 4:u % KN * 4 + 4], u % 2)
                turned_low(0, P)
                by_pairs(dve, one, 1)

            @block.gpsimd
            def _(pool):
                def q_low(i, k):
                    pool.wait_ge(q_hi, 2 * i + k + 1)
                    pool.tensor_tensor(q_hl[1][:, :, :], q_in[k % 2][:, :, :], q_hl[0][:, :, :].bitcast(F32),
                                       ALU.subtract).then_inc(q_lo, 1)

                def ctx_t_low(i, k):
                    pool.wait_ge(ctx_t_hi, 2 * i + k + 1)
                    pool.tensor_tensor(ctx_t_hl[k % 2][1][:, :, :], ctx_t_in[k % 2][:, :, :],
                                       ctx_t_hl[k % 2][0][:, :, :].bitcast(F32), ALU.subtract).then_inc(ctx_t_lo, 1)

                def rows_low(i, k):
                    pool.wait_ge(rows_hi, 2 * (2 * i + k) + 2)
                    pool.tensor_tensor(rows_hl[1][:, :, :], rows_in[k % 2][:, :, :], rows_hl[0][:, :, :].bitcast(F32),
                                       ALU.subtract).then_inc(rows_lo, 1)

                def roots(i, k, t):
                    done = ST * (2 * i + k) + t + 1
                    pool.wait_ge(keys_summed, unit(i, k, (t + 1) * KN))
                    pool.tensor_tensor(k_var[:, t, :], k_ms[:, t, :], eps[:, 0:1].to_broadcast([P, H]),
                                       ALU.add).then_inc(keys_var, 1)
                    pool.wait_ge(turned, 2 * i + k + 1)
                    pool.wait_ge(keys_var, done + 1)
                    pool.tensor_tensor(k_rstd[:, t, :], k_var[:, t, :], minus_half[:, 0:1].to_broadcast([P, H]),
                                       ALU.pow).then_inc(keys_root, 1)

                def one(i, k):
                    if within(i, k - 1):
                        pool.wait_ge(scores_scaled, HG * (2 * i + k))
                        pool.tensor_tensor(spare2[:, :], eps[:, 0:1], eps[:, 0:1], ALU.add)
                    pool.tensor_copy(factor[:, :, L:S], last_factor[:, :, bass.ds(2 * i + k, 1)]).then_inc(factor_last, 1)
                    rows_low(i, k)
                    if within(i, k + 1):
                        q_low(i, k + 1)
                    if within(i, k + 2):
                        ctx_t_low(i, k + 2)
                    if within(i, k + 1):
                        for t in range(ST):
                            roots(i, k + 1, t)

                pool.memset(last_in[:, :, :], 0.0).then_inc(padded, 1)
                for r in row_in:
                    pool.memset(r[:, :], 0.0).then_inc(padded, 1)
                pool.memset(zeros[:, :], 0.0).then_inc(padded, 1)
                pool.memset(spread_f32[:, :, :], 0.0).then_inc(spread_filled, 1)
                for part in range(2):
                    pool.wait_ge(spread_filled, part + 1)
                    view = spread_f32[:, :, :].rearrange("p g (h q) -> p (g h) q", h=4)
                    pool.affine_select(out=view, in_=view, compare_op=ALU.not_equal, fill=1.0, base=part * Q,
                                       pattern=[[1, H], [0, Q]], channel_multiplier=-1).then_inc(spread_filled, 1)
                ctx_t_low(0, 0)
                ctx_t_low(0, 1)
                q_low(0, 0)
                pool.wait_ge(keys_summed, KN)
                pool.tensor_tensor(last_var[:, :], last_ms[:, :], eps[:, 0:1].to_broadcast([P, H]),
                                   ALU.add).then_inc(keys_var, 1)
                pool.wait_ge(keys_var, 1)
                pool.tensor_tensor(last_rstd[:, :], last_var[:, :], minus_half[:, 0:1].to_broadcast([P, H]),
                                   ALU.pow).then_inc(keys_root, 1)
                for t in range(ST):
                    roots(0, 0, t)
                pool.wait_ge(last_kept, 1)
                by_pairs(pool, one, 1)


def project_values(nc, x, wv, wo, values_scratch, x_res):
    B, Q, M = x.shape
    _, _, CC, H, _ = values_scratch.shape
    D = wv.shape[1] // H
    HG = H // 4
    BT = P // Q
    T = 2
    W = T * P
    BLOCKS = B // (T * BT)
    LAST = BLOCKS - 1
    x_blocks = x.rearrange("(i t b) q m -> i (b q) t m", t=T, b=BT)
    in_blocks = values_scratch.rearrange("(i b) p c h q -> i p b c (h q)", b=T * BT)
    wv_groups = wv.rearrange("(c p) (g n) -> g p c n", p=P, n=BANK)
    wo_groups = wo.rearrange("(g h d) m -> g d h m", h=4, d=D)

    with ExitStack() as stack:
        mem = Memory(nc, stack, "v")
        piece = [mem.sbuf(f"piece{i}", [P, 4 * BANK]) for i in range(2)]
        wv_hl = mem.pair("wv", [P, CC, H * D])
        wo_hl = mem.pair("wo", [P, H, M])
        u_in = [mem.sbuf(f"u_in{i}", [P, T * BT, CC, 4 * Q]) for i in range(2)]
        u_hl = mem.pair("u", [P, T * BT, CC, 4 * Q])
        o_hl = [mem.pair(f"o{i}", [P, 4, W]) for i in range(2)]
        x_in = mem.sbuf("x_in", [P, T, M])
        ps_o = mem.banks("ps_o", 4)
        ps_y = mem.banks("ps_y", T)
        piece_in = [mem.sem(f"piece_in{i}") for i in range(2)]
        w_hi = mem.sem("w_hi")
        w_lo = mem.sem("w_lo")
        u_loaded = [mem.sem(f"u_loaded{i}") for i in range(2)]
        x_loaded = mem.sem("x_loaded")
        u_hi = mem.sem("u_hi")
        u_lo = mem.sem("u_lo")
        o_ready = mem.sem("o_ready")
        o_hi = mem.sem("o_hi")
        o_lo = mem.sem("o_lo")
        y_ready = mem.sem("y_ready")
        y_added = mem.sem("y_added")

        pieces = [("wv", 0), ("wv", 1)] + [(kind, g + 2 * (kind == "wv")) for g in range(HG)
                                           for kind in ("wo", "wv") if g + 2 * (kind == "wv") < HG]
        PIECES = len(pieces)
        SPLIT_BEFORE = {0: (0, 1), 1: (2, 3), 2: (4, 5), 3: (6,)}
        SPLIT_AFTER = (7,)
        LOAD_AFTER = {0: (4, 5), 1: (6, 7)}

        def raw_piece(k):
            if pieces[k][0] == "wv":
                return piece[k % 2][:, 0:CC * BANK].rearrange("p (c n) -> p c n", c=CC)
            return piece[k % 2][:, :].rearrange("p (h m) -> p h m", h=4)

        def half_of_piece(k, which):
            kind, g = pieces[k]
            return wv_hl[which][:, :, g * BANK:(g + 1) * BANK] if kind == "wv" else wo_hl[which][:, 4 * g:4 * g + 4, :]

        def each_block(eng, block_of, peel_last=1):
            block_of(0)
            with eng.Fori(1, BLOCKS - peel_last) as i:
                block_of(i)
            for i in range(BLOCKS - peel_last, BLOCKS):
                block_of(i)

        def after(i, n, steps):
            return not isinstance(i, int) or HG * i + n >= steps

        with nc.Block() as block:
            @block.sync
            def _(sp):
                def load(i, n):
                    if after(i, n, 2):
                        sp.wait_ge(u_lo, HG * i + n - 1)
                    for c in range(CC):
                        sp.dma_start(u_in[n % 2][:, :, c, :],
                                     in_blocks[i + n // HG, :, :, c, 4 * Q * (n % HG):4 * Q * (n % HG + 1)]
                                     ).then_inc(u_loaded[n % 2], 16)

                def load_piece(k):
                    if k >= 2:
                        sp.wait_ge(w_lo, k - 1)
                    kind, g = pieces[k]
                    sp.dma_start(raw_piece(k), (wv_groups if kind == "wv" else wo_groups)[g]
                                 ).then_inc(piece_in[k % 2], 16)

                load(0, 0)
                for k in range(2):
                    load_piece(k)
                load(0, 1)
                for k in range(2, 4):
                    load_piece(k)

                def block_of(i):
                    for n in range(HG):
                        if n == 2:
                            if after(i, 0, 1):
                                sp.wait_ge(y_added, T * i)
                            sp.dma_start(x_in[:, :, :], x_blocks[i]).then_inc(x_loaded, 16)
                        if not (isinstance(i, int) and i == LAST and n >= HG - 2):
                            load(i, n + 2)
                        if isinstance(i, int) and i == 0:
                            for k in LOAD_AFTER.get(n, ()):
                                load_piece(k)
                each_block(sp, block_of)

            @block.tensor
            def _(pe):
                def through_wv(i, n):
                    if isinstance(i, int) and i == 0:
                        pe.wait_ge(w_lo, pieces.index(("wv", n)) + 1)
                    pe.wait_ge(u_lo, HG * i + n + 1)
                    for h in range(4):
                        bank = ps_o[n % 2 * 2 + h // 2]
                        if h % 2 == 0 and after(i, n, 2):
                            pe.wait_ge(o_lo, 2 * (HG * i + n - 2) + h // 2 + 1)
                        for c in range(CC):
                            done = three_products(
                                pe, bank[:, h % 2 * W:(h % 2 + 1) * W],
                                [w[:, c, (4 * n + h) * D:(4 * n + h + 1) * D] for w in wv_hl],
                                [w[:, :, c, h * Q:(h + 1) * Q] for w in u_hl], c == 0, c == CC - 1)
                        if h % 2:
                            done.then_inc(o_ready, 1)

                def through_wo(i, n):
                    pe.wait_ge(o_lo, 2 * (HG * i + n) + 2)
                    if isinstance(i, int) and i == 0:
                        pe.wait_ge(w_lo, pieces.index(("wo", n)) + 1)
                    for t in range(T):
                        if n == 0 and after(i, n, 1):
                            pe.wait_ge(y_added, T * (i - 1) + t + 1)
                        for h in range(4):
                            done = three_products(
                                pe, ps_y[t][:, :], [w[:, h, t * P:(t + 1) * P] for w in o_hl[n % 2]],
                                [w[:, 4 * n + h, :] for w in wo_hl], n == 0 and h == 0, n == HG - 1 and h == 3)
                        if n == HG - 1:
                            done.then_inc(y_ready, 1)

                def block_of(i):
                    for n in range(HG):
                        through_wv(i, n)
                        if n >= 1:
                            through_wo(i, n - 1)
                        elif after(i, n, 1):
                            through_wo(i - 1, HG - 1)
                    if isinstance(i, int) and i == 0:
                        pe.wait_ge(w_lo, PIECES)
                each_block(pe, block_of)
                through_wo(LAST, HG - 1)

            @block.scalar
            def _(act):
                def piece_high(k):
                    act.wait_ge(piece_in[k % 2], 16 * (k // 2 + 1))
                    act.activation(half_of_piece(k, 0), raw_piece(k), ACT.Copy).then_inc(w_hi, 1)

                def u_high(i, n):
                    act.wait_ge(u_loaded[n % 2], 16 * CC * (HG // 2 * i + n // 2 + 1))
                    if after(i, n, 1):
                        act.wait_ge(o_ready, 2 * (HG * i + n))
                    act.activation(u_hl[0][:, :, :, :], u_in[n % 2][:, :, :, :], ACT.Copy).then_inc(u_hi, 1)

                def o_high(i, n):
                    for j in range(2):
                        act.wait_ge(o_ready, 2 * (HG * i + n) + j + 1)
                        act.activation(o_hl[n % 2][0][:, 2 * j:2 * j + 2, :],
                                       ps_o[n % 2 * 2 + j][:, :].rearrange("p (h w) -> p h w", h=2),
                                       ACT.Copy).then_inc(o_hi, 1)

                u_high(0, 0)

                def block_of(i):
                    first = isinstance(i, int) and i == 0
                    for n in range(HG):
                        if first:
                            for k in SPLIT_BEFORE[n]:
                                piece_high(k)
                        o_high(i, n)
                        if not (isinstance(i, int) and i == LAST and n == HG - 1):
                            u_high(i, n + 1)
                    if first:
                        for k in SPLIT_AFTER:
                            piece_high(k)
                each_block(act, block_of)

            @block.vector
            def _(dve):
                def piece_low(k):
                    dve.wait_ge(w_hi, k + 1)
                    dve.tensor_tensor(half_of_piece(k, 1), raw_piece(k), half_of_piece(k, 0).bitcast(F32),
                                      ALU.subtract).then_inc(w_lo, 1)

                def u_low(i, n):
                    dve.wait_ge(u_hi, HG * i + n + 1)
                    dve.tensor_tensor(u_hl[1][:, :, :, :], u_in[n % 2][:, :, :, :],
                                      u_hl[0][:, :, :, :].bitcast(F32), ALU.subtract).then_inc(u_lo, 1)

                def o_low(i, n):
                    for j in range(2):
                        dve.wait_ge(o_hi, 2 * (HG * i + n) + j + 1)
                        dve.tensor_tensor(o_hl[n % 2][1][:, 2 * j:2 * j + 2, :],
                                          ps_o[n % 2 * 2 + j][:, :].rearrange("p (h w) -> p h w", h=2),
                                          o_hl[n % 2][0][:, 2 * j:2 * j + 2, :].bitcast(F32),
                                          ALU.subtract).then_inc(o_lo, 1)

                def add(i):
                    dve.wait_ge(x_loaded, 16 * (i + 1))
                    for t in range(T):
                        dve.wait_ge(y_ready, T * i + t + 1)
                        dve.tensor_tensor(x_res[:, bass.ds(T * i + t, 1), :],
                                          ps_y[t][:, :].unsqueeze(1), x_in[:, t:t + 1, :],
                                          ALU.add).then_inc(y_added, 1)

                u_low(0, 0)

                def block_of(i):
                    first = isinstance(i, int) and i == 0
                    for n in range(HG):
                        if first:
                            for k in SPLIT_BEFORE[n]:
                                piece_low(k)
                        o_low(i, n)
                        if not (isinstance(i, int) and i == LAST and n == HG - 1):
                            u_low(i, n + 1)
                        if n == 0 and after(i, n, 1):
                            add(i - 1)
                    if first:
                        for k in SPLIT_AFTER:
                            piece_low(k)
                each_block(dve, block_of)
                add(LAST)


def self_attend(nc, wqkv_t, x_res, mixed, ident, minus_half, eps):
    M, _ = wqkv_t.shape
    MC = M // P
    D, BT = 32, 4
    Q = P // BT
    H = M // D
    HG = H // 4
    T = 4
    W = T * P
    BLOCKS = x_res.shape[1] // T
    UNITS = 2 * HG + T

    with ExitStack() as stack:
        mem = Memory(nc, stack, "s")
        piece = [mem.sbuf(f"piece{i}", [P, 3 * M]) for i in range(2)]
        w_hl = mem.pair("w", [P, MC, 3 * M])
        stats = mem.sbuf("stats", [P, T, 6])
        moments = mem.sbuf("moments", [P, T, 2])
        x_var = mem.sbuf("x_var", [P, T, 2])
        x_norm = mem.sbuf("x_norm", [P, T, M])
        x_hl = mem.pair("x", [P, MC, W])
        qk_t = mem.sbuf("qk_t", [P, 2 * HG, W])
        v_sb = mem.sbuf("v_sb", [P, T, M])
        scores = mem.sbuf("scores", [P, H, Q])
        top = mem.sbuf("top", [P, H])
        shifted = mem.sbuf("shifted", [P, H, Q])
        exps = mem.sbuf("exps", [P, H, Q])
        total = mem.sbuf("total", [P, H])
        share = mem.sbuf("share", [P, H])
        probs = mem.sbuf("probs", [P, H, Q])
        probs_t = mem.sbuf("probs_t", [P, H, Q])
        spare = mem.sbuf("spare", [P, 1])
        act_spare = mem.sbuf("act_spare", [P, T])
        own = [mem.sbuf(f"own{i}", [P, H, P]) for i in range(2)]
        ps_a = stack.enter_context(nc.psum_tensor("s_ps_a", [P, 4, BANK], F32))
        ps_b = stack.enter_context(nc.psum_tensor("s_ps_b", [P, 4, BANK], F32))

        piece_in = [mem.sem(f"piece_in{i}") for i in range(2)]
        w_hi = mem.sem("w_hi")
        w_lo = mem.sem("w_lo")
        own_zeroed = mem.sem("own_zeroed")
        x_stats = mem.sem("x_stats")
        x_moments = mem.sem("x_moments")
        x_eps = mem.sem("x_eps")
        x_root = mem.sem("x_root")
        x_normed = mem.sem("x_normed")
        xt_ready = mem.sem("xt_ready")
        xt_hi = mem.sem("xt_hi")
        xt_lo = mem.sem("xt_lo")
        qkv_ready = mem.sem("qkv_ready")
        qkv_by_act = mem.sem("qkv_by_act")
        qkv_by_dve = mem.sem("qkv_by_dve")
        scores_ready = mem.sem("scores_ready")
        scores_by_act = mem.sem("scores_by_act")
        scores_by_dve = mem.sem("scores_by_dve")
        top_ready = mem.sem("top_ready")
        shift_ready = mem.sem("shift_ready")
        exp_ready = mem.sem("exp_ready")
        total_ready = mem.sem("total_ready")
        share_ready = mem.sem("share_ready")
        probs_ready = mem.sem("probs_ready")
        probs_turned = mem.sem("probs_turned")
        own_by_act = mem.sem("own_by_act")
        own_by_dve = mem.sem("own_by_dve")
        out_ready = mem.sem("out_ready")
        out_copied = mem.sem("out_copied")

        def started(i):
            return not isinstance(i, int) or i > 0

        def each_block(eng, block_of):
            block_of(0)
            with eng.Fori(1, BLOCKS) as i:
                block_of(i)

        def quadrant(b):
            return slice(b * Q, (b + 1) * Q)

        with nc.Block() as block:
            @block.sync
            def _(sp):
                for c in range(MC):
                    if c >= 2:
                        sp.wait_ge(w_lo, c - 1)
                    sp.dma_start(piece[c % 2][:, :], wqkv_t[c * P:(c + 1) * P, :]).then_inc(piece_in[c % 2], 16)

            @block.tensor
            def _(pe):
                def block_of(i):
                    for t in range(T):
                        pe.wait_ge(x_normed, T * i + t + 1)
                        for c in range(MC):
                            done = pe.transpose(ps_a[:, t, c * P:(c + 1) * P], x_norm[:, t, c * P:(c + 1) * P],
                                                ident[:, :])
                        done.then_inc(xt_ready, 1)
                    if not started(i):
                        pe.wait_ge(w_lo, MC)
                    pe.wait_ge(xt_lo, T * (i + 1))
                    if started(i):
                        pe.wait_ge(out_copied, T * i)
                    for u in range(UNITS):
                        if u >= 4:
                            pe.wait_ge(qkv_by_act if u % 2 == 0 else qkv_by_dve,
                                       UNITS // 2 * i + (u - 4) // 2 + 1)
                        for c in range(MC):
                            if u < 2 * HG:
                                left = [w[:, c, u * P:(u + 1) * P] for w in w_hl]
                                right = [w[:, c, :] for w in x_hl]
                            else:
                                t = u - 2 * HG
                                left = [w[:, c, t * P:(t + 1) * P] for w in x_hl]
                                right = [w[:, c, 2 * M:3 * M] for w in w_hl]
                            done = three_products(pe, ps_b[:, u % 4, :], left, right, c == 0, c == MC - 1)
                        done.then_inc(qkv_ready, 1)
                    pe.wait_ge(qkv_by_act, UNITS // 2 * (i + 1))
                    pe.wait_ge(qkv_by_dve, UNITS // 2 * (i + 1))

                    def score(t):
                        if t >= 1:
                            pe.wait_ge(scores_by_act, 2 * (T * i + t))
                            pe.wait_ge(scores_by_dve, 2 * (T * i + t))
                        for g in range(HG):
                            for h in range(4):
                                done = pe.matmul(ps_a[:, h, g * P:(g + 1) * P],
                                                 qk_t[quadrant(h), g, t * P:(t + 1) * P],
                                                 qk_t[quadrant(h), HG + g, t * P:(t + 1) * P],
                                                 start=True, stop=True)
                        done.then_inc(scores_ready, 1)

                    def weigh(t):
                        pe.wait_ge(own_by_act, 2 * (T * i + t) + 2)
                        pe.wait_ge(own_by_dve, 2 * (T * i + t) + 2)
                        for h in range(H):
                            done = pe.matmul(ps_b[quadrant(t), h // 4, h % 4 * P:(h % 4 + 1) * P],
                                             v_sb[:, t, h * D:(h + 1) * D], own[t % 2][:, h, :],
                                             start=True, stop=True)
                        done.then_inc(out_ready, 1)

                    for t in range(T):
                        score(t)
                        if t >= 1:
                            weigh(t - 1)
                    weigh(T - 1)
                each_block(pe, block_of)

            @block.scalar
            def _(act):
                for c in range(MC):
                    act.wait_ge(piece_in[c % 2], 16 * (c // 2 + 1))
                    act.activation(w_hl[0][:, c, :], piece[c % 2][:, :], ACT.Copy).then_inc(w_hi, 1)

                def block_of(i):
                    for t in range(T):
                        act.wait_ge(xt_ready, T * i + t + 1)
                        act.activation(x_hl[0][:, :, t * P:(t + 1) * P],
                                       ps_a[:, t, :].rearrange("p (c w) -> p c w", c=MC),
                                       ACT.Copy).then_inc(xt_hi, 1)
                    for u in range(0, UNITS, 2):
                        act.wait_ge(qkv_ready, UNITS * i + u + 1)
                        dst = qk_t[:, u, :] if u < 2 * HG else v_sb[:, u - 2 * HG, :]
                        act.activation(dst, ps_b[:, u % 4, :], ACT.Copy).then_inc(qkv_by_act, 1)

                    def collect(t):
                        act.wait_ge(scores_ready, T * i + t + 1)
                        if t >= 1 or started(i):
                            act.wait_ge(shift_ready, T * i + t)
                        for b in (0, 1):
                            act.activation(
                                scores[quadrant(b), :, :].rearrange("p (g h) k -> p h g k", h=4),
                                ps_a[quadrant(b), :, :].rearrange("p h (g w) -> p h g w", w=P)[:, :, :, quadrant(b)],
                                ACT.Copy).then_inc(scores_by_act, 1)

                    def exp(t):
                        act.wait_ge(shift_ready, T * i + t + 1)
                        act.activation(exps[:, :, :], shifted[:, :, :], ACT.Exp,
                                       scale=float(D) ** -0.5).then_inc(exp_ready, 1)

                    def place(t):
                        act.wait_ge(probs_turned, T * i + t + 1)
                        if t >= 2 or started(i):
                            act.wait_ge(out_ready, T * i + t - 1)
                        for b in (0, 1):
                            act.activation(own[t % 2][quadrant(b), :, quadrant(b)], probs_t[quadrant(b), :, :],
                                           ACT.Copy).then_inc(own_by_act, 1)

                    def regroup(t):
                        act.wait_ge(out_ready, T * i + t + 1)
                        act.activation(act_spare[:, t:t + 1], eps[:, :], ACT.Copy)
                        act.activation(
                            mixed[quadrant(t), bass.ds(i, 1), :, :].rearrange("p c (b n) q -> p (c n) b q", n=H),
                            ps_b[quadrant(t), :, :].rearrange("p a (n b q) -> p (a n) b q", b=BT, q=Q),
                            ACT.Copy).then_inc(out_copied, 1)

                    for t in range(T):
                        collect(t)
                        exp(t)
                        place(t)
                        if t >= 1:
                            regroup(t - 1)
                    regroup(T - 1)
                act.wait_ge(own_zeroed, 2)
                each_block(act, block_of)

            @block.vector
            def _(dve):
                for o in own:
                    dve.memset(o[:, :, :], 0.0).then_inc(own_zeroed, 1)
                for c in range(MC):
                    dve.wait_ge(w_hi, c + 1)
                    dve.tensor_tensor(w_hl[1][:, c, :], piece[c % 2][:, :], w_hl[0][:, c, :].bitcast(F32),
                                      ALU.subtract).then_inc(w_lo, 1)
                dve.wait_ge(own_zeroed, 2)

                def block_of(i):
                    for t in range(T):
                        dve.bn_stats(stats[:, t, :], x_res[:, bass.ds(T * i + t, 1), :]).then_inc(x_stats, 1)
                    dve.wait_ge(x_stats, T * (i + 1))
                    dve.memset(spare[:, :], 0.0)
                    for t in range(T):
                        dve.bn_aggr(moments[:, t, :], stats[:, t, :]).then_inc(x_moments, 1)
                    for t in range(T):
                        dve.wait_ge(x_root, i + 1)
                        dve.tensor_scalar(x_norm[:, t:t + 1, :], x_res[:, bass.ds(T * i + t, 1), :],
                                          moments[:, t, 0:1], x_var[:, t, 1:2],
                                          ALU.subtract, ALU.mult).then_inc(x_normed, 1)
                    for t in range(T):
                        dve.wait_ge(xt_hi, T * i + t + 1)
                        dve.tensor_tensor(x_hl[1][:, :, t * P:(t + 1) * P],
                                          ps_a[:, t, :].rearrange("p (c w) -> p c w", c=MC),
                                          x_hl[0][:, :, t * P:(t + 1) * P].bitcast(F32),
                                          ALU.subtract).then_inc(xt_lo, 1)
                    for u in range(1, UNITS, 2):
                        dve.wait_ge(qkv_ready, UNITS * i + u + 1)
                        dst = qk_t[:, u, :] if u < 2 * HG else v_sb[:, u - 2 * HG, :]
                        dve.tensor_copy(dst, ps_b[:, u % 4, :]).then_inc(qkv_by_dve, 1)

                    for t in range(T):
                        at = T * i + t + 1
                        dve.wait_ge(scores_ready, at)
                        for b in (2, 3):
                            dve.tensor_copy(
                                scores[quadrant(b), :, :].rearrange("p (g h) k -> p h g k", h=4),
                                ps_a[quadrant(b), :, :].rearrange("p h (g w) -> p h g w", w=P)[:, :, :, quadrant(b)],
                            ).then_inc(scores_by_dve, 1)
                        dve.wait_ge(scores_by_act, 2 * at)
                        dve.wait_ge(scores_by_dve, 2 * at)
                        dve.tensor_reduce(top[:, :], scores[:, :, :], AX_X, ALU.max).then_inc(top_ready, 1)
                        dve.wait_ge(top_ready, at)
                        dve.tensor_tensor(shifted[:, :, :], scores[:, :, :],
                                          top[:, :].unsqueeze(2).to_broadcast([P, H, Q]),
                                          ALU.subtract).then_inc(shift_ready, 1)
                        dve.wait_ge(exp_ready, at)
                        dve.tensor_reduce(total[:, :], exps[:, :, :], AX_X, ALU.add).then_inc(total_ready, 1)
                        dve.wait_ge(total_ready, at)
                        dve.reciprocal(share[:, :], total[:, :]).then_inc(share_ready, 1)
                        dve.wait_ge(share_ready, at)
                        dve.tensor_tensor(probs[:, :, :], exps[:, :, :],
                                          share[:, :].unsqueeze(2).to_broadcast([P, H, Q]),
                                          ALU.mult).then_inc(probs_ready, 1)
                        if t >= 1 or started(i):
                            dve.wait_ge(own_by_act, 2 * at - 2)
                        dve.wait_ge(probs_ready, at)
                        dve.transpose(probs_t[:, :, :].rearrange("p h q -> p (h q)"),
                                      probs[:, :, :].rearrange("p h q -> p (h q)")).then_inc(probs_turned, 1)
                        if t >= 2 or started(i):
                            dve.wait_ge(out_ready, at - 2)
                        dve.wait_ge(probs_turned, at)
                        for b in (2, 3):
                            dve.tensor_copy(own[t % 2][quadrant(b), :, quadrant(b)],
                                            probs_t[quadrant(b), :, :]).then_inc(own_by_dve, 1)
                each_block(dve, block_of)

            @block.gpsimd
            def _(pool):
                def block_of(i):
                    pool.wait_ge(x_moments, T * (i + 1))
                    pool.tensor_tensor(x_var[:, :, 0], moments[:, :, 1], eps[:, 0:1].to_broadcast([P, T]),
                                       ALU.add).then_inc(x_eps, 1)
                    pool.wait_ge(x_eps, i + 1)
                    pool.tensor_tensor(x_var[:, :, 1], x_var[:, :, 0], minus_half[:, 0:T],
                                       ALU.pow).then_inc(x_root, 1)
                each_block(pool, block_of)


def project_and_route(nc, wproj_t, bproj, gate_t, gate_b, bias, x_res, mixed, x_hl, logits, ident, minus_half, eps):
    M = wproj_t.shape[0]
    MC = M // P
    E = gate_t.shape[1]
    TILES = x_res.shape[1]
    J = P // mixed.shape[3]

    with ExitStack() as stack:
        mem = Memory(nc, stack, "p")
        piece = mem.sbuf("piece", [P, MC, M])
        w_hl = mem.pair("w", [P, MC, M])
        b_in = mem.sbuf("b_in", [P, M])
        gate_sb = mem.sbuf("gate_sb", [P, MC, E])
        gate_bias = mem.sbuf("gate_bias", [P, 2, E])
        c_hl = [mem.pair(f"c{i}", [P, MC, P]) for i in range(2)]
        stats = mem.sbuf("stats", [P, 2, 6])
        moments = mem.sbuf("moments", [P, 2, 2])
        x_var = mem.sbuf("x_var", [P, 2, 2])
        x_norm = [mem.sbuf(f"x_norm{i}", [P, M]) for i in range(2)]
        xt_sb = [mem.sbuf(f"xt_sb{i}", [P, MC, P]) for i in range(2)]
        spare = mem.sbuf("spare", [P, 4])
        ps_y = mem.banks("ps_y", 2)
        ps_xt = mem.banks("ps_xt", 2)
        ps_r = mem.banks("ps_r", 2)

        w_in = [mem.sem(f"w_in{c}") for c in range(MC)]
        rows_in = mem.sem("rows_in")
        w_hi = mem.sem("w_hi")
        w_lo = mem.sem("w_lo")
        c_hi = mem.sem("c_hi")
        c_lo = mem.sem("c_lo")
        y_ready = mem.sem("y_ready")
        y_added = mem.sem("y_added")
        b_added = mem.sem("b_added")
        x_stats = mem.sem("x_stats")
        x_moments = mem.sem("x_moments")
        x_eps = mem.sem("x_eps")
        x_root = mem.sem("x_root")
        x_normed = mem.sem("x_normed")
        xt_ready = mem.sem("xt_ready")
        xt_copied = mem.sem("xt_copied")
        xt_hi = mem.sem("xt_hi")
        xt_lo = mem.sem("xt_lo")
        r_ready = mem.sem("r_ready")
        r_added = mem.sem("r_added")
        r_done = mem.sem("r_done")

        def since(i, k):
            return not isinstance(i, int) or 2 * i + k >= 0

        def ahead(i, k):
            return not isinstance(i, int) or 2 * i + k < TILES - 1

        def by_pairs(eng, one):
            for i in range(2):
                for k in range(2):
                    one(i, k)
            with eng.Fori(2, TILES // 2 - 1) as i:
                for k in range(2):
                    one(i, k)
            for k in range(2):
                one(TILES // 2 - 1, k)

        with nc.Block() as block:
            @block.sync
            def _(sp):
                for c in range(MC):
                    sp.dma_start(piece[:, c, :], wproj_t[c * P:(c + 1) * P, :]).then_inc(w_in[c], 16)
                sp.dma_start(b_in[:, :], bproj.rearrange("(a m) -> a m", a=1).to_broadcast([P, M])
                             ).then_inc(rows_in, 16)
                sp.dma_start(gate_sb[:, :, :], gate_t.rearrange("(c p) e -> p c e", p=P)).then_inc(rows_in, 16)
                for j, row in enumerate((gate_b, bias)):
                    sp.dma_start(gate_bias[:, j, :], row.rearrange("(a e) -> a e", a=1).to_broadcast([P, E])
                                 ).then_inc(rows_in, 16)

            @block.tensor
            def _(pe):
                def project(i, k):
                    n = 2 * i + k
                    pe.wait_ge(c_lo, n + 1)
                    if since(i, k - 2):
                        pe.wait_ge(y_added, n - 1)
                    for c in range(MC):
                        if isinstance(i, int) and n == 0:
                            pe.wait_ge(w_lo, c + 1)
                        done = three_products(pe, ps_y[k][:, :], [w[:, c, :] for w in c_hl[k]],
                                              [w[:, c, :] for w in w_hl], c == 0, c == MC - 1)
                    done.then_inc(y_ready, 1)

                def turn(i, k):
                    n = 2 * i + k
                    pe.wait_ge(x_normed, n + 1)
                    if since(i, k - 2):
                        pe.wait_ge(xt_hi, n - 1)
                    for c in range(MC):
                        done = pe.transpose(ps_xt[k % 2][:, c * P:(c + 1) * P], x_norm[k % 2][:, c * P:(c + 1) * P],
                                            ident[:, :])
                    done.then_inc(xt_ready, 1)

                def route(i, k):
                    n = 2 * i + k
                    pe.wait_ge(xt_copied, n + 1)
                    if since(i, k - 2):
                        pe.wait_ge(r_added, n - 1)
                    for c in range(MC):
                        done = pe.matmul(ps_r[k % 2][:, 0:E], xt_sb[k % 2][:, c, :], gate_sb[:, c, :],
                                         start=c == 0, stop=c == MC - 1)
                    done.then_inc(r_ready, 1)

                pe.wait_ge(rows_in, 64)

                def one(i, k):
                    project(i, k)
                    if since(i, k - 2):
                        turn(i, k - 2)
                    if since(i, k - 3):
                        route(i, k - 3)
                by_pairs(pe, one)
                turn(TILES // 2, -2)
                route(TILES // 2, -3)
                turn(TILES // 2, -1)
                route(TILES // 2, -2)
                route(TILES // 2, -1)

            @block.scalar
            def _(act):
                def c_high(i, k):
                    if since(i, k - 2):
                        act.wait_ge(y_ready, 2 * i + k - 1)
                        act.activation(spare[:, 2 + k % 2:3 + k % 2], eps[:, :], ACT.Copy)
                    act.activation(c_hl[k % 2][0][:, :, :].rearrange("p c (j q) -> p c j q", j=J),
                                   mixed[:, :, bass.ds(J * (2 * i + k), J), :], ACT.Copy).then_inc(c_hi, 1)

                def x_copy(i, k):
                    n = 2 * i + k
                    act.wait_ge(xt_ready, n + 1)
                    if since(i, k - 2):
                        act.wait_ge(xt_lo, n - 1)
                        act.wait_ge(r_ready, n - 1)
                    act.activation(xt_sb[k % 2][:, :, :], ps_xt[k % 2][:, :].rearrange("p (c w) -> p c w", c=MC),
                                   ACT.Copy).then_inc(xt_copied, 1)
                    act.activation(x_hl[0][:, :, bass.ds(P * n, P)],
                                   ps_xt[k % 2][:, :].rearrange("p (c w) -> p c w", c=MC),
                                   ACT.Copy).then_inc(xt_hi, 1)

                c_high(0, 0)
                for c in range(MC):
                    act.wait_ge(w_in[c], 16)
                    act.activation(w_hl[0][:, c, :], piece[:, c, :], ACT.Copy).then_inc(w_hi, 1)

                def one(i, k):
                    if ahead(i, k):
                        c_high(i, k + 1)
                    if since(i, k - 2):
                        x_copy(i, k - 2)
                by_pairs(act, one)
                x_copy(TILES // 2, -2)
                x_copy(TILES // 2, -1)

            @block.vector
            def _(dve):
                def c_low(i, k):
                    dve.wait_ge(c_hi, 2 * i + k + 1)
                    dve.tensor_tensor(c_hl[k % 2][1][:, :, :].rearrange("p c (j q) -> p c j q", j=J),
                                      mixed[:, :, bass.ds(J * (2 * i + k), J), :],
                                      c_hl[k % 2][0][:, :, :].bitcast(F32).rearrange("p c (j q) -> p c j q", j=J),
                                      ALU.subtract).then_inc(c_lo, 1)

                def add(i, k):
                    n = 2 * i + k
                    tile = x_res[:, bass.ds(n, 1), :]
                    dve.wait_ge(y_ready, n + 1)
                    dve.tensor_tensor(tile, ps_y[k % 2][:, :].unsqueeze(1), tile, ALU.add).then_inc(y_added, 1)
                    dve.wait_ge(y_added, n + 1)
                    dve.tensor_tensor(tile, tile, b_in[:, :].unsqueeze(1), ALU.add).then_inc(b_added, 1)
                    dve.wait_ge(b_added, n + 1)
                    dve.memset(spare[:, 0:1], 0.0)
                    dve.bn_stats(stats[:, k % 2, :], tile).then_inc(x_stats, 1)
                    dve.wait_ge(x_stats, n + 1)
                    dve.memset(spare[:, 1:2], 0.0)
                    dve.bn_aggr(moments[:, k % 2, :], stats[:, k % 2, :]).then_inc(x_moments, 1)

                def norm(i, k):
                    n = 2 * i + k
                    dve.wait_ge(x_root, n + 1)
                    if since(i, k - 2):
                        dve.wait_ge(xt_ready, n - 1)
                    dve.tensor_scalar(x_norm[k % 2][:, :].unsqueeze(1), x_res[:, bass.ds(n, 1), :],
                                      moments[:, k % 2, 0:1], x_var[:, k % 2, 1:2],
                                      ALU.subtract, ALU.mult).then_inc(x_normed, 1)

                def x_low(i, k):
                    n = 2 * i + k
                    dve.wait_ge(xt_hi, n + 1)
                    dve.tensor_tensor(x_hl[1][:, :, bass.ds(P * n, P)], xt_sb[k % 2][:, :, :],
                                      x_hl[0][:, :, bass.ds(P * n, P)].bitcast(F32), ALU.subtract).then_inc(xt_lo, 1)

                def score(i, k):
                    n = 2 * i + k
                    dve.wait_ge(r_ready, n + 1)
                    dve.tensor_tensor(logits[:, bass.ds(n, 1), :], ps_r[k % 2][:, 0:E].unsqueeze(1),
                                      gate_bias[:, 0:1, :], ALU.add).then_inc(r_added, 1)
                    dve.wait_ge(r_added, n + 1)
                    dve.tensor_tensor(logits[:, bass.ds(n, 1), :], logits[:, bass.ds(n, 1), :],
                                      gate_bias[:, 1:2, :], ALU.add).then_inc(r_done, 1)

                c_low(0, 0)
                for c in range(MC):
                    dve.wait_ge(w_hi, c + 1)
                    dve.tensor_tensor(w_hl[1][:, c, :], piece[:, c, :], w_hl[0][:, c, :].bitcast(F32),
                                      ALU.subtract).then_inc(w_lo, 1)
                dve.wait_ge(rows_in, 64)

                def one(i, k):
                    if since(i, k - 2):
                        norm(i, k - 2)
                    if ahead(i, k):
                        c_low(i, k + 1)
                    if since(i, k - 1):
                        add(i, k - 1)
                    if since(i, k - 3):
                        x_low(i, k - 3)
                        score(i, k - 3)
                by_pairs(dve, one)
                norm(TILES // 2, -2)
                add(TILES // 2, -1)
                x_low(TILES // 2, -3)
                score(TILES // 2, -3)
                norm(TILES // 2, -1)
                x_low(TILES // 2, -2)
                score(TILES // 2, -2)
                x_low(TILES // 2, -1)
                score(TILES // 2, -1)

            @block.gpsimd
            def _(pool):
                def one(i, k):
                    n = 2 * i + k
                    pool.wait_ge(x_moments, n + 1)
                    pool.tensor_tensor(x_var[:, k, 0:1], moments[:, k, 1:2], eps[:, 0:1],
                                       ALU.add).then_inc(x_eps, 1)
                    pool.wait_ge(x_eps, n + 1)
                    pool.tensor_tensor(x_var[:, k, 1:2], x_var[:, k, 0:1], minus_half[:, 0:1],
                                       ALU.pow).then_inc(x_root, 1)
                by_pairs(pool, one)


def gate(nc, logits, gates):
    _, T, E = logits.shape

    with ExitStack() as stack:
        mem = Memory(nc, stack, "g")
        rank = mem.sbuf("rank", [P, T, E])
        top = [mem.sbuf(f"top{i}", [P, T]) for i in range(2)]
        best = [mem.sbuf(f"best{i}", [P, T]) for i in range(2)]
        at_top = [mem.sbuf(f"at_top{i}", [P, T, E]) for i in range(2)]
        pick = [mem.sbuf(f"pick{i}", [P, T, E]) for i in range(2)]
        rest = mem.sbuf("rest", [P, T, E])
        gap = mem.sbuf("gap", [P, T])
        second = mem.sbuf("second", [P, T])
        total = mem.sbuf("total", [P, T])
        weight = [mem.sbuf(f"weight{i}", [P, T]) for i in range(2)]
        share = [mem.sbuf(f"share{i}", [P, T, E]) for i in range(2)]
        ranked = mem.sem("ranked")
        step = mem.sem("step")
        gap_ready = mem.sem("gap_ready")
        second_ready = mem.sem("second_ready")

        def over_experts(a):
            return a[:, :].unsqueeze(2).to_broadcast([P, T, E])

        with nc.Block() as block:
            @block.gpsimd
            def _(pool):
                for e in range(E):
                    pool.memset(rank[:, :, e:e + 1], float(E - e)).then_inc(ranked, 1)

            @block.scalar
            def _(act):
                act.wait_ge(gap_ready, 1)
                act.activation(second[:, :], gap[:, :], ACT.Exp).then_inc(second_ready, 1)

            @block.vector
            def _(dve):
                dve.wait_ge(ranked, E)
                scores = logits
                for i in range(2):
                    at = 6 * i
                    dve.tensor_reduce(top[i][:, :], scores[:, :, :], AX_X, ALU.max).then_inc(step, 1)
                    dve.wait_ge(step, at + 1)
                    dve.tensor_tensor(at_top[i][:, :, :], scores[:, :, :], over_experts(top[i]),
                                      ALU.is_equal).then_inc(step, 1)
                    dve.wait_ge(step, at + 2)
                    dve.tensor_tensor(at_top[i][:, :, :], at_top[i][:, :, :], rank[:, :, :],
                                      ALU.mult).then_inc(step, 1)
                    dve.wait_ge(step, at + 3)
                    dve.tensor_reduce(best[i][:, :], at_top[i][:, :, :], AX_X, ALU.max).then_inc(step, 1)
                    dve.wait_ge(step, at + 4)
                    dve.tensor_tensor(pick[i][:, :, :], rank[:, :, :], over_experts(best[i]),
                                      ALU.is_equal).then_inc(step, 1)
                    dve.wait_ge(step, at + 5)
                    if i == 0:
                        dve.scalar_tensor_tensor(rest[:, :, :], pick[0][:, :, :], LOWEST, logits[:, :, :],
                                                 ALU.mult, ALU.add).then_inc(step, 1)
                        dve.wait_ge(step, at + 6)
                        scores = rest
                dve.tensor_tensor(gap[:, :], top[1][:, :], top[0][:, :], ALU.subtract).then_inc(gap_ready, 1)
                dve.wait_ge(second_ready, 1)
                dve.tensor_scalar(total[:, :], second[:, :], 1.0, None, ALU.add).then_inc(step, 1)
                dve.wait_ge(step, 12)
                dve.reciprocal(weight[0][:, :], total[:, :]).then_inc(step, 1)
                dve.wait_ge(step, 13)
                dve.tensor_tensor(weight[1][:, :], second[:, :], weight[0][:, :], ALU.mult).then_inc(step, 1)
                dve.wait_ge(step, 14)
                for i in range(2):
                    dve.tensor_tensor(share[i][:, :, :], pick[i][:, :, :], over_experts(weight[i]),
                                      ALU.mult).then_inc(step, 1)
                dve.wait_ge(step, 16)
                dve.tensor_tensor(gates[:, :, :].rearrange("p e t -> p t e"), share[0][:, :, :], share[1][:, :, :],
                                  ALU.add)


def places_in(room):
    used = [0]

    def place(columns):
        used[0] += columns
        return room[:, used[0] - columns:used[0]]
    return place


def experts(nc, w1_t, b1_t, w2_t, b2, x_res, x_hl, gates, room, out):
    E, M, F = w1_t.shape
    MC = M // P
    FC = -(-F // P)
    REST = F - (FC - 1) * P
    TILES = x_res.shape[1]
    T = 4
    W = T * P
    BLOCKS = TILES // T

    def width(m):
        return P if m < FC - 1 else REST

    def depth(m):
        return P if m < FC - 1 else REST + 1

    with ExitStack() as stack:
        mem = Memory(nc, stack, "e")
        places = places_in(room)
        w1_in = places(MC * F).rearrange("p (c f) -> p c f", c=MC)
        w2_in = places(FC * M).rearrange("p (c m) -> p c m", c=FC)
        w1_hl = [mem.pair(f"w1_{i}", [P, MC, F]) for i in range(2)]
        w2_hl = [mem.pair(f"w2_{i}", [P, FC, M]) for i in range(2)]
        b1_sb = mem.sbuf("b1_sb", [P, FC, E])
        b1_now = [mem.sbuf(f"b1_now{i}", [P, FC]) for i in range(2)]
        hidden = [places(W) for i in range(2)]
        h_hl = [mem.pair(f"h{i}", [P, FC, W]) for i in range(2)]
        bias_row = places(W)
        ps_h = mem.banks("ps_h", 2)
        ps_y = mem.banks("ps_y", 4)
        loaded = mem.sem("loaded")
        b1_loaded = mem.sem("b1_loaded")
        b1_padded = mem.sem("b1_padded")
        b1_picked = mem.sem("b1_picked")
        w_hi = mem.sem("w_hi")
        w_lo = mem.sem("w_lo")
        row_filled = mem.sem("row_filled")
        row_ready = mem.sem("row_ready")
        h_ready = mem.sem("h_ready")
        h_act = mem.sem("h_act")
        h_hi = mem.sem("h_hi")
        h_lo = mem.sem("h_lo")
        y_ready = mem.sem("y_ready")
        y_added = mem.sem("y_added")
        stored = mem.sem("stored")

        def within(i, k):
            return not isinstance(i, int) or 0 <= 2 * i + k < E

        def by_pairs(eng, one):
            for k in range(2):
                one(0, k)
            with eng.Fori(1, E // 2 - 1) as i:
                for k in range(2):
                    one(i, k)
            for k in range(2):
                one(E // 2 - 1, k)

        def steps(i, k, tb):
            return 2 * BLOCKS * i + BLOCKS * k + tb

        with nc.Block() as block:
            @block.sync
            def _(sp):
                def load(i, k):
                    if within(i, k - 1):
                        sp.wait_ge(w_lo, 2 * (2 * i + k))
                    e = 2 * i + k
                    sp.dma_start(w1_in[:, :, :], w1_t[e].rearrange("(c p) f -> p c f", p=P)).then_inc(loaded, 16)
                    sp.dma_start(w2_in[:, 0:FC - 1, :],
                                 w2_t[e, 0:(FC - 1) * P].rearrange("(c p) m -> p c m", p=P)).then_inc(loaded, 16)
                    sp.dma_start(w2_in[0:REST, FC - 1, :], w2_t[e, (FC - 1) * P:F]).then_inc(loaded, 16)
                    sp.dma_start(w2_in[REST:REST + 1, FC - 1, :], b2[e]).then_inc(loaded, 16)

                load(0, 0)
                sp.wait_ge(b1_padded, 1)
                sp.dma_start(b1_sb[:, 0:FC - 1, :],
                             b1_t[0:(FC - 1) * P, :].rearrange("(c p) e -> p c e", p=P)).then_inc(b1_loaded, 16)
                sp.dma_start(b1_sb[0:REST, FC - 1, :], b1_t[(FC - 1) * P:F, :]).then_inc(b1_loaded, 16)

                def one(i, k):
                    if within(i, k + 1):
                        load(i, k + 1)
                by_pairs(sp, one)
                for tb in range(BLOCKS):
                    sp.wait_ge(y_added, T * steps(0, E - 1, tb) + T)
                    sp.dma_start(out[tb * W:(tb + 1) * W, :].rearrange("(t p) m -> p t m", p=P),
                                 x_res[:, tb * T:(tb + 1) * T, :]).then_inc(stored, 16)
                sp.wait_ge(stored, 16 * BLOCKS)

            @block.tensor
            def _(pe):
                def hidden_layer(i, k, tb):
                    s = steps(i, k, tb)
                    if tb == 0:
                        pe.wait_ge(w_lo, 2 * (2 * i + k) + 2)
                    for m in range(FC):
                        if not (isinstance(i, int) and FC * s + m < 2):
                            pe.wait_ge(h_act, FC * s + m - 1)
                        bank = ps_h[(FC * (BLOCKS * k + tb) + m) % 2]
                        for c in range(MC):
                            done = three_products(
                                pe, bank[0:width(m), :],
                                [w[:, c, m * P:m * P + width(m)] for w in w1_hl[k % 2]],
                                [w[:, c, tb * W:(tb + 1) * W] for w in x_hl], c == 0, c == MC - 1)
                        done.then_inc(h_ready, 1)

                def output_layer(i, k, tb):
                    s = steps(i, k, tb)
                    pe.wait_ge(h_lo, FC * s + FC)
                    for t in range(T):
                        if within(i, k - 1) or tb > 0:
                            pe.wait_ge(y_added, T * (s - 1) + t + 1)
                        for m in range(FC):
                            done = three_products(
                                pe, ps_y[t][:, :],
                                [w[0:depth(m), m, t * P:(t + 1) * P] for w in h_hl[tb % 2]],
                                [w[0:depth(m), m, :] for w in w2_hl[k % 2]], m == 0, m == FC - 1)
                        done.then_inc(y_ready, 1)

                pe.wait_ge(row_ready, 4)

                def one(i, k):
                    for tb in range(BLOCKS):
                        hidden_layer(i, k, tb)
                        if tb > 0:
                            output_layer(i, k, tb - 1)
                        elif within(i, k - 1):
                            output_layer(i, k - 1, BLOCKS - 1)
                by_pairs(pe, one)
                output_layer(0, E - 1, BLOCKS - 1)

            @block.scalar
            def _(act):
                def weights_high(i, k):
                    act.wait_ge(loaded, 64 * (2 * i + k + 1))
                    if within(i, k - 2):
                        act.wait_ge(y_ready, T * steps(i, k - 1, 0))
                    act.activation(w1_hl[k % 2][0][:, :, :], w1_in[:, :, :], ACT.Copy).then_inc(w_hi, 1)
                    act.activation(w2_hl[k % 2][0][:, 0:FC - 1, :], w2_in[:, 0:FC - 1, :], ACT.Copy).then_inc(w_hi, 1)
                    act.activation(w2_hl[k % 2][0][0:REST + 1, FC - 1, :], w2_in[0:REST + 1, FC - 1, :],
                                   ACT.Copy).then_inc(w_hi, 1)

                def one(i, k):
                    act.wait_ge(b1_picked, 2 * i + k + 1)
                    for tb in range(BLOCKS):
                        s = steps(i, k, tb)
                        for m in range(FC):
                            act.wait_ge(h_ready, FC * s + m + 1)
                            bank = (FC * (BLOCKS * k + tb) + m) % 2
                            if not (isinstance(i, int) and FC * s + m < 2):
                                act.wait_ge(h_lo, FC * s + m - 1)
                            act.activation(hidden[bank][0:width(m), :], ps_h[bank][0:width(m), :], ACT.Silu,
                                           bias=b1_now[k % 2][0:width(m), m:m + 1]).then_inc(h_act, 1)
                        if tb == 1 and within(i, k + 1):
                            weights_high(i, k + 1)
                weights_high(0, 0)
                by_pairs(act, one)

            @block.gpsimd
            def _(pool):
                pool.memset(b1_sb[:, :, :], 0.0).then_inc(b1_padded, 1)
                pool.memset(bias_row[:, :], 1.0).then_inc(row_filled, 1)

            @block.vector
            def _(dve):
                def weights_low(i, k):
                    dve.wait_ge(w_hi, 3 * (2 * i + k) + 3)
                    dve.tensor_tensor(w1_hl[k % 2][1][:, :, :], w1_in[:, :, :], w1_hl[k % 2][0][:, :, :].bitcast(F32),
                                      ALU.subtract).then_inc(w_lo, 1)
                    dve.tensor_copy(b1_now[k % 2][:, :].unsqueeze(2), b1_sb[:, :, bass.ds(2 * i + k, 1)]).then_inc(b1_picked, 1)
                    dve.tensor_tensor(w2_hl[k % 2][1][:, 0:FC - 1, :], w2_in[:, 0:FC - 1, :],
                                      w2_hl[k % 2][0][:, 0:FC - 1, :].bitcast(F32), ALU.subtract)
                    dve.tensor_tensor(w2_hl[k % 2][1][0:REST + 1, FC - 1, :], w2_in[0:REST + 1, FC - 1, :],
                                      w2_hl[k % 2][0][0:REST + 1, FC - 1, :].bitcast(F32),
                                      ALU.subtract).then_inc(w_lo, 1)

                def split(i, k, tb):
                    s = steps(i, k, tb)
                    for m in range(FC):
                        bank = (FC * (BLOCKS * k + tb) + m) % 2
                        hi, lo = [w[0:width(m), m, :] for w in h_hl[tb % 2]]
                        dve.wait_ge(h_act, FC * s + m + 1)
                        if m == 0 and (within(i, k - 1) or tb >= 2):
                            dve.wait_ge(y_ready, T * (s - 1))
                        dve.tensor_copy(hi, hidden[bank][0:width(m), :]).then_inc(h_hi, 1)
                        dve.wait_ge(h_hi, FC * s + m + 1)
                        dve.tensor_tensor(lo, hidden[bank][0:width(m), :], hi.bitcast(F32),
                                          ALU.subtract).then_inc(h_lo, 1)

                def add(i, k, tb):
                    s = steps(i, k, tb)
                    for t in range(T):
                        tile = tb * T + t
                        dve.wait_ge(y_ready, T * s + t + 1)
                        dve.scalar_tensor_tensor(x_res[:, tile, :], ps_y[t][:, :],
                                                 gates[:, bass.ds(2 * i + k, 1), tile], x_res[:, tile, :],
                                                 ALU.mult, ALU.add).then_inc(y_added, 1)

                dve.wait_ge(row_filled, 1)
                for hi, lo in h_hl:
                    dve.tensor_copy(hi[REST:REST + 1, FC - 1, :], bias_row[REST:REST + 1, :]).then_inc(row_ready, 1)
                    dve.tensor_scalar(lo[REST:REST + 1, FC - 1, :], bias_row[REST:REST + 1, :], 0.0, None,
                                      ALU.mult).then_inc(row_ready, 1)
                dve.wait_ge(b1_loaded, 32)
                weights_low(0, 0)

                def one(i, k):
                    for tb in range(BLOCKS):
                        split(i, k, tb)
                        if tb > 0:
                            add(i, k, tb - 1)
                        elif within(i, k - 1):
                            add(i, k - 1, BLOCKS - 1)
                        if tb == 1 and within(i, k + 1):
                            weights_low(i, k + 1)
                by_pairs(dve, one)
                add(0, E - 1, BLOCKS - 1)


def perceiver_layer(nc, a, out):
    B, Q, M = a["x"].shape
    C = a["wk"].shape[0]
    H = a["wk_t"].shape[1]
    E = a["w1_t"].shape[0]
    TILES = B * Q // P
    scores_scratch = nc.dram_tensor("scores_scratch", (B, P, C // P, H, Q), F32).ap()
    values_scratch = nc.dram_tensor("values_scratch", (B, P, C // P, H, Q), F32).ap()
    with ExitStack() as stack:
        mem = Memory(nc, stack, "all")
        ident = mem.sbuf("ident", [P, P])
        minus_half = mem.sbuf("minus_half", [P, 16])
        eps = mem.sbuf("eps", [P, 1])
        shared_constants(nc, ident, minus_half, eps)
        queries(nc, a["x"], a["wq"], a["wk_t"], a["gq"], a["gk"], scores_scratch, ident, minus_half, eps)
        attend(nc, a["ctx_t"], a["ctx_rows"], a["ctx_last"], a["last_t"], a["wk"], scores_scratch, values_scratch,
               ident, minus_half, eps)
        x_res = mem.sbuf("x_res", [P, TILES, M])
        project_values(nc, a["x"], a["wv"], a["wo"], values_scratch, x_res)
        logits = mem.sbuf("logits", [P, TILES, E])
        gates = mem.sbuf("gates", [P, E, TILES])
        mixed = mem.sbuf("mixed", [P, M // P, B, Q])
        self_attend(nc, a["wqkv_t"], x_res, mixed, ident, minus_half, eps)
        x_hl = mem.pair("x", [P, M // P, B * Q])
        project_and_route(nc, a["wproj_t"], a["bproj"], a["gate_t"], a["gate_b"], a["bias"], x_res, mixed, x_hl,
                          logits, ident, minus_half, eps)
        gate(nc, logits, gates)
        experts(nc, a["w1_t"], a["b1_t"], a["w2_t"], a["b2"], x_res, x_hl, gates,
                mixed[:, :, :, :].rearrange("p c b q -> p (c b q)"), out)


def kernel(**inputs):
    import numpy as _np
    import concourse.bacc as _bacc
    from concourse.bass_utils import run_bass_kernel_spmd as _run

    g = {k.replace("L0_", ""): _np.asarray(v) for k, v in inputs.items()}
    B, Q, M = g["x"].shape
    _, S, C = g["ctx_1024"].shape
    D = g["xattn_gq"].shape[0]
    H = g["xattn_Wk"].shape[1] // D
    E, F, _ = g["ffn_w1"].shape
    n, d = 16, M // 16
    ctx = g["ctx_1024"]
    ctx_t = ctx.transpose(0, 2, 1).reshape(B, C // P, P, S).transpose(0, 2, 1, 3)
    laid = {
        "x": g["x"],
        "wq": g["xattn_Wq"], "wk": g["xattn_Wk"], "wv": g["xattn_Wv"], "wo": g["xattn_Wo"],
        "gq": g["xattn_gq"], "gk": g["xattn_gk"],
        "wk_t": g["xattn_Wk"].reshape(C, H, D).transpose(2, 1, 0),
        "ctx_t": _np.pad(ctx_t, ((0, 0), (0, 0), (0, 0), (0, S % 2))),
        "ctx_rows": ctx[:, :S - 1], "ctx_last": ctx[:, S - 1:], "last_t": ctx[:, S - 1].T,
        "wqkv_t": g["attn_Wqkv"].reshape(n, 3, d, M).transpose(3, 1, 0, 2).reshape(M, 3 * M),
        "wproj_t": g["attn_Wproj"].T, "bproj": g["attn_bproj"],
        "gate_t": g["ffn_gate_w"].T, "gate_b": g["ffn_gate_b"], "bias": g["ffn_bias"],
        "w1_t": g["ffn_w1"].transpose(0, 2, 1), "b1_t": g["ffn_b1"].T,
        "w2_t": g["ffn_w2"].transpose(0, 2, 1), "b2": g["ffn_b2"].reshape(E, 1, M),
    }
    nc = _bacc.Bacc("TRN2", target_bir_lowering=False, num_devices=1)
    arrays, args = {}, {}
    for name, value in laid.items():
        arrays[f"in_{name}"] = _np.ascontiguousarray(value)
        args[name] = nc.dram_tensor(f"in_{name}", value.shape, F32, kind="ExternalInput").ap()
    out = nc.dram_tensor("out_x", (B * Q, M), F32, kind="ExternalOutput").ap()
    perceiver_layer(nc, args, out)
    r = _run(nc, [arrays], core_ids=[0])
    return r.results[0]["out_x"].reshape(B, Q, M)
```

```python
from contextlib import ExitStack

import concourse.bass as bass
from concourse import mybir

F32 = mybir.dt.float32
F32R = mybir.dt.float32r
ALU = mybir.AluOpType
ACT = mybir.ActivationFunctionType
AX_X = mybir.AxisListType.X

P = 128
BANK = 512
EPS = 1e-5
LOWEST = -3.0e38


def three_products(pe, out, left, right, first, last):
    (left_hi, left_lo), (right_hi, right_lo) = left, right
    pe.matmul(out, left_hi, right_hi, start=first, stop=False)
    pe.matmul(out, left_hi, right_lo, start=False, stop=False)
    return pe.matmul(out, left_lo, right_hi, start=False, stop=last)


class Memory:

    def __init__(self, nc, stack, phase):
        self.nc, self.stack, self.phase = nc, stack, phase
        self.sems = []
        stack.callback(self.clear)

    def clear(self):
        if self.sems:
            self.nc.clear_and_free_semaphores(self.sems)
            self.nc.all_engine_barrier(sem_only=True)

    def sbuf(self, name, shape, dtype=F32):
        return self.stack.enter_context(self.nc.sbuf_tensor(f"{self.phase}_{name}", shape, dtype))

    def pair(self, name, shape):
        return self.sbuf(name + "_hi", shape, F32R), self.sbuf(name + "_lo", shape, F32R)

    def banks(self, name, count):
        return [self.stack.enter_context(self.nc.psum_tensor(f"{self.phase}_{name}{i}", [P, BANK], F32))
                for i in range(count)]

    def sem(self, name):
        self.sems.append(self.nc.alloc_semaphore(f"{self.phase}_{name}"))
        return self.sems[-1]


def places_in(room):
    used = [0]

    def place(columns):
        used[0] += columns
        return room[:, used[0] - columns:used[0]]
    return place


def shared_constants(nc, ident, minus_half, eps):
    with ExitStack() as stack:
        mem = Memory(nc, stack, "const")
        filled = mem.sem("filled")
        with nc.Block() as block:
            @block.gpsimd
            def _(pool):
                pool.memset(minus_half[:, :], -0.5)
                pool.memset(eps[:, :], EPS)
                pool.memset(ident[:, :], 0.0).then_inc(filled, 1)
                pool.wait_ge(filled, 1)
                pool.affine_select(out=ident[:, :], in_=ident[:, :], compare_op=ALU.not_equal, fill=1.0,
                                   base=0, pattern=[[-1, P]], channel_multiplier=1)


def queries(nc, x, wq, wk_t, gq, gk, scores_scratch, ident, minus_half, eps):
    B, Q, M = x.shape
    D, H, C = wk_t.shape
    MC, CC, HG = M // P, C // P, H // 4
    BT = P // Q
    T = 2
    W = T * P
    BLOCKS = B // (T * BT)
    x_blocks = x.rearrange("(i t b) q m -> i (b q) t m", t=T, b=BT)
    wq_rows = wq.rearrange("(c p) n -> p c n", p=P)
    out_blocks = scores_scratch.rearrange("(i b) p c h q -> i p b c (h q)", b=T * BT)

    with ExitStack() as stack:
        mem = Memory(nc, stack, "q")
        piece = [mem.sbuf(f"piece{i}", [P, H * D]) for i in range(2)]
        gain = mem.sbuf("gain", [P, 3])
        wq_hl = mem.pair("wq", [P, MC, H * D])
        wk_hl = mem.pair("wk", [P, H, C])
        x_in = mem.sbuf("x_in", [P, T, M])
        stats = mem.sbuf("stats", [P, T, 6])
        moments = mem.sbuf("moments", [P, T, 2])
        x_rstd = mem.sbuf("x_rstd", [P, T, 2])
        x_norm = mem.sbuf("x_norm", [P, T, M])
        x_hl = mem.pair("x", [P, MC, W])
        q_sb = mem.sbuf("q_sb", [P, 2, T, 4, D])
        q_sq = mem.sbuf("q_sq", [P, T, 4, D])
        spare = mem.sbuf("spare", [P, 1])
        q_var = mem.sbuf("q_var", [P, 2, T, 4])
        q_rstd = mem.sbuf("q_rstd", [P, 2, T, 4])
        q_hl = [mem.pair(f"q{i}", [P, 4, W]) for i in range(2)]
        staged = [mem.sbuf(f"staged{i}", [P, T * BT, CC, 4 * Q]) for i in range(2)]
        ps_q = mem.banks("ps_q", T)
        ps_xt = mem.banks("ps_xt", T)
        ps_qt = mem.banks("ps_qt", T)
        ps_out = mem.banks("ps_out", 2)

        piece_in = [mem.sem(f"piece_in{i}") for i in range(2)]
        gains_in = mem.sem("gains_in")
        gain_made = mem.sem("gain_made")
        wk_scaled = mem.sem("wk_scaled")
        w_hi = mem.sem("w_hi")
        w_lo = mem.sem("w_lo")
        x_loaded = mem.sem("x_loaded")
        x_stats = mem.sem("x_stats")
        x_moments = mem.sem("x_moments")
        x_var = mem.sem("x_var")
        x_root = mem.sem("x_root")
        x_normed = mem.sem("x_normed")
        xt_ready = mem.sem("xt_ready")
        xt_hi = mem.sem("xt_hi")
        xt_lo = mem.sem("xt_lo")
        q_ready = mem.sem("q_ready")
        q_copied = mem.sem("q_copied")
        q_summed = mem.sem("q_summed")
        q_root = mem.sem("q_root")
        q_scaled = mem.sem("q_scaled")
        qt_ready = mem.sem("qt_ready")
        qt_hi = mem.sem("qt_hi")
        qt_lo = mem.sem("qt_lo")
        out_ready = mem.sem("out_ready")
        out_by_act = mem.sem("out_by_act")
        out_by_dve = mem.sem("out_by_dve")
        stored = [mem.sem(f"stored{i}") for i in range(2)]

        wk_flat = wk_t.rearrange("d h c -> d (h c)")
        wk_hl_flat = [w[:, :, :].rearrange("p h c -> p (h c)") for w in wk_hl]
        PW = H * D
        WK_PIECES = H * C // PW
        pieces = [("wq", n) for n in range(HG - 1)] + [("wk", 0), ("wq", HG - 1)]
        pieces += [("wk", n) for n in range(1, WK_PIECES)]
        PIECES = len(pieces)
        SPLIT_BEFORE = {0: (0, 1), 1: (2,), 2: (3, 4), 3: (5,)}

        def scaled_before(k):
            return sum(kind == "wk" for kind, _ in pieces[:k + 1])

        def half_of_piece(k, which):
            kind, n = pieces[k]
            if kind == "wq":
                return wq_hl[which][:, :, n * BANK:(n + 1) * BANK]
            return wk_hl_flat[which][:, n * PW:(n + 1) * PW]

        def raw_piece(k):
            if pieces[k][0] == "wq":
                return piece[k % 2][:, :].rearrange("p (c n) -> p c n", c=MC)
            return piece[k % 2][:, :]

        def step_before(i, n, first):
            if n >= 1:
                return i, n - 1, first
            return None if first else (i - 1, HG - 1, False)

        def step_before_that(i, n, first):
            if n >= 2:
                return i, n - 2, first
            return None if first else (i - 1, n + HG - 2, False)

        def each_block(eng, block_of):
            block_of(0, True, False)
            with eng.Fori(1, BLOCKS - 1) as i:
                block_of(i, False, False)
            block_of(BLOCKS - 1, False, True)

        with nc.Block() as block:
            @block.sync
            def _(sp):
                def load_x(i):
                    sp.wait_ge(x_normed, T * i)
                    sp.dma_start(x_in[:, :, :], x_blocks[i]).then_inc(x_loaded, 16)

                sp.dma_start(x_in[:, :, :], x_blocks[0]).then_inc(x_loaded, 16)
                sp.dma_start(gain[:, 0:1], gq.rearrange("(d a) -> d a", a=1)).then_inc(gains_in, 16)
                sp.dma_start(gain[:, 1:2], gk.rearrange("(d a) -> d a", a=1)).then_inc(gains_in, 16)
                for k in range(PIECES):
                    if k >= 2:
                        sp.wait_ge(w_lo, k - 1)
                    kind, n = pieces[k]
                    src = wq_rows[:, :, n * BANK:(n + 1) * BANK] if kind == "wq" else wk_flat[:, n * PW:(n + 1) * PW]
                    sp.dma_start(raw_piece(k), src).then_inc(piece_in[k % 2], 16)
                    if k == 1:
                        load_x(1)

                def store(i, n):
                    sp.wait_ge(out_by_act, 2 * (HG * i + n) + 2)
                    sp.wait_ge(out_by_dve, 2 * (HG * i + n) + 2)
                    for c in range(CC):
                        sp.dma_start(out_blocks[i, :, :, c, 4 * Q * n:4 * Q * (n + 1)],
                                     staged[n % 2][:, :, c, :]).then_inc(stored[n % 2], 16)

                def block_of(i, first, last):
                    for n in range(HG):
                        if n == 0 and not first and not last:
                            load_x(i + 1)
                        if n >= 2:
                            store(i, n - 2)
                        elif not first:
                            store(i - 1, n + HG - 2)
                each_block(sp, block_of)
                store(BLOCKS - 1, HG - 2)
                store(BLOCKS - 1, HG - 1)
                for s in stored:
                    sp.wait_ge(s, 16 * CC * BLOCKS * HG // 2)

            def norm_stats(dve, i):
                for t in range(T):
                    if t == 0:
                        dve.wait_ge(x_loaded, 16 * (i + 1))
                    dve.bn_stats(stats[:, t, :], x_in[:, t, :]).then_inc(x_stats, 1)
                dve.wait_ge(x_stats, T * (i + 1))
                dve.memset(spare[:, :], 0.0)
                for t in range(T):
                    dve.bn_aggr(moments[:, t, :], stats[:, t, :]).then_inc(x_moments, 1)

            def norm_apply(dve, i):
                for t in range(T):
                    dve.wait_ge(x_root, T * i + t + 1)
                    dve.tensor_scalar(x_norm[:, t, :], x_in[:, t, :], moments[:, t, 0:1], x_rstd[:, t, 1:2],
                                      ALU.subtract, ALU.mult).then_inc(x_normed, 1)

            def norm_root(pool, i):
                for t in range(T):
                    pool.wait_ge(x_moments, T * i + t + 1)
                    pool.tensor_tensor(x_rstd[:, t, 0:1], moments[:, t, 1:2], eps[:, 0:1],
                                       ALU.add).then_inc(x_var, 1)
                    pool.wait_ge(x_var, T * i + t + 1)
                    pool.tensor_tensor(x_rstd[:, t, 1:2], x_rstd[:, t, 0:1], minus_half[:, 0:1],
                                       ALU.pow).then_inc(x_root, 1)

            @block.tensor
            def _(pe):
                def x_transposes(i):
                    for t in range(T):
                        pe.wait_ge(x_normed, T * i + t + 1)
                        for c in range(MC):
                            done = pe.transpose(ps_xt[t][:, c * P:(c + 1) * P], x_norm[:, t, c * P:(c + 1) * P],
                                                ident[:, :])
                        done.then_inc(xt_ready, 1)

                def project(i, n, first):
                    if first:
                        pe.wait_ge(w_lo, pieces.index(("wq", n)) + 1)
                    for t in range(T):
                        if n == 0:
                            pe.wait_ge(xt_lo, T * (i + 1))
                        if not (first and n == 0):
                            pe.wait_ge(q_copied, T * (HG * i + n) + t - 1)
                        for c in range(MC):
                            done = three_products(
                                pe, ps_q[t][:, :], [w[:, c, t * P:(t + 1) * P] for w in x_hl],
                                [w[:, c, n * BANK:(n + 1) * BANK] for w in wq_hl], c == 0, c == MC - 1)
                        done.then_inc(q_ready, 1)

                def q_transposes(i, n, first):
                    for t in range(T):
                        pe.wait_ge(q_scaled, T * (HG * i + n) + t + 1)
                        if not (first and n == 0):
                            pe.wait_ge(qt_lo, T * (HG * i + n) + t - 1)
                        for h in range(4):
                            done = pe.transpose(ps_qt[t][:, h * P:(h + 1) * P], q_sb[:, n % 2, t, h, :],
                                                ident[:, :])
                        done.then_inc(qt_ready, 1)

                def through_wk(i, n, first):
                    if first and n == 0:
                        pe.wait_ge(w_lo, pieces.index(("wk", 0)) + 1)
                    pe.wait_ge(qt_lo, T * (HG * i + n) + T)
                    for h in range(4):
                        if not (first and n == 0 and h < 2):
                            pe.wait_ge(out_by_act if h % 2 == 0 else out_by_dve, 2 * (HG * i + n) + h // 2)
                        for c in range(CC):
                            done = three_products(
                                pe, ps_out[h % 2][:, c * W:(c + 1) * W],
                                [w[:, 4 * n + h, c * P:(c + 1) * P] for w in wk_hl],
                                [w[:, h, :] for w in q_hl[n % 2]], True, True)
                        done.then_inc(out_ready, 1)

                x_transposes(0)

                def block_of(i, first, last):
                    for n in range(HG):
                        project(i, n, first)
                        if n == HG - 1 and not last:
                            x_transposes(i + 1)
                        if n >= 1:
                            q_transposes(i, n - 1, first)
                        elif not first:
                            q_transposes(i - 1, HG - 1, False)
                        if n >= 2:
                            through_wk(i, n - 2, first)
                        elif not first:
                            through_wk(i - 1, n + HG - 2, False)
                    if first:
                        pe.wait_ge(w_lo, PIECES)
                each_block(pe, block_of)
                q_transposes(BLOCKS - 1, HG - 1, False)
                through_wk(BLOCKS - 1, HG - 2, False)
                through_wk(BLOCKS - 1, HG - 1, False)

            @block.scalar
            def _(act):
                def split_high(k):
                    if pieces[k][0] == "wq":
                        act.wait_ge(piece_in[k % 2], 16 * (k // 2 + 1))
                    else:
                        act.wait_ge(wk_scaled, scaled_before(k))
                    act.activation(half_of_piece(k, 0), raw_piece(k), ACT.Copy).then_inc(w_hi, 1)

                def x_high(i, first):
                    for t in range(T):
                        act.wait_ge(xt_ready, T * i + t + 1)
                        if t == 0 and not first:
                            act.wait_ge(q_ready, T * HG * i)
                        act.activation(x_hl[0][:, :, t * P:(t + 1) * P],
                                       ps_xt[t][:, :].rearrange("p (c w) -> p c w", c=MC),
                                       ACT.Copy).then_inc(xt_hi, 1)

                def q_copy(i, n, first):
                    for t in range(T):
                        act.wait_ge(q_ready, T * (HG * i + n) + t + 1)
                        if not (first and n < 2):
                            act.wait_ge(qt_ready, T * (HG * i + n - 2) + t + 1)
                        act.activation(q_sb[:, n % 2, t, :, :],
                                       ps_q[t][:, :].rearrange("p (h d) -> p h d", h=4),
                                       ACT.Copy).then_inc(q_copied, 1)

                def q_high(i, n, first, t):
                    act.wait_ge(qt_ready, T * (HG * i + n) + t + 1)
                    if not (first and n < 2):
                        act.wait_ge(out_ready, 4 * (HG * i + n - 2) + 4)
                    act.activation(q_hl[n % 2][0][:, :, t * P:(t + 1) * P],
                                   ps_qt[t][:, :].rearrange("p (h w) -> p h w", h=4),
                                   ACT.Copy).then_inc(qt_hi, 1)

                def read_out(i, n, first, h):
                    if h == 0 and not (first and n < 2):
                        act.wait_ge(stored[n % 2], 16 * CC * (HG // 2 * i + n // 2))
                    act.wait_ge(out_ready, 4 * (HG * i + n) + h + 1)
                    act.activation(
                        staged[n % 2][:, :, :, h * Q:(h + 1) * Q].rearrange("p b c q -> p c b q"),
                        ps_out[h % 2][:, :].rearrange("p (c b q) -> p c b q", c=CC, q=Q),
                        ACT.Copy).then_inc(out_by_act, 1)

                def turn_and_read_out(turned, through):
                    for j in range(T):
                        if turned:
                            q_high(*turned, j)
                        if through:
                            read_out(*through, 2 * j)

                x_high(0, True)

                def block_of(i, first, last):
                    for n in range(HG):
                        if first:
                            for k in SPLIT_BEFORE[n]:
                                split_high(k)
                        q_copy(i, n, first)
                        if n == HG - 1 and not last:
                            x_high(i + 1, False)
                        turn_and_read_out(step_before(i, n, first), step_before_that(i, n, first))
                each_block(act, block_of)
                turn_and_read_out((BLOCKS - 1, HG - 1, False), (BLOCKS - 1, HG - 2, False))
                turn_and_read_out(None, (BLOCKS - 1, HG - 1, False))

            @block.vector
            def _(dve):
                norm_stats(dve, 0)
                norm_apply(dve, 0)
                dve.wait_ge(gains_in, 32)
                dve.tensor_tensor(gain[:, 2:3], gain[:, 0:1], gain[:, 1:2], ALU.mult).then_inc(gain_made, 1)
                def split_low(k):
                    if pieces[k][0] == "wk":
                        dve.wait_ge(gain_made, 1)
                        dve.wait_ge(piece_in[k % 2], 16 * (k // 2 + 1))
                        dve.tensor_scalar(raw_piece(k), raw_piece(k), gain[:, 2:3], float(D) ** -0.5,
                                          ALU.mult, ALU.mult).then_inc(wk_scaled, 1)
                    dve.wait_ge(w_hi, k + 1)
                    dve.tensor_tensor(half_of_piece(k, 1), raw_piece(k), half_of_piece(k, 0).bitcast(F32),
                                      ALU.subtract).then_inc(w_lo, 1)

                def x_low(i):
                    for t in range(T):
                        dve.wait_ge(xt_hi, T * i + t + 1)
                        dve.tensor_tensor(x_hl[1][:, :, t * P:(t + 1) * P],
                                          ps_xt[t][:, :].rearrange("p (c w) -> p c w", c=MC),
                                          x_hl[0][:, :, t * P:(t + 1) * P].bitcast(F32),
                                          ALU.subtract).then_inc(xt_lo, 1)

                def q_squares(i, n, first):
                    for t in range(T):
                        dve.wait_ge(q_copied, T * (HG * i + n) + t + 1)
                        if not (first and n < 2):
                            dve.wait_ge(q_root, T * (HG * i + n - 2) + t + 1)
                        if not (first and n == 0):
                            dve.wait_ge(q_summed, T * (HG * i + n - 1) + t + 1)
                        for h in range(4):
                            done = dve.tensor_tensor_reduce(
                                q_sq[:, t, h, :], q_sb[:, n % 2, t, h, :], q_sb[:, n % 2, t, h, :], 1.0 / D, EPS,
                                ALU.mult, ALU.add, q_var[:, n % 2, t, h:h + 1])
                        done.then_inc(q_summed, 1)

                def q_low(i, n, first, t):
                    dve.wait_ge(qt_hi, T * (HG * i + n) + t + 1)
                    dve.tensor_tensor(q_hl[n % 2][1][:, :, t * P:(t + 1) * P],
                                      ps_qt[t][:, :].rearrange("p (h w) -> p h w", h=4),
                                      q_hl[n % 2][0][:, :, t * P:(t + 1) * P].bitcast(F32),
                                      ALU.subtract).then_inc(qt_lo, 1)

                def read_out(i, n, first, h):
                    if h == 1 and not (first and n < 2):
                        dve.wait_ge(stored[n % 2], 16 * CC * (HG // 2 * i + n // 2))
                    dve.wait_ge(out_ready, 4 * (HG * i + n) + h + 1)
                    dve.tensor_copy(
                        staged[n % 2][:, :, :, h * Q:(h + 1) * Q].rearrange("p b c q -> p c b q"),
                        ps_out[h % 2][:, :].rearrange("p (c b q) -> p c b q", c=CC, q=Q),
                    ).then_inc(out_by_dve, 1)

                def turn_and_read_out(turned, through):
                    for j in range(T):
                        if through:
                            read_out(*through, 2 * j + 1)
                        if turned:
                            q_low(*turned, j)

                x_low(0)

                def block_of(i, first, last):
                    for n in range(HG):
                        if first:
                            for k in SPLIT_BEFORE[n]:
                                split_low(k)
                        q_squares(i, n, first)
                        if n == HG - 1 and not last:
                            x_low(i + 1)
                        turn_and_read_out(step_before(i, n, first), step_before_that(i, n, first))
                        if n == 0 and not last:
                            norm_stats(dve, i + 1)
                        if n == 1 and not last:
                            dve.wait_ge(xt_ready, T * (i + 1))
                            norm_apply(dve, i + 1)
                each_block(dve, block_of)
                turn_and_read_out((BLOCKS - 1, HG - 1, False), (BLOCKS - 1, HG - 2, False))
                turn_and_read_out(None, (BLOCKS - 1, HG - 1, False))

            @block.gpsimd
            def _(pool):
                norm_root(pool, 0)

                def q_norm(i, n):
                    for t in range(T):
                        at = T * (HG * i + n) + t + 1
                        pool.wait_ge(q_summed, at)
                        pool.tensor_tensor(q_rstd[:, n % 2, t, :], q_var[:, n % 2, t, :], minus_half[:, 0:4],
                                           ALU.pow).then_inc(q_root, 1)
                        pool.wait_ge(q_root, at)
                        pool.tensor_tensor(q_sb[:, n % 2, t, :, :], q_sb[:, n % 2, t, :, :],
                                           q_rstd[:, n % 2, t, :].unsqueeze(2).to_broadcast([P, 4, D]),
                                           ALU.mult).then_inc(q_scaled, 1)

                def block_of(i, first, last):
                    for n in range(HG):
                        q_norm(i, n)
                        if n == 0 and not last:
                            norm_root(pool, i + 1)
                each_block(pool, block_of)


def attend(nc, ctx_t, ctx_rows, ctx_last, last_t, wk, scores_scratch, values_scratch, wv, wv_hl, u_in, room,
           ident, minus_half, eps):
    B, _, CC, SP2 = ctx_t.shape
    ST = 2
    L = ST * P
    S = L + 1
    HD = wk.shape[1]
    C = CC * P
    H = HD // P
    HG = H // 4
    Q = P // 4
    KN = HD // BANK
    UNITS = ST * KN
    LAST = 2 * Q + 1
    wk_rows, wv_rows = [w.rearrange("(c p) (j n) -> j p c n", p=P, n=BANK) for w in (wk, wv)]
    UB = u_in[0].shape[1]
    first_values = values_scratch[0:UB].rearrange("b p c h q -> p b c (h q)")

    def within(i, k):
        return not isinstance(i, int) or 0 <= 2 * i + k < B

    with ExitStack() as stack:
        mem = Memory(nc, stack, "a")
        piece = [mem.sbuf(f"piece{i}", [P, CC, BANK]) for i in range(KN)]
        wk_hl = mem.pair("wk", [P, CC, HD])
        last_in = mem.sbuf("last_in", [P, CC, P])
        last_hl = mem.pair("last", [P, CC, P])
        ctx_t_in = [mem.sbuf(f"ctx_t_in{i}", [P, CC, SP2]) for i in range(2)]
        ctx_t_hl = [mem.pair(f"ctx_t{i}", [P, CC, SP2]) for i in range(2)]
        rows_in = [mem.sbuf(f"rows_in{i}", [P, ST, C]) for i in range(2)]
        row_in = [mem.sbuf(f"row_in{i}", [LAST, C]) for i in range(2)]
        rows_hl = mem.pair("rows", [P, ST, C])
        row_parts = mem.sbuf("row_parts", [LAST, C], F32R)
        q_in = [mem.sbuf(f"q_in{i}", [P, CC, H * Q]) for i in range(2)]
        q_hl = mem.pair("q", [P, CC, H * Q])
        k_sq = [mem.sbuf(f"k_sq{i}", [P, BANK]) for i in range(2)]
        k_ms = mem.sbuf("k_ms", [P, ST, H])
        k_var = mem.sbuf("k_var", [P, ST, H])
        k_rstd = mem.sbuf("k_rstd", [P, ST, H])
        last_ms = mem.sbuf("last_ms", [P, H])
        last_var = mem.sbuf("last_var", [P, H])
        last_rstd = mem.sbuf("last_rstd", [P, H])
        last_factor = mem.sbuf("last_factor", [P, HG, P])
        factor = mem.sbuf("factor", [P, HG, S])
        scaled = mem.sbuf("scaled", [P, HG, S])
        top = mem.sbuf("top", [P, HG])
        minus_top = mem.sbuf("minus_top", [P, HG])
        probs = mem.sbuf("probs", [P, HG, S])
        total = mem.sbuf("total", [P, HG])
        share = mem.sbuf("share", [P, HG])
        probs_hl = mem.pair("probs", [P, ST, H * Q])
        prob_parts = mem.sbuf("prob_parts", [LAST, H * Q], F32R)
        places = places_in(room)
        out_sb = [places(CC * H * Q).rearrange("p (c n) -> p c n", c=CC) for i in range(2)]
        spare = mem.sbuf("spare", [P, 1])
        zeros = mem.sbuf("zeros", [Q + H, L])
        spread_f32 = mem.sbuf("spread_f32", [Q + H, HG, P])
        spread = mem.sbuf("spread", [Q + H, HG, P], F32R)
        turned_parts = mem.sbuf("turned_parts", [Q + H, L], F32R)
        spare2 = mem.sbuf("spare2", [P, 1])
        ps_scores = mem.banks("ps_scores", HG)
        ps_keys = mem.banks("ps_keys", 2)
        ps_turn = mem.banks("ps_turn", 2)

        piece_in = [mem.sem(f"piece_in{i}") for i in range(KN)]
        wk_hi = mem.sem("wk_hi")
        wk_lo = mem.sem("wk_lo")
        padded = mem.sem("padded")
        last_loaded = mem.sem("last_loaded")
        last_hi = mem.sem("last_hi")
        last_lo = mem.sem("last_lo")
        ctx_t_loaded = [mem.sem(f"ctx_t_loaded{i}") for i in range(2)]
        rows_loaded = [mem.sem(f"rows_loaded{i}") for i in range(2)]
        q_loaded = [mem.sem(f"q_loaded{i}") for i in range(2)]
        ctx_t_hi = mem.sem("ctx_t_hi")
        ctx_t_lo = mem.sem("ctx_t_lo")
        rows_hi = mem.sem("rows_hi")
        rows_lo = mem.sem("rows_lo")
        row_lo = mem.sem("row_lo")
        q_hi = mem.sem("q_hi")
        q_lo = mem.sem("q_lo")
        keys_ready = mem.sem("keys_ready")
        keys_squared = mem.sem("keys_squared")
        keys_summed = mem.sem("keys_summed")
        keys_var = mem.sem("keys_var")
        keys_root = mem.sem("keys_root")
        spread_filled = mem.sem("spread_filled")
        spread_made = mem.sem("spread_made")
        turned = mem.sem("turned")
        turned_hi = mem.sem("turned_hi")
        turned_lo = mem.sem("turned_lo")
        last_turned = mem.sem("last_turned")
        last_kept = mem.sem("last_kept")
        factor_turned = mem.sem("factor_turned")
        factor_out = mem.sem("factor_out")
        factor_last = mem.sem("factor_last")
        scores_ready = mem.sem("scores_ready")
        scores_scaled = mem.sem("scores_scaled")
        top_ready = mem.sem("top_ready")
        exp_ready = mem.sem("exp_ready")
        share_ready = mem.sem("share_ready")
        probs_ready = mem.sem("probs_ready")
        probs_turned = mem.sem("probs_turned")
        probs_hi = mem.sem("probs_hi")
        probs_lo = mem.sem("probs_lo")
        wv_in = mem.sem("wv_in")
        wv_hi = mem.sem("wv_hi")
        wv_lo = mem.sem("wv_lo")
        u_loaded = mem.sem("u_loaded")
        out_ready = mem.sem("out_ready")
        out_copied = mem.sem("out_copied")
        stored = [mem.sem(f"stored{i}") for i in range(2)]

        def unit(i, k, u):
            return 2 * UNITS * i + UNITS * k + KN + u

        def wv_pieces(i, k):
            return range(KN // 2 * k, KN // 2 * (k + 1)) if isinstance(i, int) and i == B // 2 - 1 else ()

        def columns(w, n):
            return w[:, :, n * BANK:(n + 1) * BANK]

        def by_pairs(eng, one, tail):
            for k in range(2):
                one(0, k)
            with eng.Fori(1, B // 2 - tail) as i:
                for k in range(2):
                    one(i, k)
            for i in range(B // 2 - tail, B // 2):
                for k in range(2):
                    one(i, k)

        with nc.Block() as block:
            @block.sync
            def _(sp):
                def load_ctx_t(i, k):
                    if within(i, k - 2):
                        sp.wait_ge(ctx_t_lo, 2 * i + k - 1)
                    sp.dma_start(ctx_t_in[k % 2][:, :, :], ctx_t[2 * i + k]).then_inc(ctx_t_loaded[k % 2], 16)

                def load_rows(i, k):
                    if within(i, k - 2):
                        sp.wait_ge(rows_lo, 2 * i + k - 1)
                        sp.wait_ge(row_lo, 2 * i + k - 1)
                    b = 2 * i + k
                    sp.dma_start(rows_in[k % 2][:, :, :],
                                 ctx_rows[b].rearrange("(t p) c -> p t c", p=P)).then_inc(rows_loaded[k % 2], 16)
                    sp.dma_start(row_in[k % 2][0:LAST:Q, :],
                                 ctx_last[b].to_broadcast([3, C])).then_inc(rows_loaded[k % 2], 16)

                def load_q(i, k):
                    if within(i, k - 2):
                        sp.wait_ge(q_lo, 2 * i + k - 1)
                    sp.dma_start(q_in[k % 2][:, :, :],
                                 scores_scratch[2 * i + k].rearrange("p c h q -> p c (h q)")
                                 ).then_inc(q_loaded[k % 2], 16)

                def store(i, k):
                    sp.wait_ge(out_copied, CC * (2 * i + k + 1))
                    sp.dma_start(values_scratch[2 * i + k].rearrange("p c h q -> p c (h q)"),
                                 out_sb[k % 2][:, :, :]).then_inc(stored[k % 2], 16)

                sp.dma_start(piece[0][:, :, :], wk_rows[0]).then_inc(piece_in[0], 16)
                sp.wait_ge(padded, 1)
                sp.dma_start(last_in[:, :, 0:B], last_t.rearrange("(c p) b -> p c b", p=P)).then_inc(last_loaded, 16)
                for n in range(1, KN):
                    sp.dma_start(piece[n][:, :, :], wk_rows[n]).then_inc(piece_in[n], 16)
                load_ctx_t(0, 0)
                load_ctx_t(0, 1)
                load_q(0, 0)
                sp.wait_ge(padded, 3)
                load_rows(0, 0)
                load_q(0, 1)
                load_ctx_t(0, 2)

                def one(i, k):
                    if within(i, k - 1):
                        store(i, k - 1)
                    if within(i, k + 1):
                        load_rows(i, k + 1)
                    if within(i, k + 2):
                        load_q(i, k + 2)
                    if within(i, k + 3):
                        load_ctx_t(i, k + 3)
                    if isinstance(i, int) and i == B // 2 - 1 and k == 0:
                        sp.wait_ge(wk_lo, KN)
                        for n in range(KN):
                            sp.dma_start(piece[n][:, :, :], wv_rows[n]).then_inc(wv_in, 16)
                        for s in stored:
                            sp.wait_ge(s, 16 * UB // 2)
                        for n in range(2):
                            for c in range(CC):
                                sp.dma_start(u_in[n][:, :, c, :], first_values[:, :, c, n * P:(n + 1) * P]
                                             ).then_inc(u_loaded, 16)
                by_pairs(sp, one, 2)
                store(B // 2 - 1, 1)
                for s in stored:
                    sp.wait_ge(s, 16 * B // 2)
                sp.wait_ge(u_loaded, 16 * 2 * CC)

            @block.tensor
            def _(pe):
                def last_keys(n):
                    if n >= 2:
                        pe.wait_ge(keys_squared, n - 1)
                    for c in range(CC):
                        done = three_products(pe, ps_keys[n % 2][:, :], [w[:, c, :] for w in last_hl],
                                              [w[:, c, n * BANK:(n + 1) * BANK] for w in wk_hl],
                                              c == 0, c == CC - 1)
                    done.then_inc(keys_ready, 1)

                def turn_factors(count, tiles):
                    pe.wait_ge(keys_root, ST * count + 1)
                    for t, factors in enumerate(tiles):
                        done = pe.transpose(ps_turn[1][0:H, t * P:(t + 1) * P], factors, ident[:, :])
                    done.then_inc(turned, 1)

                def keys(i, k, units):
                    for u in units:
                        t, n = u // KN, u % KN
                        if u == 0:
                            pe.wait_ge(ctx_t_lo, 2 * i + k + 1)
                        pe.wait_ge(keys_squared, unit(i, k, u) - 1)
                        for c in range(CC):
                            done = three_products(
                                pe, ps_keys[u % 2][:, :], [w[:, c, t * P:(t + 1) * P] for w in ctx_t_hl[k % 2]],
                                [w[:, c, n * BANK:(n + 1) * BANK] for w in wk_hl], c == 0, c == CC - 1)
                        done.then_inc(keys_ready, 1)

                def one(i, k):
                    pe.wait_ge(q_lo, 2 * i + k + 1)
                    for g in range(HG):
                        for c in range(CC):
                            done = three_products(
                                pe, ps_scores[g][:, 0:SP2], [w[:, c, g * P:(g + 1) * P] for w in q_hl],
                                [w[:, c, :] for w in ctx_t_hl[k % 2]], c == 0, c == CC - 1)
                        done.then_inc(scores_ready, 1)
                    if within(i, k - 1):
                        pe.wait_ge(out_copied, CC * (2 * i + k))
                    turn_factors(2 * i + k + 1, [k_rstd[:, t, :] for t in range(ST)])
                    if within(i, k + 1):
                        keys(i, k + 1, range(0, 1))
                    pe.wait_ge(turned_lo, 2 * i + k + 2)
                    for g in range(HG):
                        done = pe.matmul(ps_turn[g // 2][:, g % 2 * L:(g % 2 + 1) * L], spread[:, g, :],
                                         turned_parts[:, :], start=True, stop=True)
                        if g % 2:
                            done.then_inc(factor_turned, 1)
                    if within(i, k + 1):
                        keys(i, k + 1, range(1, 5))
                    pe.wait_ge(factor_out, 2 * (2 * i + k) + 2)
                    for t in range(ST):
                        for g in range(HG):
                            if t == 0:
                                pe.wait_ge(probs_ready, HG * (2 * i + k) + g + 1)
                            done = pe.transpose(ps_turn[t][:, g * P:(g + 1) * P], probs[:, g, t * P:(t + 1) * P],
                                                ident[:, :])
                        done.then_inc(probs_turned, 1)
                    for g in range(HG):
                        done = pe.transpose(ps_scores[0][0:LAST, g * P:(g + 1) * P],
                                            probs[:, g, L:S].to_broadcast([P, LAST]), ident[:, :])
                    done.then_inc(probs_turned, 1)
                    if within(i, k + 1):
                        keys(i, k + 1, range(5, UNITS))
                    pe.wait_ge(probs_lo, 3 * (2 * i + k) + 3)
                    pe.wait_ge(rows_lo, 2 * i + k + 1)
                    pe.wait_ge(row_lo, 2 * i + k + 1)
                    for c in range(CC):
                        for t in range(ST):
                            three_products(pe, ps_turn[c][:, :], [w[:, t, c * P:(c + 1) * P] for w in rows_hl],
                                           [w[:, t, :] for w in probs_hl], t == 0, False)
                        pe.matmul(ps_turn[c][:, :], row_parts[:, c * P:(c + 1) * P], prob_parts[:, :],
                                  start=False, stop=True).then_inc(out_ready, 1)

                pe.wait_ge(last_lo, 1)
                for n in range(KN):
                    pe.wait_ge(wk_lo, n + 1)
                    last_keys(n)
                keys(0, 0, range(UNITS))
                turn_factors(0, [last_rstd[:, :]])
                pe.wait_ge(spread_made, 1)
                pe.wait_ge(turned_lo, 1)
                for g in range(HG):
                    done = pe.matmul(ps_turn[0][:, g * P:(g + 1) * P], spread[:, g, :], turned_parts[:, 0:P],
                                     start=True, stop=True)
                done.then_inc(last_turned, 1)
                pe.wait_ge(last_kept, 1)
                by_pairs(pe, one, 1)

            @block.scalar
            def _(act):
                def square(g, place, first):
                    act.wait_ge(keys_ready, g + 1)
                    if not first:
                        act.wait_ge(keys_summed, g - 1)
                    act.activation(k_sq[place][:, :], ps_keys[place][:, :], ACT.Square,
                                   scale=float(P) ** -0.5).then_inc(keys_squared, 1)

                def squares(i, k, units):
                    if within(i, k):
                        for u in units:
                            square(unit(i, k, u), u % 2, False)

                def turned_high(count, width):
                    act.wait_ge(turned, count + 1)
                    act.activation(turned_parts[0:H, 0:width], ps_turn[1][0:H, 0:width],
                                   ACT.Copy).then_inc(turned_hi, 1)

                def one(i, k):
                    turned_high(2 * i + k + 1, L)
                    squares(i, k + 1, range(0, 1))
                    if within(i, k - 1):
                        act.wait_ge(scores_scaled, HG * (2 * i + k))
                    for j in range(2):
                        act.wait_ge(factor_turned, 2 * (2 * i + k) + j + 1)
                        act.activation(factor[:, 2 * j:2 * j + 2, 0:L],
                                       ps_turn[j][:, :].rearrange("p (g s) -> p g s", g=2),
                                       ACT.Copy).then_inc(factor_out, 1)
                    squares(i, k + 1, range(1, 2))
                    if within(i, k - 1):
                        act.wait_ge(probs_turned, 3 * (2 * i + k))
                    for g in range(HG):
                        if g % 2 == 0:
                            act.wait_ge(top_ready, 2 * (2 * i + k) + g // 2 + 1)
                        act.activation(probs[:, g, :], scaled[:, g, :], ACT.Exp, bias=minus_top[:, g:g + 1],
                                       accum_out=total[:, g:g + 1]).then_inc(exp_ready, 1)
                        if g == 1:
                            squares(i, k + 1, range(2, 3))
                    squares(i, k + 1, range(3, 5))
                    if within(i, k - 1):
                        act.wait_ge(out_ready, CC * (2 * i + k))
                    for t in range(ST):
                        act.wait_ge(probs_turned, 3 * (2 * i + k) + t + 1)
                        act.activation(probs_hl[0][:, t, :], ps_turn[t][:, :], ACT.Copy).then_inc(probs_hi, 1)
                    act.wait_ge(probs_turned, 3 * (2 * i + k) + 3)
                    act.activation(prob_parts[:, :], ps_scores[0][0:LAST, :], ACT.Copy).then_inc(probs_hi, 1)
                    squares(i, k + 1, range(5, UNITS))
                    for n in wv_pieces(i, k):
                        act.wait_ge(wv_in, 16 * KN)
                        act.activation(columns(wv_hl[0], n), piece[n][:, :, :], ACT.Copy).then_inc(wv_hi, 1)
                    if within(i, k - 2):
                        act.wait_ge(stored[k % 2], 16 * i)
                    for c in range(CC):
                        act.wait_ge(out_ready, CC * (2 * i + k) + c + 1)
                        act.activation(out_sb[k % 2][:, c, :], ps_turn[c][:, :], ACT.Copy).then_inc(out_copied, 1)

                for n in range(KN):
                    act.wait_ge(piece_in[n], 16)
                    act.activation(wk_hl[0][:, :, n * BANK:(n + 1) * BANK], piece[n][:, :, :],
                                   ACT.Copy).then_inc(wk_hi, 1)
                for n in range(KN):
                    square(n, n % 2, n < 2)
                squares(0, 0, range(UNITS))
                turned_high(0, P)
                act.wait_ge(last_turned, 1)
                act.activation(last_factor[:, :, :], ps_turn[0][:, :].rearrange("p (g b) -> p g b", g=HG),
                               ACT.Copy).then_inc(last_kept, 1)
                by_pairs(act, one, 1)

            @block.vector
            def _(dve):
                def sum_heads(out, place):
                    dve.tensor_reduce(out, k_sq[place][:, :].rearrange("p (h d) -> p h d", h=4), AX_X,
                                      ALU.add).then_inc(keys_summed, 1)

                def sums(i, k, units):
                    if within(i, k):
                        for u in units:
                            if u % KN == 0:
                                dve.wait_ge(keys_var, ST * (2 * i + k - 1) + u // KN + 2)
                            dve.wait_ge(keys_squared, unit(i, k, u) + 1)
                            at = u % KN * 4
                            sum_heads(k_ms[:, u // KN, at:at + 4], u % 2)

                def scale(i, k, j):
                    b = 2 * i + k
                    dve.wait_ge(scores_ready, HG * b + 2 * j + 2)
                    if j == 0:
                        dve.wait_ge(factor_last, b + 1)
                    if j == 0 and within(i, k - 1):
                        dve.wait_ge(exp_ready, HG * b)
                    dve.wait_ge(factor_out, 2 * b + j + 1)
                    dve.memset(spare[:, :], 0.0)
                    for g in (2 * j, 2 * j + 1):
                        dve.tensor_tensor_reduce(scaled[:, g, :], ps_scores[g][:, 0:S], factor[:, g, :], 1.0, LOWEST,
                                                 ALU.mult, ALU.max, top[:, g:g + 1]).then_inc(scores_scaled, 1)
                    dve.wait_ge(scores_scaled, HG * b + 2 * j + 2)
                    dve.tensor_scalar(minus_top[:, 2 * j:2 * j + 2], top[:, 2 * j:2 * j + 2], -1.0, None,
                                      ALU.mult).then_inc(top_ready, 1)

                def rows_high(i, k):
                    dve.wait_ge(rows_loaded[k % 2], 32 * (i + k // 2 + 1))
                    dve.tensor_copy(rows_hl[0][:, :, :], rows_in[k % 2][:, :, :]).then_inc(rows_hi, 1)
                    dve.tensor_copy(row_parts[:, :], row_in[k % 2][:, :]).then_inc(rows_hi, 1)
                    dve.wait_ge(rows_hi, 2 * (2 * i + k) + 2)
                    dve.tensor_tensor(row_parts[Q:Q + 1, :], row_in[k % 2][Q:Q + 1, :],
                                      row_parts[Q:Q + 1, :].bitcast(F32), ALU.subtract).then_inc(row_lo, 1)

                def q_high(i, k):
                    dve.wait_ge(q_loaded[k % 2], 16 * (i + k // 2 + 1))
                    dve.tensor_copy(q_hl[0][:, :, :], q_in[k % 2][:, :, :]).then_inc(q_hi, 1)

                def ctx_t_high(i, k):
                    dve.wait_ge(ctx_t_loaded[k % 2], 16 * (i + k // 2 + 1))
                    dve.tensor_copy(ctx_t_hl[k % 2][0][:, :, :], ctx_t_in[k % 2][:, :, :]).then_inc(ctx_t_hi, 1)

                def turned_low(count, width):
                    dve.wait_ge(turned_hi, count + 1)
                    dve.tensor_tensor(turned_parts[Q:Q + H, 0:width], ps_turn[1][0:H, 0:width],
                                      turned_parts[0:H, 0:width].bitcast(F32), ALU.subtract).then_inc(turned_lo, 1)

                def one(i, k):
                    b = 2 * i + k
                    if within(i, k - 1):
                        dve.wait_ge(out_ready, CC * b)
                    rows_high(i, k)
                    turned_low(b + 1, L)
                    dve.wait_ge(scores_ready, HG * b + HG)
                    if within(i, k + 1):
                        q_high(i, k + 1)
                    if within(i, k + 2):
                        ctx_t_high(i, k + 2)
                    sums(i, k + 1, range(0, 1))
                    scale(i, k, 0)
                    scale(i, k, 1)
                    sums(i, k + 1, range(1, 2))
                    dve.wait_ge(exp_ready, HG * b + HG)
                    dve.reciprocal(share[:, :], total[:, :]).then_inc(share_ready, 1)
                    dve.wait_ge(share_ready, b + 1)
                    for g in range(HG):
                        dve.tensor_scalar(probs[:, g, :], probs[:, g, :], share[:, g:g + 1], None,
                                          ALU.mult).then_inc(probs_ready, 1)
                    sums(i, k + 1, range(2, 5))
                    for t in range(ST):
                        dve.wait_ge(probs_hi, 3 * b + t + 1)
                        dve.tensor_tensor(probs_hl[1][:, t, :], ps_turn[t][:, :],
                                          probs_hl[0][:, t, :].bitcast(F32), ALU.subtract).then_inc(probs_lo, 1)
                    dve.wait_ge(probs_hi, 3 * b + 3)
                    dve.tensor_tensor(prob_parts[2 * Q:LAST, :], ps_scores[0][2 * Q:LAST, :],
                                      prob_parts[2 * Q:LAST, :].bitcast(F32), ALU.subtract).then_inc(probs_lo, 1)
                    sums(i, k + 1, range(5, UNITS))
                    for n in wv_pieces(i, k):
                        dve.wait_ge(wv_hi, n + 1)
                        dve.tensor_tensor(columns(wv_hl[1], n), piece[n][:, :, :], columns(wv_hl[0], n).bitcast(F32),
                                          ALU.subtract).then_inc(wv_lo, 1)

                dve.wait_ge(last_loaded, 16)
                dve.tensor_copy(last_hl[0][:, :, :], last_in[:, :, :]).then_inc(last_hi, 1)
                dve.wait_ge(last_hi, 1)
                dve.tensor_tensor(last_hl[1][:, :, :], last_in[:, :, :], last_hl[0][:, :, :].bitcast(F32),
                                  ALU.subtract).then_inc(last_lo, 1)
                for n in range(KN):
                    dve.wait_ge(wk_hi, n + 1)
                    dve.tensor_tensor(wk_hl[1][:, :, n * BANK:(n + 1) * BANK], piece[n][:, :, :],
                                      wk_hl[0][:, :, n * BANK:(n + 1) * BANK].bitcast(F32),
                                      ALU.subtract).then_inc(wk_lo, 1)
                ctx_t_high(0, 0)
                ctx_t_high(0, 1)
                q_high(0, 0)
                dve.wait_ge(padded, 4)
                dve.tensor_copy(turned_parts[:, :], zeros[:, :])
                dve.wait_ge(spread_filled, 3)
                dve.tensor_copy(spread[:, :, :], spread_f32[:, :, :]).then_inc(spread_made, 1)
                for n in range(KN):
                    dve.wait_ge(keys_squared, n + 1)
                    sum_heads(last_ms[:, 4 * n:4 * n + 4], n % 2)
                for u in range(UNITS):
                    dve.wait_ge(keys_squared, unit(0, 0, u) + 1)
                    sum_heads(k_ms[:, u // KN, u % KN * 4:u % KN * 4 + 4], u % 2)
                turned_low(0, P)
                by_pairs(dve, one, 1)

            @block.gpsimd
            def _(pool):
                def q_low(i, k):
                    pool.wait_ge(q_hi, 2 * i + k + 1)
                    pool.tensor_tensor(q_hl[1][:, :, :], q_in[k % 2][:, :, :], q_hl[0][:, :, :].bitcast(F32),
                                       ALU.subtract).then_inc(q_lo, 1)

                def ctx_t_low(i, k):
                    pool.wait_ge(ctx_t_hi, 2 * i + k + 1)
                    pool.tensor_tensor(ctx_t_hl[k % 2][1][:, :, :], ctx_t_in[k % 2][:, :, :],
                                       ctx_t_hl[k % 2][0][:, :, :].bitcast(F32), ALU.subtract).then_inc(ctx_t_lo, 1)

                def rows_low(i, k):
                    pool.wait_ge(rows_hi, 2 * (2 * i + k) + 2)
                    pool.tensor_tensor(rows_hl[1][:, :, :], rows_in[k % 2][:, :, :], rows_hl[0][:, :, :].bitcast(F32),
                                       ALU.subtract).then_inc(rows_lo, 1)

                def roots(i, k, t):
                    done = ST * (2 * i + k) + t + 1
                    pool.wait_ge(keys_summed, unit(i, k, (t + 1) * KN))
                    pool.tensor_tensor(k_var[:, t, :], k_ms[:, t, :], eps[:, 0:1].to_broadcast([P, H]),
                                       ALU.add).then_inc(keys_var, 1)
                    pool.wait_ge(turned, 2 * i + k + 1)
                    pool.wait_ge(keys_var, done + 1)
                    pool.tensor_tensor(k_rstd[:, t, :], k_var[:, t, :], minus_half[:, 0:1].to_broadcast([P, H]),
                                       ALU.pow).then_inc(keys_root, 1)

                def one(i, k):
                    if within(i, k - 1):
                        pool.wait_ge(scores_scaled, HG * (2 * i + k))
                        pool.tensor_tensor(spare2[:, :], eps[:, 0:1], eps[:, 0:1], ALU.add)
                    pool.tensor_copy(factor[:, :, L:S], last_factor[:, :, bass.ds(2 * i + k, 1)]).then_inc(factor_last, 1)
                    rows_low(i, k)
                    if within(i, k + 1):
                        q_low(i, k + 1)
                    if within(i, k + 2):
                        ctx_t_low(i, k + 2)
                    if within(i, k + 1):
                        for t in range(ST):
                            roots(i, k + 1, t)

                pool.memset(last_in[:, :, :], 0.0).then_inc(padded, 1)
                for r in row_in:
                    pool.memset(r[:, :], 0.0).then_inc(padded, 1)
                pool.memset(zeros[:, :], 0.0).then_inc(padded, 1)
                pool.memset(spread_f32[:, :, :], 0.0).then_inc(spread_filled, 1)
                for part in range(2):
                    pool.wait_ge(spread_filled, part + 1)
                    view = spread_f32[:, :, :].rearrange("p g (h q) -> p (g h) q", h=4)
                    pool.affine_select(out=view, in_=view, compare_op=ALU.not_equal, fill=1.0, base=part * Q,
                                       pattern=[[1, H], [0, Q]], channel_multiplier=-1).then_inc(spread_filled, 1)
                ctx_t_low(0, 0)
                ctx_t_low(0, 1)
                q_low(0, 0)
                pool.wait_ge(keys_summed, KN)
                pool.tensor_tensor(last_var[:, :], last_ms[:, :], eps[:, 0:1].to_broadcast([P, H]),
                                   ALU.add).then_inc(keys_var, 1)
                pool.wait_ge(keys_var, 1)
                pool.tensor_tensor(last_rstd[:, :], last_var[:, :], minus_half[:, 0:1].to_broadcast([P, H]),
                                   ALU.pow).then_inc(keys_root, 1)
                for t in range(ST):
                    roots(0, 0, t)
                pool.wait_ge(last_kept, 1)
                by_pairs(pool, one, 1)


def project_values(nc, x, wo, values_scratch, wv_hl, u_in, x_res):
    B, Q, M = x.shape
    _, _, CC, H, _ = values_scratch.shape
    D = wo.shape[0] // H
    HG = H // 4
    BT = P // Q
    T = 2
    W = T * P
    BLOCKS = B // (T * BT)
    LAST = BLOCKS - 1
    x_blocks = x.rearrange("(i t b) q m -> i (b q) t m", t=T, b=BT)
    in_blocks = values_scratch.rearrange("(i b) p c h q -> i p b c (h q)", b=T * BT)
    wo_groups = wo.rearrange("(g h d) m -> g d h m", h=4, d=D)

    with ExitStack() as stack:
        mem = Memory(nc, stack, "v")
        piece = [x_res[:, x_res.shape[1] - 4 * (i + 1):x_res.shape[1] - 4 * i, :] for i in range(2)]
        wo_hl = mem.pair("wo", [P, H, M])
        u_hl = [mem.pair(f"u{i}", [P, T * BT, CC, 4 * Q]) for i in range(2)]
        o_hl = [mem.pair(f"o{i}", [P, 4, W]) for i in range(2)]
        x_in = mem.sbuf("x_in", [P, T, M])
        ps_o = mem.banks("ps_o", 4)
        ps_y = mem.banks("ps_y", T)
        piece_in = [mem.sem(f"piece_in{i}") for i in range(2)]
        w_hi = mem.sem("w_hi")
        w_lo = mem.sem("w_lo")
        u_loaded = [mem.sem(f"u_loaded{i}") for i in range(2)]
        x_loaded = mem.sem("x_loaded")
        u_hi = mem.sem("u_hi")
        u_lo = mem.sem("u_lo")
        o_ready = mem.sem("o_ready")
        o_hi = mem.sem("o_hi")
        o_lo = mem.sem("o_lo")
        y_ready = mem.sem("y_ready")
        y_added = mem.sem("y_added")


        def raw_piece(g):
            return piece[g % 2]

        def half_of_piece(g, which):
            return wo_hl[which][:, 4 * g:4 * g + 4, :]

        def each_block(eng, block_of, peel_last=1):
            block_of(0)
            with eng.Fori(1, BLOCKS - peel_last) as i:
                block_of(i)
            for i in range(BLOCKS - peel_last, BLOCKS):
                block_of(i)

        def after(i, n, steps):
            return not isinstance(i, int) or HG * i + n >= steps

        with nc.Block() as block:
            @block.sync
            def _(sp):
                def load(i, n):
                    if after(i, n, 2):
                        sp.wait_ge(u_lo, HG * i + n - 1)
                    for c in range(CC):
                        sp.dma_start(u_in[n % 2][:, :, c, :],
                                     in_blocks[i + n // HG, :, :, c, 4 * Q * (n % HG):4 * Q * (n % HG + 1)]
                                     ).then_inc(u_loaded[n % 2], 16)

                def load_piece(k):
                    if k >= 2:
                        sp.wait_ge(w_lo, k - 1)
                    sp.dma_start(raw_piece(k), wo_groups[k]).then_inc(piece_in[k % 2], 16)

                for k in range(2):
                    load_piece(k)

                def block_of(i):
                    for n in range(HG):
                        if n == 2:
                            if after(i, 0, 1):
                                sp.wait_ge(y_added, T * i)
                            sp.dma_start(x_in[:, :, :], x_blocks[i]).then_inc(x_loaded, 16)
                        if not (isinstance(i, int) and i == LAST and n >= HG - 2):
                            load(i, n + 2)
                        if isinstance(i, int) and i == 0 and n + 2 < HG:
                            load_piece(n + 2)
                each_block(sp, block_of)

            @block.tensor
            def _(pe):
                def through_wv(i, n):
                    pe.wait_ge(u_lo, HG * i + n + 1)
                    for h in range(4):
                        bank = ps_o[n % 2 * 2 + h // 2]
                        if h % 2 == 0 and after(i, n, 2):
                            pe.wait_ge(o_lo, 2 * (HG * i + n - 2) + h // 2 + 1)
                        for c in range(CC):
                            done = three_products(
                                pe, bank[:, h % 2 * W:(h % 2 + 1) * W],
                                [w[:, c, (4 * n + h) * D:(4 * n + h + 1) * D] for w in wv_hl],
                                [w[:, :, c, h * Q:(h + 1) * Q] for w in u_hl[n % 2]], c == 0, c == CC - 1)
                        if h % 2:
                            done.then_inc(o_ready, 1)

                def through_wo(i, n):
                    pe.wait_ge(o_lo, 2 * (HG * i + n) + 2)
                    if isinstance(i, int) and i == 0:
                        pe.wait_ge(w_lo, n + 1)
                    for t in range(T):
                        if n == 0 and after(i, n, 1):
                            pe.wait_ge(y_added, T * (i - 1) + t + 1)
                        for h in range(4):
                            done = three_products(
                                pe, ps_y[t][:, :], [w[:, h, t * P:(t + 1) * P] for w in o_hl[n % 2]],
                                [w[:, 4 * n + h, :] for w in wo_hl], n == 0 and h == 0, n == HG - 1 and h == 3)
                        if n == HG - 1:
                            done.then_inc(y_ready, 1)

                def block_of(i):
                    for n in range(HG):
                        through_wv(i, n)
                        if n >= 1:
                            through_wo(i, n - 1)
                        elif after(i, n, 1):
                            through_wo(i - 1, HG - 1)
                    if isinstance(i, int) and i == 0:
                        pe.wait_ge(w_lo, HG)
                each_block(pe, block_of)
                through_wo(LAST, HG - 1)

            @block.scalar
            def _(act):
                def piece_high(k):
                    act.wait_ge(piece_in[k % 2], 16 * (k // 2 + 1))
                    act.activation(half_of_piece(k, 0), raw_piece(k), ACT.Copy).then_inc(w_hi, 1)

                def u_high(i, n):
                    if after(i, n, 2):
                        act.wait_ge(u_loaded[n % 2], 16 * CC * (HG // 2 * i + n // 2))
                    if after(i, n, 2):
                        act.wait_ge(o_ready, 2 * (HG * i + n - 1))
                    act.activation(u_hl[n % 2][0][:, :, :, :], u_in[n % 2][:, :, :, :], ACT.Copy).then_inc(u_hi, 1)

                def o_high(i, n):
                    for j in range(2):
                        act.wait_ge(o_ready, 2 * (HG * i + n) + j + 1)
                        act.activation(o_hl[n % 2][0][:, 2 * j:2 * j + 2, :],
                                       ps_o[n % 2 * 2 + j][:, :].rearrange("p (h w) -> p h w", h=2),
                                       ACT.Copy).then_inc(o_hi, 1)

                for n in range(2):
                    u_high(0, n)

                def block_of(i):
                    first = isinstance(i, int) and i == 0
                    for n in range(HG):
                        o_high(i, n)
                        if first:
                            piece_high(n)
                        if not (isinstance(i, int) and i == LAST and n >= HG - 2):
                            u_high(i, n + 2)
                each_block(act, block_of)

            @block.vector
            def _(dve):
                def piece_low(k):
                    dve.wait_ge(w_hi, k + 1)
                    dve.tensor_tensor(half_of_piece(k, 1), raw_piece(k), half_of_piece(k, 0).bitcast(F32),
                                      ALU.subtract).then_inc(w_lo, 1)

                def u_low(i, n):
                    dve.wait_ge(u_hi, HG * i + n + 1)
                    dve.tensor_tensor(u_hl[n % 2][1][:, :, :, :], u_in[n % 2][:, :, :, :],
                                      u_hl[n % 2][0][:, :, :, :].bitcast(F32), ALU.subtract).then_inc(u_lo, 1)

                def o_low(i, n):
                    for j in range(2):
                        dve.wait_ge(o_hi, 2 * (HG * i + n) + j + 1)
                        dve.tensor_tensor(o_hl[n % 2][1][:, 2 * j:2 * j + 2, :],
                                          ps_o[n % 2 * 2 + j][:, :].rearrange("p (h w) -> p h w", h=2),
                                          o_hl[n % 2][0][:, 2 * j:2 * j + 2, :].bitcast(F32),
                                          ALU.subtract).then_inc(o_lo, 1)

                def add(i):
                    dve.wait_ge(x_loaded, 16 * (i + 1))
                    for t in range(T):
                        dve.wait_ge(y_ready, T * i + t + 1)
                        dve.tensor_tensor(x_res[:, bass.ds(T * i + t, 1), :],
                                          ps_y[t][:, :].unsqueeze(1), x_in[:, t:t + 1, :],
                                          ALU.add).then_inc(y_added, 1)

                for n in range(2):
                    u_low(0, n)

                def block_of(i):
                    first = isinstance(i, int) and i == 0
                    for n in range(HG):
                        o_low(i, n)
                        if first:
                            piece_low(n)
                        if not (isinstance(i, int) and i == LAST and n >= HG - 2):
                            u_low(i, n + 2)
                        if n == 0 and after(i, n, 1):
                            add(i - 1)
                each_block(dve, block_of)
                add(LAST)


def self_attend(nc, wqkv_t, x_res, mixed, ident, minus_half, eps):
    M, _ = wqkv_t.shape
    MC = M // P
    D, BT = 32, 4
    Q = P // BT
    H = M // D
    HG = H // 4
    T = 2
    W = T * P
    BLOCKS = x_res.shape[1] // T
    UNITS = HG + T
    PW = 2 * P
    PIECES = 3 * M // PW
    PV = 2 * M // PW
    RING = 4

    with ExitStack() as stack:
        mem = Memory(nc, stack, "s")
        piece = [mem.sbuf(f"piece{i}", [P, MC, PW]) for i in range(RING)]
        w_hl = mem.pair("w", [P, MC, 3 * M])
        stats = mem.sbuf("stats", [P, T, 6])
        moments = mem.sbuf("moments", [P, T, 2])
        x_var = mem.sbuf("x_var", [P, T, 2])
        x_norm = mem.sbuf("x_norm", [P, T, M])
        x_hl = mem.pair("x", [P, MC, W])
        qk_t = [mem.sbuf(f"qk_t{i}", [P, 2 * HG, W]) for i in range(2)]
        v_sb = [mem.sbuf(f"v_sb{i}", [P, T, M]) for i in range(2)]
        scores = mem.sbuf("scores", [P, H, Q])
        top = mem.sbuf("top", [P, H])
        shifted = mem.sbuf("shifted", [P, H, Q])
        exps = mem.sbuf("exps", [P, H, Q])
        total = mem.sbuf("total", [P, H])
        share = mem.sbuf("share", [P, H])
        probs = mem.sbuf("probs", [P, H, Q])
        probs_t = mem.sbuf("probs_t", [P, H, Q])
        spare = mem.sbuf("spare", [P, 1])
        act_spare = mem.sbuf("act_spare", [P, 4 * T])
        own = [mem.sbuf(f"own{i}", [P, H, P]) for i in range(2)]
        ps_m = mem.banks("ps_m", 2)
        ps_s = stack.enter_context(nc.psum_tensor("s_ps_s", [P, 4, BANK], F32))
        ps_o = stack.enter_context(nc.psum_tensor("s_ps_o", [P, 2, BANK], F32))

        piece_in = [mem.sem(f"piece_in{i}") for i in range(RING)]
        w_hi = mem.sem("w_hi")
        w_lo = mem.sem("w_lo")
        own_zeroed = mem.sem("own_zeroed")
        x_stats = mem.sem("x_stats")
        x_moments = mem.sem("x_moments")
        x_eps = mem.sem("x_eps")
        x_root = mem.sem("x_root")
        x_normed = mem.sem("x_normed")
        xt_ready = mem.sem("xt_ready")
        xt_hi = mem.sem("xt_hi")
        xt_lo = mem.sem("xt_lo")
        qkv_ready = mem.sem("qkv_ready")
        qkv_by_act = mem.sem("qkv_by_act")
        qkv_by_dve = mem.sem("qkv_by_dve")
        scores_ready = mem.sem("scores_ready")
        scores_by_act = mem.sem("scores_by_act")
        scores_by_dve = mem.sem("scores_by_dve")
        top_ready = mem.sem("top_ready")
        shift_ready = mem.sem("shift_ready")
        exp_ready = mem.sem("exp_ready")
        total_ready = mem.sem("total_ready")
        share_ready = mem.sem("share_ready")
        probs_ready = mem.sem("probs_ready")
        probs_turned = mem.sem("probs_turned")
        own_by_act = mem.sem("own_by_act")
        own_by_dve = mem.sem("own_by_dve")
        out_ready = mem.sem("out_ready")
        out_copied = mem.sem("out_copied")

        def within(i, k):
            return not isinstance(i, int) or 0 <= 2 * i + k < BLOCKS

        def by_pairs(eng, stage):
            for k in range(2):
                stage(0, k)
            with eng.Fori(1, BLOCKS // 2 - 1) as i:
                for k in range(2):
                    stage(i, k)
            for k in range(2):
                stage(BLOCKS // 2 - 1, k)

        def tile(i, k, t):
            return 2 * T * i + T * k + t

        def quadrant(b):
            return slice(b * Q, (b + 1) * Q)

        def kept(k, u):
            if u < HG:
                return qk_t[k % 2][:, 2 * u:2 * u + 2, :]
            return v_sb[k % 2][:, u - HG, :]

        def in_bank(u):
            if u < HG:
                return ps_m[u % 2][:, :].rearrange("p (j w) -> p j w", j=2)
            return ps_m[u % 2][:, :]

        with nc.Block() as block:
            @block.sync
            def _(sp):
                for j in range(PIECES):
                    if j >= RING:
                        sp.wait_ge(w_lo, j - RING + 1)
                    sp.dma_start(piece[j % RING][:, :, :],
                                 wqkv_t.rearrange("(c p) n -> p c n", p=P)[:, :, j * PW:(j + 1) * PW]
                                 ).then_inc(piece_in[j % RING], 16)

            @block.tensor
            def _(pe):
                def x_transposes(i, k):
                    for t in range(T):
                        pe.wait_ge(x_normed, tile(i, k, t) + 1)
                        if within(i, k - 1):
                            pe.wait_ge(qkv_by_act if t == 0 else qkv_by_dve, UNITS // 2 * (2 * i + k))
                        for c in range(MC):
                            done = pe.transpose(ps_m[t][:, c * P:(c + 1) * P], x_norm[:, t, c * P:(c + 1) * P],
                                                ident[:, :])
                        done.then_inc(xt_ready, 1)

                def unit(i, k, u):
                    b = 2 * i + k
                    if not within(i, k - 1):
                        pe.wait_ge(w_lo, u + 1 if u < PV else PIECES)
                    if u == 0:
                        pe.wait_ge(xt_lo, T * (b + 1))
                    if u >= 2:
                        pe.wait_ge(qkv_by_act if u % 2 == 0 else qkv_by_dve, UNITS // 2 * b + u // 2)
                    if u < HG:
                        parts = [(j * W, (j + 1) * W,
                                  [[w[:, c, (2 * u + j) * P:(2 * u + j + 1) * P] for w in w_hl] for c in range(MC)],
                                  [[w[:, c, :] for w in x_hl] for c in range(MC)]) for j in range(2)]
                    else:
                        t = u - HG
                        parts = [(0, M, [[w[:, c, t * P:(t + 1) * P] for w in x_hl] for c in range(MC)],
                                  [[w[:, c, 2 * M:3 * M] for w in w_hl] for c in range(MC)])]
                    for start, end, left, right in parts:
                        for c in range(MC):
                            done = three_products(pe, ps_m[u % 2][:, start:end], left[c], right[c],
                                                  c == 0, c == MC - 1)
                    done.then_inc(qkv_ready, 1)

                def score(i, k, t):
                    n = tile(i, k, t)
                    if t == 0:
                        pe.wait_ge(qkv_by_act, UNITS // 2 * (2 * i + k + 1))
                        pe.wait_ge(qkv_by_dve, UNITS // 2 * (2 * i + k + 1))
                    if within(i, k - 1) or t > 0:
                        pe.wait_ge(scores_by_act, 2 * n)
                        pe.wait_ge(scores_by_dve, 2 * n)
                    for g in range(HG):
                        for h in range(4):
                            done = pe.matmul(ps_s[:, h, g * P:(g + 1) * P],
                                             qk_t[k][quadrant(h), g, t * P:(t + 1) * P],
                                             qk_t[k][quadrant(h), HG + g, t * P:(t + 1) * P],
                                             start=True, stop=True)
                    done.then_inc(scores_ready, 1)

                def weigh(i, k, t, half):
                    k, t = (k, t - 1) if t > 0 else (k - 1, T - 1)
                    if not within(i, k):
                        return
                    n = tile(i, k, t)
                    if half == 0:
                        pe.wait_ge(own_by_act, 2 * n + 2)
                        pe.wait_ge(own_by_dve, 2 * n + 2)
                    if within(i, k - 1) or t + half > 0:
                        pe.wait_ge(out_copied, 2 * n + half)
                    for h in range(half * H // 2, (half + 1) * H // 2):
                        done = pe.matmul(ps_o[quadrant((T * k + t) % 4), h // 4 % 2, h % 4 * P:(h % 4 + 1) * P],
                                         v_sb[k % 2][:, t, h * D:(h + 1) * D], own[t][:, h, :],
                                         start=True, stop=True)
                    done.then_inc(out_ready, 1)

                x_transposes(0, 0)
                for u in range(UNITS):
                    unit(0, 0, u)

                def stage(i, k):
                    follows = within(i, k + 1)
                    if follows:
                        x_transposes(i, k + 1)
                    for t in range(T):
                        score(i, k, t)
                        if follows:
                            unit(i, k + 1, 3 * t)
                        weigh(i, k, t, 0)
                        if follows:
                            unit(i, k + 1, 3 * t + 1)
                        weigh(i, k, t, 1)
                        if follows:
                            unit(i, k + 1, 3 * t + 2)
                by_pairs(pe, stage)
                for half in range(2):
                    weigh(BLOCKS // 2, 0, 0, half)

            @block.scalar
            def _(act):
                def piece_high(j):
                    act.wait_ge(piece_in[j % RING], 16 * (j // RING + 1))
                    act.activation(w_hl[0][:, :, j * PW:(j + 1) * PW], piece[j % RING][:, :, :], ACT.Copy).then_inc(w_hi, 1)

                def x_high(i, k):
                    for t in range(T):
                        act.wait_ge(xt_ready, tile(i, k, t) + 1)
                        act.activation(x_hl[0][:, :, t * P:(t + 1) * P],
                                       ps_m[t][:, :].rearrange("p (c w) -> p c w", c=MC),
                                       ACT.Copy).then_inc(xt_hi, 1)

                def keep(i, k, u):
                    if within(i, k) and u % 2 == 0:
                        act.wait_ge(qkv_ready, UNITS * (2 * i + k) + u + 1)
                        act.activation(kept(k, u), in_bank(u), ACT.Copy).then_inc(qkv_by_act, 1)

                def collect(i, k, t):
                    n = tile(i, k, t)
                    act.wait_ge(scores_ready, n + 1)
                    if within(i, k - 1) or t > 0:
                        act.wait_ge(shift_ready, n)
                    for b in (0, 1):
                        act.activation(
                            scores[quadrant(b), :, :].rearrange("p (g h) k -> p h g k", h=4),
                            ps_s[quadrant(b), :, :].rearrange("p h (g w) -> p h g w", w=P)[:, :, :, quadrant(b)],
                            ACT.Copy).then_inc(scores_by_act, 1)

                def exp(i, k, t):
                    act.wait_ge(shift_ready, tile(i, k, t) + 1)
                    act.activation(exps[:, :, :], shifted[:, :, :], ACT.Exp,
                                   scale=float(D) ** -0.5).then_inc(exp_ready, 1)

                def place(i, k, t):
                    n = tile(i, k, t)
                    act.wait_ge(probs_turned, n + 1)
                    if within(i, k - 1):
                        act.wait_ge(out_ready, 2 * (n - 1))
                    for b in (0, 1):
                        act.activation(own[t][quadrant(b), :, quadrant(b)], probs_t[quadrant(b), :, :],
                                       ACT.Copy).then_inc(own_by_act, 1)

                def regroup(i, k, t, half):
                    k, t = (k, t - 1) if t > 0 else (k - 1, T - 1)
                    if not within(i, k):
                        return
                    if k < 0:
                        i, k = i - 1, k + 2
                    place_in = T * k + t
                    act.wait_ge(out_ready, 2 * tile(i, k, t) + half + 1)
                    act.activation(act_spare[:, 2 * place_in + half:2 * place_in + half + 1], eps[:, :],
                                   ACT.Copy)
                    act.activation(
                        mixed[quadrant(place_in), bass.ds(i, 1), :, :].rearrange(
                            "p c (b n) q -> p (c n) b q", n=H)[:, half * H // 2:(half + 1) * H // 2],
                        ps_o[quadrant(place_in), :, :].rearrange("p a (n b q) -> p (a n) b q", b=BT, q=Q),
                        ACT.Copy).then_inc(out_copied, 1)

                piece_high(0)
                x_high(0, 0)
                for u in range(UNITS):
                    for j in {0: (1, 2, 3), 2: (4, 5)}.get(u, ()):
                        piece_high(j)
                    keep(0, 0, u)

                def stage(i, k):
                    if within(i, k + 1):
                        x_high(i, k + 1)
                    for t in range(T):
                        collect(i, k, t)
                        keep(i, k + 1, 3 * t)
                        exp(i, k, t)
                        regroup(i, k, t, 0)
                        keep(i, k + 1, 3 * t + 1)
                        place(i, k, t)
                        regroup(i, k, t, 1)
                        keep(i, k + 1, 3 * t + 2)
                act.wait_ge(own_zeroed, 2)
                by_pairs(act, stage)
                for half in range(2):
                    regroup(BLOCKS // 2, 0, 0, half)

            @block.vector
            def _(dve):
                def piece_low(j):
                    dve.wait_ge(w_hi, j + 1)
                    dve.tensor_tensor(w_hl[1][:, :, j * PW:(j + 1) * PW], piece[j % RING][:, :, :],
                                      w_hl[0][:, :, j * PW:(j + 1) * PW].bitcast(F32), ALU.subtract).then_inc(w_lo, 1)

                def norm_stats(i, k):
                    if within(i, k):
                        for t in range(T):
                            dve.bn_stats(stats[:, t, :], x_res[:, bass.ds(tile(i, k, t), 1), :]).then_inc(x_stats, 1)
                        dve.wait_ge(x_stats, tile(i, k, T))
                        dve.memset(spare[:, :], 0.0)
                        for t in range(T):
                            dve.bn_aggr(moments[:, t, :], stats[:, t, :]).then_inc(x_moments, 1)

                def norm_apply(i, k):
                    if within(i, k):
                        for t in range(T):
                            dve.wait_ge(x_root, 2 * i + k + 1)
                            if within(i, k - 1):
                                dve.wait_ge(xt_ready, tile(i, k, 0))
                            dve.tensor_scalar(x_norm[:, t:t + 1, :], x_res[:, bass.ds(tile(i, k, t), 1), :],
                                              moments[:, t, 0:1], x_var[:, t, 1:2],
                                              ALU.subtract, ALU.mult).then_inc(x_normed, 1)

                def x_low(i, k):
                    for t in range(T):
                        dve.wait_ge(xt_hi, tile(i, k, t) + 1)
                        dve.tensor_tensor(x_hl[1][:, :, t * P:(t + 1) * P],
                                          ps_m[t][:, :].rearrange("p (c w) -> p c w", c=MC),
                                          x_hl[0][:, :, t * P:(t + 1) * P].bitcast(F32),
                                          ALU.subtract).then_inc(xt_lo, 1)

                def keep(i, k, u):
                    if within(i, k) and u % 2 == 1:
                        dve.wait_ge(qkv_ready, UNITS * (2 * i + k) + u + 1)
                        dve.tensor_copy(kept(k, u), in_bank(u)).then_inc(qkv_by_dve, 1)

                def shift(i, k, t):
                    n = tile(i, k, t)
                    dve.wait_ge(scores_ready, n + 1)
                    for b in (2, 3):
                        dve.tensor_copy(
                            scores[quadrant(b), :, :].rearrange("p (g h) k -> p h g k", h=4),
                            ps_s[quadrant(b), :, :].rearrange("p h (g w) -> p h g w", w=P)[:, :, :, quadrant(b)],
                        ).then_inc(scores_by_dve, 1)
                    dve.wait_ge(scores_by_act, 2 * n + 2)
                    dve.wait_ge(scores_by_dve, 2 * n + 2)
                    dve.tensor_reduce(top[:, :], scores[:, :, :], AX_X, ALU.max).then_inc(top_ready, 1)
                    dve.wait_ge(top_ready, n + 1)
                    dve.tensor_tensor(shifted[:, :, :], scores[:, :, :],
                                      top[:, :].unsqueeze(2).to_broadcast([P, H, Q]),
                                      ALU.subtract).then_inc(shift_ready, 1)

                def normalise(i, k, t):
                    n = tile(i, k, t)
                    dve.wait_ge(exp_ready, n + 1)
                    dve.tensor_reduce(total[:, :], exps[:, :, :], AX_X, ALU.add).then_inc(total_ready, 1)
                    dve.wait_ge(total_ready, n + 1)
                    dve.reciprocal(share[:, :], total[:, :]).then_inc(share_ready, 1)
                    dve.wait_ge(share_ready, n + 1)
                    dve.tensor_tensor(probs[:, :, :], exps[:, :, :],
                                      share[:, :].unsqueeze(2).to_broadcast([P, H, Q]),
                                      ALU.mult).then_inc(probs_ready, 1)
                    if within(i, k - 1) or t > 0:
                        dve.wait_ge(own_by_act, 2 * n)
                    dve.wait_ge(probs_ready, n + 1)
                    dve.transpose(probs_t[:, :, :].rearrange("p h q -> p (h q)"),
                                  probs[:, :, :].rearrange("p h q -> p (h q)")).then_inc(probs_turned, 1)

                def place(i, k, t):
                    n = tile(i, k, t)
                    if within(i, k - 1):
                        dve.wait_ge(out_ready, 2 * (n - 1))
                    dve.wait_ge(probs_turned, n + 1)
                    for b in (2, 3):
                        dve.tensor_copy(own[t][quadrant(b), :, quadrant(b)],
                                        probs_t[quadrant(b), :, :]).then_inc(own_by_dve, 1)

                norm_stats(0, 0)
                norm_apply(0, 0)
                piece_low(0)
                x_low(0, 0)
                for u in range(UNITS):
                    for j in {1: (1, 2, 3), 3: (4, 5)}.get(u, ()):
                        piece_low(j)
                    if u == UNITS - 1:
                        norm_stats(0, 1)
                        norm_apply(0, 1)
                    keep(0, 0, u)
                dve.wait_ge(own_zeroed, 2)

                def stage(i, k):
                    if within(i, k + 1):
                        x_low(i, k + 1)
                    for t in range(T):
                        shift(i, k, t)
                        keep(i, k + 1, 3 * t)
                        normalise(i, k, t)
                        keep(i, k + 1, 3 * t + 1)
                        place(i, k, t)
                        if t == 0:
                            norm_stats(i, k + 2)
                        if t == T - 1:
                            norm_apply(i, k + 2)
                        keep(i, k + 1, 3 * t + 2)
                by_pairs(dve, stage)

            @block.gpsimd
            def _(pool):
                def root(i, k):
                    if within(i, k):
                        b = 2 * i + k
                        pool.wait_ge(x_moments, T * (b + 1))
                        pool.tensor_tensor(x_var[:, :, 0], moments[:, :, 1], eps[:, 0:1].to_broadcast([P, T]),
                                           ALU.add).then_inc(x_eps, 1)
                        pool.wait_ge(x_eps, b + 1)
                        pool.tensor_tensor(x_var[:, :, 1], x_var[:, :, 0], minus_half[:, 0:T],
                                           ALU.pow).then_inc(x_root, 1)

                root(0, 0)
                for o in own:
                    pool.memset(o[:, :, :], 0.0).then_inc(own_zeroed, 1)
                root(0, 1)
                by_pairs(pool, lambda i, k: root(i, k + 2))


def project_and_route(nc, wproj_t, bproj, gate_t, gate_b, bias, w1_t, w2_t, b2, weights, x_res, mixed, x_hl, logits,
                      ident, minus_half, eps):
    M = wproj_t.shape[0]
    MC = M // P
    E = gate_t.shape[1]
    TILES = x_res.shape[1]
    J = P // mixed.shape[3]

    with ExitStack() as stack:
        mem = Memory(nc, stack, "p")
        piece = mem.sbuf("piece", [P, MC, M])
        w_hl = mem.pair("w", [P, MC, M])
        b_in = mem.sbuf("b_in", [P, M])
        gate_sb = mem.sbuf("gate_sb", [P, MC, E])
        gate_bias = mem.sbuf("gate_bias", [P, 2, E])
        c_hl = [mem.pair(f"c{i}", [P, MC, P]) for i in range(2)]
        stats = mem.sbuf("stats", [P, 2, 6])
        moments = mem.sbuf("moments", [P, 2, 2])
        x_var = mem.sbuf("x_var", [P, 2, 2])
        x_norm = [mem.sbuf(f"x_norm{i}", [P, M]) for i in range(2)]
        xt_sb = [mem.sbuf(f"xt_sb{i}", [P, MC, P]) for i in range(2)]
        spare = mem.sbuf("spare", [P, 4])
        ps_y = mem.banks("ps_y", 2)
        ps_xt = mem.banks("ps_xt", 2)
        ps_r = mem.banks("ps_r", 2)

        w_in = [mem.sem(f"w_in{c}") for c in range(MC)]
        rows_in = mem.sem("rows_in")
        w_hi = mem.sem("w_hi")
        w_lo = mem.sem("w_lo")
        c_hi = mem.sem("c_hi")
        c_lo = mem.sem("c_lo")
        y_ready = mem.sem("y_ready")
        y_added = mem.sem("y_added")
        b_added = mem.sem("b_added")
        x_stats = mem.sem("x_stats")
        x_moments = mem.sem("x_moments")
        x_eps = mem.sem("x_eps")
        x_root = mem.sem("x_root")
        x_normed = mem.sem("x_normed")
        xt_ready = mem.sem("xt_ready")
        xt_copied = mem.sem("xt_copied")
        xt_hi = mem.sem("xt_hi")
        xt_lo = mem.sem("xt_lo")
        r_ready = mem.sem("r_ready")
        r_added = mem.sem("r_added")
        r_done = mem.sem("r_done")
        expert_room = mem.sbuf("expert_room", [P, weights.MC * weights.F + weights.FC * M])
        weights.load_into(places_in(expert_room))
        expert_in = mem.sem("expert_in")
        expert_hi = mem.sem("expert_hi")
        expert_lo = mem.sem("expert_lo")
        PARTS_AT = {1: (0,), 2: (1,), 3: (2, 3)}

        def since(i, k):
            return not isinstance(i, int) or 2 * i + k >= 0

        def ahead(i, k):
            return not isinstance(i, int) or 2 * i + k < TILES - 1

        def by_pairs(eng, one):
            for i in range(2):
                for k in range(2):
                    one(i, k)
            with eng.Fori(2, TILES // 2 - 1) as i:
                for k in range(2):
                    one(i, k)
            for k in range(2):
                one(TILES // 2 - 1, k)

        with nc.Block() as block:
            @block.sync
            def _(sp):
                for c in range(MC):
                    sp.dma_start(piece[:, c, :], wproj_t[c * P:(c + 1) * P, :]).then_inc(w_in[c], 16)
                sp.dma_start(b_in[:, :], bproj.rearrange("(a m) -> a m", a=1).to_broadcast([P, M])
                             ).then_inc(rows_in, 16)
                sp.dma_start(gate_sb[:, :, :], gate_t.rearrange("(c p) e -> p c e", p=P)).then_inc(rows_in, 16)
                for j, row in enumerate((gate_b, bias)):
                    sp.dma_start(gate_bias[:, j, :], row.rearrange("(a e) -> a e", a=1).to_broadcast([P, E])
                                 ).then_inc(rows_in, 16)
                weights.load(sp, 0, w1_t, w2_t, b2, expert_in)

            @block.tensor
            def _(pe):
                def project(i, k):
                    n = 2 * i + k
                    pe.wait_ge(c_lo, n + 1)
                    if since(i, k - 2):
                        pe.wait_ge(y_added, n - 1)
                    for c in range(MC):
                        if isinstance(i, int) and n == 0:
                            pe.wait_ge(w_lo, c + 1)
                        done = three_products(pe, ps_y[k][:, :], [w[:, c, :] for w in c_hl[k]],
                                              [w[:, c, :] for w in w_hl], c == 0, c == MC - 1)
                    done.then_inc(y_ready, 1)

                def turn(i, k):
                    n = 2 * i + k
                    pe.wait_ge(x_normed, n + 1)
                    if since(i, k - 2):
                        pe.wait_ge(xt_hi, n - 1)
                    for c in range(MC):
                        done = pe.transpose(ps_xt[k % 2][:, c * P:(c + 1) * P], x_norm[k % 2][:, c * P:(c + 1) * P],
                                            ident[:, :])
                    done.then_inc(xt_ready, 1)

                def route(i, k):
                    n = 2 * i + k
                    pe.wait_ge(xt_copied, n + 1)
                    if since(i, k - 2):
                        pe.wait_ge(r_added, n - 1)
                    for c in range(MC):
                        done = pe.matmul(ps_r[k % 2][:, 0:E], xt_sb[k % 2][:, c, :], gate_sb[:, c, :],
                                         start=c == 0, stop=c == MC - 1)
                    done.then_inc(r_ready, 1)

                pe.wait_ge(rows_in, 64)

                def one(i, k):
                    project(i, k)
                    if since(i, k - 2):
                        turn(i, k - 2)
                    if since(i, k - 3):
                        route(i, k - 3)
                by_pairs(pe, one)
                turn(TILES // 2, -2)
                route(TILES // 2, -3)
                turn(TILES // 2, -1)
                route(TILES // 2, -2)
                route(TILES // 2, -1)

            @block.scalar
            def _(act):
                def c_high(i, k):
                    if since(i, k - 2):
                        act.wait_ge(y_ready, 2 * i + k - 1)
                        act.activation(spare[:, 2 + k % 2:3 + k % 2], eps[:, :], ACT.Copy)
                    act.activation(c_hl[k % 2][0][:, :, :].rearrange("p c (j q) -> p c j q", j=J),
                                   mixed[:, :, bass.ds(J * (2 * i + k), J), :], ACT.Copy).then_inc(c_hi, 1)

                def x_copy(i, k):
                    n = 2 * i + k
                    act.wait_ge(xt_ready, n + 1)
                    if since(i, k - 2):
                        act.wait_ge(xt_lo, n - 1)
                        act.wait_ge(r_ready, n - 1)
                    act.activation(xt_sb[k % 2][:, :, :], ps_xt[k % 2][:, :].rearrange("p (c w) -> p c w", c=MC),
                                   ACT.Copy).then_inc(xt_copied, 1)
                    act.activation(x_hl[0][:, :, bass.ds(P * n, P)],
                                   ps_xt[k % 2][:, :].rearrange("p (c w) -> p c w", c=MC),
                                   ACT.Copy).then_inc(xt_hi, 1)

                c_high(0, 0)
                for c in range(MC):
                    act.wait_ge(w_in[c], 16)
                    act.activation(w_hl[0][:, c, :], piece[:, c, :], ACT.Copy).then_inc(w_hi, 1)

                def one(i, k):
                    if ahead(i, k):
                        c_high(i, k + 1)
                    if since(i, k - 2):
                        x_copy(i, k - 2)
                    if isinstance(i, int):
                        for j in PARTS_AT.get(2 * i + k, ()):
                            act.wait_ge(expert_in, 64)
                            raw, hi, _ = weights.parts(0)[j]
                            act.activation(hi, raw, ACT.Copy).then_inc(expert_hi, 1)
                by_pairs(act, one)
                x_copy(TILES // 2, -2)
                x_copy(TILES // 2, -1)

            @block.vector
            def _(dve):
                def c_low(i, k):
                    dve.wait_ge(c_hi, 2 * i + k + 1)
                    dve.tensor_tensor(c_hl[k % 2][1][:, :, :].rearrange("p c (j q) -> p c j q", j=J),
                                      mixed[:, :, bass.ds(J * (2 * i + k), J), :],
                                      c_hl[k % 2][0][:, :, :].bitcast(F32).rearrange("p c (j q) -> p c j q", j=J),
                                      ALU.subtract).then_inc(c_lo, 1)

                def add(i, k):
                    n = 2 * i + k
                    tile = x_res[:, bass.ds(n, 1), :]
                    dve.wait_ge(y_ready, n + 1)
                    dve.tensor_tensor(tile, ps_y[k % 2][:, :].unsqueeze(1), tile, ALU.add).then_inc(y_added, 1)
                    dve.wait_ge(y_added, n + 1)
                    dve.tensor_tensor(tile, tile, b_in[:, :].unsqueeze(1), ALU.add).then_inc(b_added, 1)
                    dve.wait_ge(b_added, n + 1)
                    dve.memset(spare[:, 0:1], 0.0)
                    dve.bn_stats(stats[:, k % 2, :], tile).then_inc(x_stats, 1)
                    dve.wait_ge(x_stats, n + 1)
                    dve.memset(spare[:, 1:2], 0.0)
                    dve.bn_aggr(moments[:, k % 2, :], stats[:, k % 2, :]).then_inc(x_moments, 1)

                def norm(i, k):
                    n = 2 * i + k
                    dve.wait_ge(x_root, n + 1)
                    if since(i, k - 2):
                        dve.wait_ge(xt_ready, n - 1)
                    dve.tensor_scalar(x_norm[k % 2][:, :].unsqueeze(1), x_res[:, bass.ds(n, 1), :],
                                      moments[:, k % 2, 0:1], x_var[:, k % 2, 1:2],
                                      ALU.subtract, ALU.mult).then_inc(x_normed, 1)

                def x_low(i, k):
                    n = 2 * i + k
                    dve.wait_ge(xt_hi, n + 1)
                    dve.tensor_tensor(x_hl[1][:, :, bass.ds(P * n, P)], xt_sb[k % 2][:, :, :],
                                      x_hl[0][:, :, bass.ds(P * n, P)].bitcast(F32), ALU.subtract).then_inc(xt_lo, 1)

                def score(i, k):
                    n = 2 * i + k
                    dve.wait_ge(r_ready, n + 1)
                    dve.tensor_tensor(logits[:, bass.ds(n, 1), :], ps_r[k % 2][:, 0:E].unsqueeze(1),
                                      gate_bias[:, 0:1, :], ALU.add).then_inc(r_added, 1)
                    dve.wait_ge(r_added, n + 1)
                    dve.tensor_tensor(logits[:, bass.ds(n, 1), :], logits[:, bass.ds(n, 1), :],
                                      gate_bias[:, 1:2, :], ALU.add).then_inc(r_done, 1)

                c_low(0, 0)
                for c in range(MC):
                    dve.wait_ge(w_hi, c + 1)
                    dve.tensor_tensor(w_hl[1][:, c, :], piece[:, c, :], w_hl[0][:, c, :].bitcast(F32),
                                      ALU.subtract).then_inc(w_lo, 1)
                dve.wait_ge(rows_in, 64)

                def one(i, k):
                    if since(i, k - 2):
                        norm(i, k - 2)
                    if ahead(i, k):
                        c_low(i, k + 1)
                    if since(i, k - 1):
                        add(i, k - 1)
                    if since(i, k - 3):
                        x_low(i, k - 3)
                        score(i, k - 3)
                    if isinstance(i, int):
                        for j in PARTS_AT.get(2 * i + k, ()):
                            dve.wait_ge(expert_hi, j + 1)
                            raw, hi, lo = weights.parts(0)[j]
                            dve.tensor_tensor(lo, raw, hi.bitcast(F32), ALU.subtract).then_inc(expert_lo, 1)
                by_pairs(dve, one)
                norm(TILES // 2, -2)
                add(TILES // 2, -1)
                x_low(TILES // 2, -3)
                score(TILES // 2, -3)
                norm(TILES // 2, -1)
                x_low(TILES // 2, -2)
                score(TILES // 2, -2)
                x_low(TILES // 2, -1)
                score(TILES // 2, -1)

            @block.gpsimd
            def _(pool):
                def one(i, k):
                    n = 2 * i + k
                    pool.wait_ge(x_moments, n + 1)
                    pool.tensor_tensor(x_var[:, k, 0:1], moments[:, k, 1:2], eps[:, 0:1],
                                       ALU.add).then_inc(x_eps, 1)
                    pool.wait_ge(x_eps, n + 1)
                    pool.tensor_tensor(x_var[:, k, 1:2], x_var[:, k, 0:1], minus_half[:, 0:1],
                                       ALU.pow).then_inc(x_root, 1)
                by_pairs(pool, one)


class Gate:

    def __init__(self, mem, places, logits, gates):
        _, T, E = logits.shape
        self.T, self.E, self.logits, self.gates = T, E, logits, gates

        def scores_like():
            return places(T * E).rearrange("p (t e) -> p t e", t=T)

        self.rank = scores_like()
        self.top = [mem.sbuf(f"top{i}", [P, T]) for i in range(2)]
        self.best = [mem.sbuf(f"best{i}", [P, T]) for i in range(2)]
        self.at_top = [scores_like() for i in range(2)]
        self.pick = [scores_like() for i in range(2)]
        self.rest = scores_like()
        self.gap = mem.sbuf("gap", [P, T])
        self.second = mem.sbuf("second", [P, T])
        self.total = mem.sbuf("total", [P, T])
        self.weight = [mem.sbuf(f"weight{i}", [P, T]) for i in range(2)]
        self.share = [scores_like() for i in range(2)]
        self.ranked = mem.sem("ranked")
        self.step = mem.sem("step")
        self.gap_ready = mem.sem("gap_ready")
        self.second_ready = mem.sem("second_ready")
        self.gates_ready = mem.sem("gates_ready")

    def over_experts(self, a):
        return a[:, :].unsqueeze(2).to_broadcast([P, self.T, self.E])

    def ranks(self, pool):
        for e in range(self.E):
            pool.memset(self.rank[:, :, e:e + 1], float(self.E - e)).then_inc(self.ranked, 1)

    def exponential(self, act):
        act.wait_ge(self.gap_ready, 1)
        act.activation(self.second[:, :], self.gap[:, :], ACT.Exp).then_inc(self.second_ready, 1)

    def chain(self, dve):
        step, rank, pick, top, second = self.step, self.rank, self.pick, self.top, self.second
        dve.wait_ge(self.ranked, self.E)
        scores = self.logits
        for i in range(2):
            at = 6 * i
            at_top, best = self.at_top[i], self.best[i]
            dve.tensor_reduce(top[i][:, :], scores[:, :, :], AX_X, ALU.max).then_inc(step, 1)
            dve.wait_ge(step, at + 1)
            dve.tensor_tensor(at_top[:, :, :], scores[:, :, :], self.over_experts(top[i]),
                              ALU.is_equal).then_inc(step, 1)
            dve.wait_ge(step, at + 2)
            dve.tensor_tensor(at_top[:, :, :], at_top[:, :, :], rank[:, :, :], ALU.mult).then_inc(step, 1)
            dve.wait_ge(step, at + 3)
            dve.tensor_reduce(best[:, :], at_top[:, :, :], AX_X, ALU.max).then_inc(step, 1)
            dve.wait_ge(step, at + 4)
            dve.tensor_tensor(pick[i][:, :, :], rank[:, :, :], self.over_experts(best),
                              ALU.is_equal).then_inc(step, 1)
            dve.wait_ge(step, at + 5)
            if i == 0:
                dve.scalar_tensor_tensor(self.rest[:, :, :], pick[0][:, :, :], LOWEST, self.logits[:, :, :],
                                         ALU.mult, ALU.add).then_inc(step, 1)
                dve.wait_ge(step, at + 6)
                scores = self.rest
        dve.tensor_tensor(self.gap[:, :], top[1][:, :], top[0][:, :], ALU.subtract).then_inc(self.gap_ready, 1)
        dve.wait_ge(self.second_ready, 1)
        dve.tensor_scalar(self.total[:, :], second[:, :], 1.0, None, ALU.add).then_inc(step, 1)
        dve.wait_ge(step, 12)
        dve.reciprocal(self.weight[0][:, :], self.total[:, :]).then_inc(step, 1)
        dve.wait_ge(step, 13)
        dve.tensor_tensor(self.weight[1][:, :], second[:, :], self.weight[0][:, :], ALU.mult).then_inc(step, 1)
        dve.wait_ge(step, 14)
        for i in range(2):
            dve.tensor_tensor(self.share[i][:, :, :], pick[i][:, :, :], self.over_experts(self.weight[i]),
                              ALU.mult).then_inc(step, 1)
        dve.wait_ge(step, 16)
        dve.tensor_tensor(self.gates[:, :, :].rearrange("p e t -> p t e"), self.share[0][:, :, :],
                          self.share[1][:, :, :], ALU.add).then_inc(self.gates_ready, 1)
        dve.wait_ge(self.gates_ready, 1)


class ExpertWeights:

    def __init__(self, mem, w1_t):
        E, M, F = w1_t.shape
        self.MC, self.FC = M // P, -(-F // P)
        self.REST = F - (self.FC - 1) * P
        self.F, self.M = F, M
        self.w1_hl = [mem.pair("w1_0", [P, self.MC, F])]
        self.w2_hl = [mem.pair("w2_0", [P, self.FC, M])]

    def load_into(self, places):
        self.w1_in = places(self.MC * self.F).rearrange("p (c f) -> p c f", c=self.MC)
        self.w2_in = places(self.FC * self.M).rearrange("p (c m) -> p c m", c=self.FC)

    def second_buffers(self, mem):
        self.w1_hl.append(mem.pair("w1_1", [P, self.MC, self.F]))
        self.w2_hl.append(mem.pair("w2_1", [P, self.FC, self.M]))

    def load(self, sp, e, w1_t, w2_t, b2, loaded):
        MC, FC, REST, F = self.MC, self.FC, self.REST, self.F
        sp.dma_start(self.w1_in[:, :, :], w1_t[e].rearrange("(c p) f -> p c f", p=P)).then_inc(loaded, 16)
        sp.dma_start(self.w2_in[:, 0:FC - 1, :],
                     w2_t[e, 0:(FC - 1) * P].rearrange("(c p) m -> p c m", p=P)).then_inc(loaded, 16)
        sp.dma_start(self.w2_in[0:REST, FC - 1, :], w2_t[e, (FC - 1) * P:F]).then_inc(loaded, 16)
        sp.dma_start(self.w2_in[REST:REST + 1, FC - 1, :], b2[e]).then_inc(loaded, 16)

    def parts(self, k):
        half, FC, rows = self.MC // 2, self.FC, self.REST + 1
        (w1_hi, w1_lo), (w2_hi, w2_lo) = self.w1_hl[k], self.w2_hl[k]
        return [tuple(w[:, 0:half, :] for w in (self.w1_in, w1_hi, w1_lo)),
                tuple(w[:, half:, :] for w in (self.w1_in, w1_hi, w1_lo)),
                tuple(w[:, 0:FC - 1, :] for w in (self.w2_in, w2_hi, w2_lo)),
                tuple(w[0:rows, FC - 1, :] for w in (self.w2_in, w2_hi, w2_lo))]


def experts(nc, w1_t, b1_t, w2_t, b2, weights, logits, x_res, x_hl, gates, room, out):
    E, M, F = w1_t.shape
    MC = M // P
    FC = -(-F // P)
    REST = F - (FC - 1) * P
    TILES = x_res.shape[1]
    T = 4
    W = T * P
    BLOCKS = TILES // T

    def width(m):
        return P if m < FC - 1 else REST

    def depth(m):
        return P if m < FC - 1 else REST + 1

    with ExitStack() as stack:
        mem = Memory(nc, stack, "e")
        places = places_in(room)
        weights.load_into(places)
        weights.second_buffers(mem)
        w1_hl, w2_hl = weights.w1_hl, weights.w2_hl
        b1_sb = mem.sbuf("b1_sb", [P, FC, E])
        b1_now = [mem.sbuf(f"b1_now{i}", [P, FC]) for i in range(2)]
        hidden = [places(W) for i in range(2)]
        h_hl = [mem.pair(f"h{i}", [P, FC, W]) for i in range(2)]
        bias_row = places(W)
        ps_h = mem.banks("ps_h", 2)
        ps_y = mem.banks("ps_y", 4)
        loaded = mem.sem("loaded")
        b1_loaded = mem.sem("b1_loaded")
        b1_padded = mem.sem("b1_padded")
        b1_picked = mem.sem("b1_picked")
        w_hi = mem.sem("w_hi")
        w_lo = mem.sem("w_lo")
        row_filled = mem.sem("row_filled")
        row_ready = mem.sem("row_ready")
        h_ready = mem.sem("h_ready")
        h_act = mem.sem("h_act")
        h_hi = mem.sem("h_hi")
        h_lo = mem.sem("h_lo")
        y_ready = mem.sem("y_ready")
        y_added = mem.sem("y_added")
        stored = mem.sem("stored")
        gate = Gate(mem, places, logits, gates)
        PARTS = len(weights.parts(0))

        def within(i, k):
            return not isinstance(i, int) or 0 <= 2 * i + k < E

        def by_pairs(eng, one):
            for k in range(2):
                one(0, k)
            with eng.Fori(1, E // 2 - 1) as i:
                for k in range(2):
                    one(i, k)
            for k in range(2):
                one(E // 2 - 1, k)

        def steps(i, k, tb):
            return 2 * BLOCKS * i + BLOCKS * k + tb

        with nc.Block() as block:
            @block.sync
            def _(sp):
                def load(i, k):
                    if within(i, k - 2):
                        sp.wait_ge(w_lo, PARTS * (2 * i + k - 1))
                    weights.load(sp, 2 * i + k, w1_t, w2_t, b2, loaded)

                sp.wait_ge(b1_padded, 1)
                sp.dma_start(b1_sb[:, 0:FC - 1, :],
                             b1_t[0:(FC - 1) * P, :].rearrange("(c p) e -> p c e", p=P)).then_inc(b1_loaded, 16)
                sp.dma_start(b1_sb[0:REST, FC - 1, :], b1_t[(FC - 1) * P:F, :]).then_inc(b1_loaded, 16)

                def one(i, k):
                    if within(i, k + 1):
                        load(i, k + 1)
                by_pairs(sp, one)
                for tb in range(BLOCKS):
                    sp.wait_ge(y_added, T * steps(0, E - 1, tb) + T)
                    sp.dma_start(out[tb * W:(tb + 1) * W, :].rearrange("(t p) m -> p t m", p=P),
                                 x_res[:, tb * T:(tb + 1) * T, :]).then_inc(stored, 16)
                sp.wait_ge(stored, 16 * BLOCKS)

            @block.tensor
            def _(pe):
                def hidden_layer(i, k, tb):
                    s = steps(i, k, tb)
                    if tb == 0 and within(i, k - 1):
                        pe.wait_ge(w_lo, PARTS * (2 * i + k))
                    for m in range(FC):
                        if not (isinstance(i, int) and FC * s + m < 2):
                            pe.wait_ge(h_act, FC * s + m - 1)
                        bank = ps_h[(FC * (BLOCKS * k + tb) + m) % 2]
                        for c in range(MC):
                            done = three_products(
                                pe, bank[0:width(m), :],
                                [w[:, c, m * P:m * P + width(m)] for w in w1_hl[k % 2]],
                                [w[:, c, tb * W:(tb + 1) * W] for w in x_hl], c == 0, c == MC - 1)
                        done.then_inc(h_ready, 1)

                def output_layer(i, k, tb):
                    s = steps(i, k, tb)
                    pe.wait_ge(h_lo, FC * s + FC)
                    if tb == 0 and not within(i, k - 1):
                        pe.wait_ge(row_ready, 4)
                    for t in range(T):
                        if within(i, k - 1) or tb > 0:
                            pe.wait_ge(y_added, T * (s - 1) + t + 1)
                        for m in range(FC):
                            done = three_products(
                                pe, ps_y[t][:, :],
                                [w[0:depth(m), m, t * P:(t + 1) * P] for w in h_hl[tb % 2]],
                                [w[0:depth(m), m, :] for w in w2_hl[k % 2]], m == 0, m == FC - 1)
                        done.then_inc(y_ready, 1)

                def one(i, k):
                    for tb in range(BLOCKS):
                        hidden_layer(i, k, tb)
                        if tb > 0:
                            output_layer(i, k, tb - 1)
                        elif within(i, k - 1):
                            output_layer(i, k - 1, BLOCKS - 1)
                by_pairs(pe, one)
                output_layer(0, E - 1, BLOCKS - 1)

            @block.scalar
            def _(act):
                def weights_high(i, k):
                    act.wait_ge(loaded, 64 * (2 * i + k))
                    if within(i, k - 2):
                        act.wait_ge(y_ready, T * steps(i, k - 1, 0))
                    for raw, hi, _ in weights.parts(k % 2):
                        act.activation(hi, raw, ACT.Copy).then_inc(w_hi, 1)

                def one(i, k):
                    act.wait_ge(b1_picked, 2 * i + k + 1)
                    for tb in range(BLOCKS):
                        s = steps(i, k, tb)
                        for m in range(FC):
                            act.wait_ge(h_ready, FC * s + m + 1)
                            bank = (FC * (BLOCKS * k + tb) + m) % 2
                            if not (isinstance(i, int) and FC * s + m < 2):
                                act.wait_ge(h_lo, FC * s + m - 1)
                            act.activation(hidden[bank][0:width(m), :], ps_h[bank][0:width(m), :], ACT.Silu,
                                           bias=b1_now[k % 2][0:width(m), m:m + 1]).then_inc(h_act, 1)
                        if tb == 0 and not within(i, k - 1):
                            gate.exponential(act)
                        if tb == 1 and within(i, k + 1):
                            weights_high(i, k + 1)
                by_pairs(act, one)

            @block.gpsimd
            def _(pool):
                pool.memset(b1_sb[:, :, :], 0.0).then_inc(b1_padded, 1)
                pool.memset(bias_row[:, :], 1.0).then_inc(row_filled, 1)
                gate.ranks(pool)

            @block.vector
            def _(dve):
                def pick_bias(i, k):
                    dve.tensor_copy(b1_now[k % 2][:, :].unsqueeze(2),
                                    b1_sb[:, :, bass.ds(2 * i + k, 1)]).then_inc(b1_picked, 1)

                def weights_low(i, k):
                    for j, (raw, hi, lo) in enumerate(weights.parts(k % 2)):
                        dve.wait_ge(w_hi, PARTS * (2 * i + k - 1) + j + 1)
                        dve.tensor_tensor(lo, raw, hi.bitcast(F32), ALU.subtract).then_inc(w_lo, 1)
                    pick_bias(i, k)

                def split(i, k, tb):
                    s = steps(i, k, tb)
                    for m in range(FC):
                        bank = (FC * (BLOCKS * k + tb) + m) % 2
                        hi, lo = [w[0:width(m), m, :] for w in h_hl[tb % 2]]
                        dve.wait_ge(h_act, FC * s + m + 1)
                        if m == 0 and (within(i, k - 1) or tb >= 2):
                            dve.wait_ge(y_ready, T * (s - 1))
                        dve.tensor_copy(hi, hidden[bank][0:width(m), :]).then_inc(h_hi, 1)
                        dve.wait_ge(h_hi, FC * s + m + 1)
                        dve.tensor_tensor(lo, hidden[bank][0:width(m), :], hi.bitcast(F32),
                                          ALU.subtract).then_inc(h_lo, 1)

                def add(i, k, tb):
                    s = steps(i, k, tb)
                    for t in range(T):
                        tile = tb * T + t
                        dve.wait_ge(y_ready, T * s + t + 1)
                        dve.scalar_tensor_tensor(x_res[:, tile, :], ps_y[t][:, :],
                                                 gates[:, bass.ds(2 * i + k, 1), tile], x_res[:, tile, :],
                                                 ALU.mult, ALU.add).then_inc(y_added, 1)

                dve.wait_ge(b1_loaded, 32)
                pick_bias(0, 0)
                dve.wait_ge(row_filled, 1)
                for hi, lo in h_hl:
                    dve.tensor_copy(hi[REST:REST + 1, FC - 1, :], bias_row[REST:REST + 1, :]).then_inc(row_ready, 1)
                    dve.tensor_scalar(lo[REST:REST + 1, FC - 1, :], bias_row[REST:REST + 1, :], 0.0, None,
                                      ALU.mult).then_inc(row_ready, 1)

                def one(i, k):
                    for tb in range(BLOCKS):
                        split(i, k, tb)
                        if tb == 0 and not within(i, k - 1):
                            gate.chain(dve)
                        if tb > 0:
                            add(i, k, tb - 1)
                        elif within(i, k - 1):
                            add(i, k - 1, BLOCKS - 1)
                        if tb == 1 and within(i, k + 1):
                            weights_low(i, k + 1)
                by_pairs(dve, one)
                add(0, E - 1, BLOCKS - 1)


def perceiver_layer(nc, a, out):
    B, Q, M = a["x"].shape
    C = a["wk"].shape[0]
    H = a["wk_t"].shape[1]
    E = a["w1_t"].shape[0]
    TILES = B * Q // P
    scores_scratch = nc.dram_tensor("scores_scratch", (B, P, C // P, H, Q), F32).ap()
    values_scratch = nc.dram_tensor("values_scratch", (B, P, C // P, H, Q), F32).ap()
    with ExitStack() as stack:
        mem = Memory(nc, stack, "all")
        ident = mem.sbuf("ident", [P, P])
        minus_half = mem.sbuf("minus_half", [P, 16])
        eps = mem.sbuf("eps", [P, 1])
        shared_constants(nc, ident, minus_half, eps)
        queries(nc, a["x"], a["wq"], a["wk_t"], a["gq"], a["gk"], scores_scratch, ident, minus_half, eps)
        x_res = mem.sbuf("x_res", [P, TILES, M])
        with ExitStack() as both:
            ahead = Memory(nc, both, "ahead")
            wv_hl = ahead.pair("wv", [P, C // P, a["wv"].shape[1]])
            u_in = [ahead.sbuf(f"u_in{i}", [P, 8, C // P, P]) for i in range(2)]
            attend(nc, a["ctx_t"], a["ctx_rows"], a["ctx_last"], a["last_t"], a["wk"], scores_scratch,
                   values_scratch, a["wv"], wv_hl, u_in,
                   x_res[:, :, :].rearrange("p t m -> p (t m)"), ident, minus_half, eps)
            project_values(nc, a["x"], a["wo"], values_scratch, wv_hl, u_in, x_res)
        logits = mem.sbuf("logits", [P, TILES, E])
        gates = mem.sbuf("gates", [P, E, TILES])
        mixed = mem.sbuf("mixed", [P, M // P, B, Q])
        self_attend(nc, a["wqkv_t"], x_res, mixed, ident, minus_half, eps)
        x_hl = mem.pair("x", [P, M // P, B * Q])
        weights = ExpertWeights(mem, a["w1_t"])
        project_and_route(nc, a["wproj_t"], a["bproj"], a["gate_t"], a["gate_b"], a["bias"], a["w1_t"], a["w2_t"],
                          a["b2"], weights, x_res, mixed, x_hl, logits, ident, minus_half, eps)
        experts(nc, a["w1_t"], a["b1_t"], a["w2_t"], a["b2"], weights, logits, x_res, x_hl, gates,
                mixed[:, :, :, :].rearrange("p c b q -> p (c b q)"), out)


def kernel(**inputs):
    import numpy as _np
    import concourse.bacc as _bacc
    from concourse.bass_utils import run_bass_kernel_spmd as _run

    g = {k.replace("L0_", ""): _np.asarray(v) for k, v in inputs.items()}
    B, Q, M = g["x"].shape
    _, S, C = g["ctx_1024"].shape
    D = g["xattn_gq"].shape[0]
    H = g["xattn_Wk"].shape[1] // D
    E, F, _ = g["ffn_w1"].shape
    n, d = 16, M // 16
    ctx = g["ctx_1024"]
    ctx_t = ctx.transpose(0, 2, 1).reshape(B, C // P, P, S).transpose(0, 2, 1, 3)
    laid = {
        "x": g["x"],
        "wq": g["xattn_Wq"], "wk": g["xattn_Wk"], "wv": g["xattn_Wv"], "wo": g["xattn_Wo"],
        "gq": g["xattn_gq"], "gk": g["xattn_gk"],
        "wk_t": g["xattn_Wk"].reshape(C, H, D).transpose(2, 1, 0),
        "ctx_t": _np.pad(ctx_t, ((0, 0), (0, 0), (0, 0), (0, S % 2))),
        "ctx_rows": ctx[:, :S - 1], "ctx_last": ctx[:, S - 1:], "last_t": ctx[:, S - 1].T,
        "wqkv_t": g["attn_Wqkv"].reshape(n, 3, d, M).transpose(3, 1, 0, 2).reshape(M, 3 * M),
        "wproj_t": g["attn_Wproj"].T, "bproj": g["attn_bproj"],
        "gate_t": g["ffn_gate_w"].T, "gate_b": g["ffn_gate_b"], "bias": g["ffn_bias"],
        "w1_t": g["ffn_w1"].transpose(0, 2, 1), "b1_t": g["ffn_b1"].T,
        "w2_t": g["ffn_w2"].transpose(0, 2, 1), "b2": g["ffn_b2"].reshape(E, 1, M),
    }
    nc = _bacc.Bacc("TRN2", target_bir_lowering=False, num_devices=1)
    arrays, args = {}, {}
    for name, value in laid.items():
        arrays[f"in_{name}"] = _np.ascontiguousarray(value)
        args[name] = nc.dram_tensor(f"in_{name}", value.shape, F32, kind="ExternalInput").ap()
    out = nc.dram_tensor("out_x", (B * Q, M), F32, kind="ExternalOutput").ap()
    perceiver_layer(nc, args, out)
    r = _run(nc, [arrays], core_ids=[0])
    return r.results[0]["out_x"].reshape(B, Q, M)
```
